# Optimizing a Trainium2 kernel written in Bass

```python
import numpy as np
import jax
import jax.numpy as jnp

def _softmax(x, axis=-1):
    return jax.nn.softmax(x, axis=axis)
def _gelu(x):
    return jax.nn.gelu(x, approximate=True)
def _silu(x):
    return jax.nn.silu(x)
def _sigmoid(x):
    return jax.nn.sigmoid(x)
def _layernorm(x, axis=-1, eps=1e-5):
    m = jnp.mean(x, axis=axis, keepdims=True)
    v = jnp.var(x, axis=axis, keepdims=True)
    return (x - m) / jnp.sqrt(v + eps)
def _scatter_add(tgt, idx, src, axis=0):
    return tgt.at[idx].add(src)
def _segment_sum(src, seg, n):
    return jax.ops.segment_sum(src, seg, n)

kernel_name = 'mk_conv_preact_d4_conv_nchw16_5314a9'

def setup_inputs(seed: int = 0):
    np.random.seed(seed)
    _w = jnp.asarray
    def _rec_inputs():
        import jax
        import jax.numpy as jnp
        _gk = jax.random.key(seed)
        x = 0.5 + 0.2886 * jax.random.normal(jax.random.fold_in(_gk, 1), (512, 16, 64, 64), jnp.float32)
        return x
    x = _rec_inputs()
    def _L0_conv_setup():
        import jax, jax.numpy as jnp
        import numpy as np
        B, T = (512, 16)
        FRAME, DIGIT = (64, 28)

        def _st(image, where, out_size):
            translate = abs(image.shape[-1] - out_size) * (where[::-1] + 1) / 2
            return jax.image.scale_and_translate(image, (out_size, out_size), (0, 1), jnp.ones(2, image.dtype), translate, method='cubic', antialias=False)
        key = jax.random.key(seed)
        ks = jax.random.split(key, 20)
        p = lambda i, shape: jax.random.normal(ks[i], shape, jnp.float32) * 0.05
        conv_out = FRAME - DIGIT + 1
        return dict(frames=jax.random.uniform(ks[0], (B, T, FRAME, FRAME), jnp.float32), digit_mean=jax.random.uniform(ks[1], (DIGIT, DIGIT), jnp.float32), where_w1=p(2, (conv_out * conv_out, 200)), where_b1=p(3, (200,)), where_w2=p(4, (200, 200)), where_b2=p(5, (200,)), where_wloc=p(6, (100, 2)), where_bloc=p(7, (2,)), what_w1=p(8, (DIGIT * DIGIT, 400)), what_b1=p(9, (400,)), what_w2=p(10, (400, 200)), what_b2=p(11, (200,)), what_wloc=p(12, (200, 10)), what_bloc=p(13, (10,)), dec_w1=p(14, (10, 200)), dec_b1=p(15, (200,)), dec_w2=p(16, (200, 400)), dec_b2=p(17, (400,)), dec_w3=p(18, (400, DIGIT * DIGIT)), dec_b3=p(19, (DIGIT * DIGIT,)))
    _L0_conv_all = _L0_conv_setup()
    _L0_conv_in = {k: v for k, v in _L0_conv_all.items() if k in ('digit_mean', 'where_w1', 'where_b1', 'where_w2', 'where_b2', 'where_wloc', 'where_bloc', 'what_w1', 'what_b1', 'what_w2', 'what_b2', 'what_wloc', 'what_bloc', 'dec_w1', 'dec_b1', 'dec_w2', 'dec_b2', 'dec_w3', 'dec_b3', )}
    del _L0_conv_all

    def _L1_conv_setup():
        import jax, jax.numpy as jnp
        import numpy as np
        from jax import lax
        K = 3
        P = 1
        _CONV_PAD = K - 1 - P

        def _rconv(a, w):
            return lax.conv_general_dilated(a, w, window_strides=(1, 1), padding=[(_CONV_PAD, _CONV_PAD), (_CONV_PAD, _CONV_PAD)], dimension_numbers=('NCHW', 'OIHW', 'NCHW'))
        key = jax.random.key(seed)
        k1, k2, k3, k4, k5 = jax.random.split(key, 5)
        N, C_IN, C_OUT, H, W = (8, 16, 16, 512, 512)
        x = jax.random.normal(k1, (N, C_IN, H, W), dtype=jnp.float32)
        scale = 1.0 / np.sqrt(C_IN * K * K)
        w_real = jax.random.normal(k2, (C_IN, C_OUT, K, K), dtype=jnp.float32) * scale
        w_imag = jax.random.normal(k3, (C_IN, C_OUT, K, K), dtype=jnp.float32) * scale
        b_real = jax.random.normal(k4, (C_OUT,), dtype=jnp.float32) * scale
        b_imag = jax.random.normal(k5, (C_OUT,), dtype=jnp.float32) * scale
        return {'x': x, 'w_real': w_real, 'w_imag': w_imag, 'b_real': b_real, 'b_imag': b_imag}
    _L1_conv_all = _L1_conv_setup()
    _L1_conv_in = {k: v for k, v in _L1_conv_all.items() if k in ('w_real', 'w_imag', 'b_real', 'b_imag', )}
    del _L1_conv_all

    def _L2_conv_setup():
        import jax, jax.numpy as jnp
        import numpy as np
        KERNEL_SIZE = 3
        STRIDE = 1
        PADDING = 1
        key = jax.random.key(seed)
        k1, k2 = jax.random.split(key)
        x = jax.random.normal(k1, (16, 16, 512, 512), dtype=jnp.float32)
        K = jax.random.normal(k2, (3, 3, 16, 16), dtype=jnp.float32)
        return {'x': x, 'K': K}
    _L2_conv_all = _L2_conv_setup()
    _L2_conv_in = {k: v for k, v in _L2_conv_all.items() if k in ('K', )}
    del _L2_conv_all

    def _L3_conv_setup():
        import jax, jax.numpy as jnp
        import numpy as np
        key = jax.random.key(seed)
        uvs = jax.random.normal(key, (16, 16, 512, 256), dtype=jnp.float32)
        return {'uvs': uvs}
    _L3_conv_all = _L3_conv_setup()
    _L3_conv_in = {k: v for k, v in _L3_conv_all.items() if k in ()}
    del _L3_conv_all

    return {
        "x": x,
        "L0_conv_digit_mean": _L0_conv_in["digit_mean"],
        "L0_conv_where_w1": _L0_conv_in["where_w1"],
        "L0_conv_where_b1": _L0_conv_in["where_b1"],
        "L0_conv_where_w2": _L0_conv_in["where_w2"],
        "L0_conv_where_b2": _L0_conv_in["where_b2"],
        "L0_conv_where_wloc": _L0_conv_in["where_wloc"],
        "L0_conv_where_bloc": _L0_conv_in["where_bloc"],
        "L0_conv_what_w1": _L0_conv_in["what_w1"],
        "L0_conv_what_b1": _L0_conv_in["what_b1"],
        "L0_conv_what_w2": _L0_conv_in["what_w2"],
        "L0_conv_what_b2": _L0_conv_in["what_b2"],
        "L0_conv_what_wloc": _L0_conv_in["what_wloc"],
        "L0_conv_what_bloc": _L0_conv_in["what_bloc"],
        "L0_conv_dec_w1": _L0_conv_in["dec_w1"],
        "L0_conv_dec_b1": _L0_conv_in["dec_b1"],
        "L0_conv_dec_w2": _L0_conv_in["dec_w2"],
        "L0_conv_dec_b2": _L0_conv_in["dec_b2"],
        "L0_conv_dec_w3": _L0_conv_in["dec_w3"],
        "L0_conv_dec_b3": _L0_conv_in["dec_b3"],
        "L1_conv_w_real": _L1_conv_in["w_real"],
        "L1_conv_w_imag": _L1_conv_in["w_imag"],
        "L1_conv_b_real": _L1_conv_in["b_real"],
        "L1_conv_b_imag": _L1_conv_in["b_imag"],
        "L2_conv_K": _L2_conv_in["K"],
    }

def reference(x, L0_conv_digit_mean, L0_conv_where_w1, L0_conv_where_b1, L0_conv_where_w2, L0_conv_where_b2, L0_conv_where_wloc, L0_conv_where_bloc, L0_conv_what_w1, L0_conv_what_b1, L0_conv_what_w2, L0_conv_what_b2, L0_conv_what_wloc, L0_conv_what_bloc, L0_conv_dec_w1, L0_conv_dec_b1, L0_conv_dec_w2, L0_conv_dec_b2, L0_conv_dec_w3, L0_conv_dec_b3, L1_conv_w_real, L1_conv_w_imag, L1_conv_b_real, L1_conv_b_imag, L2_conv_K):
    import jax
    import jax.numpy as jnp
    def _L0_conv_ref(frames, digit_mean, where_w1, where_b1, where_w2, where_b2, where_wloc, where_bloc, what_w1, what_b1, what_w2, what_b2, what_wloc, what_bloc, dec_w1, dec_b1, dec_w2, dec_b2, dec_w3, dec_b3):
        import jax, jax.numpy as jnp
        import numpy as np
        B, T = (512, 16)
        FRAME, DIGIT = (64, 28)

        def _st(image, where, out_size):
            translate = abs(image.shape[-1] - out_size) * (where[::-1] + 1) / 2
            return jax.image.scale_and_translate(image, (out_size, out_size), (0, 1), jnp.ones(2, image.dtype), translate, method='cubic', antialias=False)
        b, t, fs, _ = frames.shape
        k = digit_mean[::-1, ::-1][None, None]
        fc = jax.lax.conv_general_dilated(frames.reshape(b * t, 1, fs, fs), k, (1, 1), 'VALID')
        fc = fc.reshape(b, t, -1)
        x = jax.nn.softmax(fc, -1)
        x = jax.nn.relu(x @ where_w1 + where_b1)
        x = jax.nn.relu((x @ where_w2 + where_b2).reshape(b, t, 2, 100))
        z_where = jnp.tanh(x[..., 0, :] @ where_wloc + where_bloc)
        digits = jax.vmap(jax.vmap(lambda f, w: _st(f, w, DIGIT)))(frames, z_where)
        x = jax.nn.relu(digits.reshape(b, t, -1) @ what_w1 + what_b1)
        x = jax.nn.relu(x @ what_w2 + what_b2)
        z_what = x.sum(-2) @ what_wloc + what_bloc
        x = jax.nn.relu(z_what @ dec_w1 + dec_b1)
        x = jax.nn.relu(x @ dec_w2 + dec_b2)
        digit_recon = jax.nn.sigmoid((x @ dec_w3 + dec_b3).reshape(b, DIGIT, DIGIT))
        frames_recon = jax.vmap(lambda d, ws: jax.vmap(lambda w: _st(d, w, fs))(ws))(digit_recon, z_where)
        return frames_recon

    def _L1_conv_ref(x, w_real, w_imag, b_real, b_imag):
        import jax, jax.numpy as jnp
        import numpy as np
        from jax import lax
        K = 3
        P = 1
        _CONV_PAD = K - 1 - P

        def _rconv(a, w):
            return lax.conv_general_dilated(a, w, window_strides=(1, 1), padding=[(_CONV_PAD, _CONV_PAD), (_CONV_PAD, _CONV_PAD)], dimension_numbers=('NCHW', 'OIHW', 'NCHW'))
        X = jnp.fft.rfftn(x, axes=(-2, -1), norm='backward')
        Xr, Xi = (jnp.real(X), jnp.imag(X))
        wr = jnp.transpose(jnp.flip(w_real, axis=(-2, -1)), (1, 0, 2, 3))
        wi = jnp.transpose(jnp.flip(w_imag, axis=(-2, -1)), (1, 0, 2, 3))
        Yr = _rconv(Xr, wr) - _rconv(Xi, wi) + b_real[:, None, None]
        Yi = _rconv(Xr, wi) + _rconv(Xi, wr) + b_imag[:, None, None]
        Y = lax.complex(Yr, Yi)
        return jnp.fft.irfftn(Y, axes=(-2, -1), norm='backward')

    def _L2_conv_ref(x, K):
        import jax, jax.numpy as jnp
        import numpy as np
        KERNEL_SIZE = 3
        STRIDE = 1
        PADDING = 1
        k = KERNEL_SIZE
        C = x.shape[1]
        O = K.shape[-1]
        Kw = K.reshape(k * k * C, O).reshape(C, k, k, O)
        Kw = jnp.transpose(Kw, (1, 2, 0, 3))
        y = jax.lax.conv_general_dilated(x, Kw, window_strides=(STRIDE, STRIDE), padding=[(PADDING, PADDING), (PADDING, PADDING)], dimension_numbers=('NCHW', 'HWIO', 'NCHW'))
        P = x.shape[-1] + 2 * PADDING
        n_loop = len(range(0, P - k, STRIDE))
        out_size = (P - k) // STRIDE + 1
        idx = jnp.arange(out_size)
        m = (idx < n_loop).astype(y.dtype)
        y = y * m[:, None] * m[None, :]
        return y

    def _L3_conv_ref(uvs):
        import jax, jax.numpy as jnp
        import numpy as np
        u, v = jnp.split(uvs, 2, axis=1)
        left_gate = jax.nn.relu(jnp.sign(jnp.einsum('bkmd,bkd->bkm', u, v.sum(axis=2))))[..., None]
        right_gate = jax.nn.relu(jnp.sign(jnp.einsum('bknd,bkd->bkn', v, u.sum(axis=2))))[..., None]
        return jnp.concatenate([left_gate * u, right_gate * v], axis=1)

    def _gn(v, G=8, eps=1e-5):
        B_, C_, H_, W_ = v.shape
        g = v.reshape(B_, G, C_ // G, H_, W_)
        m = jnp.mean(g, axis=(2, 3, 4), keepdims=True)
        s = jnp.var(g, axis=(2, 3, 4), keepdims=True)
        return ((g - m) / jnp.sqrt(s + eps)).reshape(v.shape)

    def _ln_c(v, eps=1e-6):
        m = jnp.mean(v, axis=1, keepdims=True)
        s = jnp.var(v, axis=1, keepdims=True)
        return (v - m) / jnp.sqrt(s + eps)

    def _ln_t(v, eps=1e-5):
        m = jnp.mean(v, axis=-1, keepdims=True)
        s = jnp.var(v, axis=-1, keepdims=True)
        return (v - m) / jnp.sqrt(s + eps)

    def _to_tokens(v):
        B_, C_, H_, W_ = v.shape
        return v.reshape(B_, C_, H_ * W_).transpose(0, 2, 1)
    def _from_tokens(t, like):
        B_, C_, H_, W_ = like.shape
        return t.transpose(0, 2, 1).reshape(B_, C_, H_, W_)

    x = x + _L0_conv_ref(_gn(x), L0_conv_digit_mean, L0_conv_where_w1, L0_conv_where_b1, L0_conv_where_w2, L0_conv_where_b2, L0_conv_where_wloc, L0_conv_where_bloc, L0_conv_what_w1, L0_conv_what_b1, L0_conv_what_w2, L0_conv_what_b2, L0_conv_what_wloc, L0_conv_what_bloc, L0_conv_dec_w1, L0_conv_dec_b1, L0_conv_dec_w2, L0_conv_dec_b2, L0_conv_dec_w3, L0_conv_dec_b3)
    x = x + _L1_conv_ref(_gn(x), L1_conv_w_real, L1_conv_w_imag, L1_conv_b_real, L1_conv_b_imag)
    x = x + _L2_conv_ref(_gn(x), L2_conv_K)
    x = x + _L3_conv_ref(_gn(x))
    return x


_drawn_inputs = setup_inputs


def setup_inputs(seed=0):
    import zlib

    import numpy as np

    out = dict(_drawn_inputs(seed))
    spreads = {}
    factors = {'L0_conv_what_w1': 8.0,
     'L0_conv_what_b1': 8.0,
     'L0_conv_what_w2': 5.723,
     'L0_conv_what_b2': 8.0,
     'L0_conv_what_wloc': 3.889,
     'L0_conv_what_bloc': 64.0,
     'L0_conv_dec_w1': 2.97,
     'L0_conv_dec_b1': 56.805,
     'L0_conv_dec_w2': 2.977,
     'L0_conv_dec_b2': 58.384,
     'L0_conv_dec_b3': 36.6,
     'L1_conv_b_real': 62.178,
     'L1_conv_b_imag': 64.0}
    for name, (base, spread) in spreads.items():
        noise = np.random.default_rng([zlib.crc32(name.encode()), seed]).standard_normal(out[name].shape)
        drawn = base * np.exp(spread * noise) if base else spread * noise
        out[name] = jnp.asarray(drawn.astype(out[name].dtype))
    for name, factor in factors.items():
        out[name] = (out[name] * factor).astype(out[name].dtype)
    return out
```

```python
from contextlib import ExitStack

import numpy as np

import concourse.bass as bass
from concourse import mybir

F32 = mybir.dt.float32
ALU = mybir.AluOpType
ACT = mybir.ActivationFunctionType
AX = mybir.AxisListType.X

B, C, N = 512, 16, 64
S = 8
GROUPS = B // S
FR = S * C
D = 28
CO = N - D + 1
PH, XS = 3, 13
CM = PH * CO
TAPS = 15
HID = 100
PROF = 96
K2 = N // 2 + 1
KB = 17
NA = N + 3
NH = 34
WB = 11
CNT = 2 * N * N
THR = 1000.0 * float(np.finfo(np.float32).eps)
EPS = 1e-5
LINKS = 51

SIGNALS = {
    "group_begun": 1, "raw_loaded": 256, "squares": 4, "sums": 4, "variance": 4, "deviation": 4, "stats": 4,
    "vector_link": LINKS, "xn_ready": 4, "xd_loaded": 128, "conv": 4, "conv_copied": 4, "conv_max": 1,
    "max_turned": 1, "max_diag": 1, "max_spread": 1, "conv_shifted": 1, "conv_exp": 1, "exp_sum": 1,
    "exp_sum_copied": 1, "where_h1": 1, "where_h1_copied": 1, "where_h2": 1, "where_h2_copied": 1,
    "where_z": 1, "where_zz": 1, "where_tanh": 1, "shift": 1, "profile_abs": 1, "profiles": 1, "norms": 1,
    "profiles_turned": 1, "turned_profiles_copied": 1, "rec_stored": 32, "cut_stored": 32, "cut_loaded": 64,
    "cut_norms_loaded": 128, "rec_loaded": 128, "rec_norms_loaded": 128, "wrx_normed": 1, "o1": 8,
    "o1_copied": 8, "digits": 8, "digits_copied_a": 4, "digits_copied_v": 4, "digits_normed": 1, "what_h1": 1,
    "what_h1_copied": 1, "what_h2": 1, "what_h2_copied": 1, "what_sum": 1, "what_z": 1, "what_z_copied": 1,
    "dec_h1": 1, "dec_h1_copied": 1, "dec_h2": 1, "dec_h2_copied": 1, "dec_out": 1, "dec_tanh": 1,
    "dec_sig": 1, "dec_stored": 16, "digit_loaded": 64, "aa": 4, "aa_copied": 4, "x1": 8, "x1_copied": 8,
    "moments": 1, "dft": 10, "dft_copied": 10, "z_stored": 128, "v_loaded": 128, "mixed": 12,
    "mixed_copied": 12, "y_stored": 128, "y_loaded": 128, "corr": 1, "corr_copied": 1, "idft": 8,
    "x2_ready": 8, "xn2_stored": 32, "edge_cleared": 1, "v2_loaded": 128, "conv2": 11, "conv2_copied": 11,
    "y2_stored": 96, "y2_loaded": 32, "x3_ready": 1, "gate_prod": 2, "gate_sum": 8, "gated": 8, "added": 1,
    "turned": 8, "turned_copied": 8, "out_stored": 128,
}


def constants():
    k = {}
    p = np.arange(128)
    k["ident"] = np.eye(128)
    k["ones"] = np.ones((128, 128))
    k["halves"] = (p[:, None] // 64 == p[None, :] // 64) * 1.0
    n = np.arange(N)
    f = np.zeros((N, N))
    g = np.zeros((N, N))
    for kk in range(K2):
        f[:, kk] = np.cos(2 * np.pi * kk * n / N)
        g[kk, :] = (1 if kk in (0, N // 2) else 2) * np.cos(2 * np.pi * kk * n / N) / N
    for kk in range(1, N // 2):
        f[:, N // 2 + kk] = -np.sin(2 * np.pi * kk * n / N)
        g[N // 2 + kk, :] = -2 * np.sin(2 * np.pi * kk * n / N) / N
    k["dft"] = np.kron(np.eye(2), f)
    k["idft"] = np.kron(np.eye(2), g)
    k["iota"] = np.broadcast_to(np.arange(PROF) - 31.0, (128, PROF))
    i = np.concatenate([np.arange(D)[::-1], np.arange(D)[::-1], np.arange(N), np.arange(N)]) + 0.5
    k["place"] = np.broadcast_to(i, (128, 2 * D + 2 * N))
    ok = np.zeros((128, XS))
    for ph in range(PH):
        for x in range(XS):
            if PH * x + ph < CO:
                ok[ph * CO:(ph + 1) * CO, x] = 1
    k["ok"] = ok
    k["low"] = (1 - ok[:, XS - 1:]) * -1e30
    th = 2 * np.pi * n / N
    k["cos"] = np.broadcast_to(np.cos(th), (128, N))
    k["sin"] = np.broadcast_to(np.sin(th), (128, N))
    sel = np.zeros((2, 4, 2, S, 4, 2, S, 32))
    for a in range(4):
        for t in range(S):
            for par in range(2):
                rows = 2 * np.arange(32) + par
                sel[0, a, 0, t, a, par, t] = 1
                sel[0, a, 1, t, a, par, t] = np.cos(th)[rows]
                sel[1, a, 0, t, a, par, t] = np.sin(th)[rows]
    k["sel"] = sel.reshape(128, 2048)
    sa = np.ones((4, 2, C, 2, 2, C))
    sa[:, 1, :, :, 0] = -1
    sb = np.ones((4, 2, C, 2, 2, C))
    sb[:, :, :, :, 0] = -1
    sb[:, 1, :, :, 1] = -1
    sb[:, 0, :, :, 0] = -1
    k["sign_a"], k["sign_b"] = sa.reshape(128, 64), sb.reshape(128, 64)
    k["zero"] = np.zeros((16, C * S * NA))
    return {n_: np.ascontiguousarray(a, dtype=np.float32) for n_, a in k.items()}


def layouts(a):
    w = {}
    k = a["L0_conv_digit_mean"][::-1, ::-1]
    t = np.zeros((TAPS, 2, N, PH, CO), np.float32)
    for e in range(2 * TAPS):
        for ph in range(PH):
            if 0 <= e - ph < D:
                for y in range(CO):
                    t[e // 2, e % 2, y:y + D, ph, y] = k[:, e - ph]
    w["toep"] = t.reshape(TAPS, 128, CM).transpose(1, 0, 2)
    t = np.zeros((PH, CO, XS, 2 * HID), np.float32)
    w1 = a["L0_conv_where_w1"].reshape(CO, CO, 2 * HID)
    for ph in range(PH):
        for x in range(XS):
            if PH * x + ph < CO:
                t[ph, :, x] = w1[:, PH * x + ph]
    w["where_w1"] = t.reshape(CM, XS, 2 * HID)
    w["where_b1"] = a["L0_conv_where_b1"][None]
    w["where_w2"] = a["L0_conv_where_w2"].reshape(2, HID, 2 * HID)[:, :, :HID].transpose(1, 0, 2)
    w["where_b2"] = a["L0_conv_where_b2"][None, :HID]
    w["where_wloc"] = a["L0_conv_where_wloc"]
    w["where_bloc"] = np.broadcast_to(a["L0_conv_where_bloc"], (128, 2))
    t = np.zeros((4, 32, 7, 400), np.float32)
    t[:, 32 - D:] = a["L0_conv_what_w1"].reshape(D, D, 400)[::-1, ::-1].reshape(4, 7, D, 400).transpose(0, 2, 1, 3)
    w["what_w1"] = t.reshape(128, 7, 400)
    w["what_b1"] = a["L0_conv_what_b1"].reshape(4, HID).T
    w["what_w2"] = a["L0_conv_what_w2"].reshape(4, HID, 200).transpose(1, 0, 2)
    w["what_b2"] = a["L0_conv_what_b2"].reshape(2, HID).T
    w["what_wloc"] = a["L0_conv_what_wloc"].reshape(2, HID, 10).transpose(1, 0, 2)
    w["what_bloc"] = a["L0_conv_what_bloc"][:, None]
    w["dec_w1"] = a["L0_conv_dec_w1"]
    w["dec_b1"] = a["L0_conv_dec_b1"].reshape(2, HID).T
    w["dec_w2"] = a["L0_conv_dec_w2"].reshape(2, HID, 400).transpose(1, 0, 2)
    w["dec_b2"] = a["L0_conv_dec_b2"].reshape(4, HID).T
    w["dec_w3"] = a["L0_conv_dec_w3"][:, ::-1].reshape(4, HID, D * D).transpose(1, 0, 2)
    w["dec_b3"] = a["L0_conv_dec_b3"][None, ::-1]
    real, imag = a["L1_conv_w_real"], a["L1_conv_w_imag"]
    pl = np.zeros((3, 2, 4, 2, C, 2, 2, C), np.float32)
    for t_ in range(3):
        for b in range(3):
            wr, wi = real[:, :, 2 - t_, 2 - b], imag[:, :, 2 - t_, 2 - b]
            for w_ in range(2):
                for part in range(2):
                    pl[t_, 0, w_ + b, part, :, w_, part] = wr
                    pl[t_, 0, w_ + b, part, :, w_, 1 - part] = wi
                    pl[t_, 1, w_ + b, part, :, w_, part] = wi
                    pl[t_, 1, w_ + b, part, :, w_, 1 - part] = wr
    w["taps"] = pl.reshape(6, 128, 64).transpose(1, 0, 2)
    w["l1_bias"] = np.stack([np.stack([a["L1_conv_b_real"], a["L1_conv_b_imag"]])] * 2).reshape(1, 64)
    kw = a["L2_conv_K"].reshape(C, 3, 3, C)
    t = np.zeros((3, 8, C, 6, C), np.float32)
    for ky in range(3):
        for kx in range(3):
            for w_ in range(6):
                t[ky, w_ + kx, :, w_] = kw[:, ky, kx]
    w["l2_taps"] = t.reshape(3, 128, 96).transpose(1, 0, 2)
    return {n_: np.ascontiguousarray(v) for n_, v in w.items()}


PERSIST = ["toep", "where_w1", "where_b1", "where_w2", "where_b2", "where_wloc", "where_bloc", "what_w1", "what_b1",
           "what_w2", "what_b2", "what_wloc", "what_bloc", "dec_w1", "dec_b1", "dec_w2", "dec_b2", "dec_w3", "dec_b3",
           "l1_bias", "l2_taps", "ident", "ones", "halves", "dft", "idft", "iota", "place", "ok", "low", "cos", "sin", "sel"]


def program(nc, x, out, src, groups=GROUPS):
    ctx = ExitStack()
    with ctx:
        def sb(name, *shape):
            return ctx.enter_context(nc.sbuf_tensor(name, [128, *shape], F32))

        def view(t, off, *dims):
            row = t.shape[1]
            return bass.AP(tensor=t[:, :].tensor, offset=off, ap=[[row, 128]] + [list(d) for d in dims])

        def rows(t, p0, p1, off, *dims):
            row = t.shape[1]
            return bass.AP(tensor=t[:, :].tensor, offset=p0 * row + off, ap=[[row, p1 - p0]] + [list(d) for d in dims])

        tab = {}
        for n in PERSIST:
            shape = src[n].shape
            tab[n] = sb("t_" + n, int(np.prod(shape[1:])))
        mix_w = sb("mix_w", N * 64)
        mix_e = sb("mix_e", 4 * 64)
        raw = sb("raw", 4096)
        x1 = sb("x1", 4096)
        small = sb("small", 3200)
        digit = sb("digit", S * 128)
        pool_a = sb("pool_a", 9112)
        pool_b = sb("pool_b", 8980)
        PS = ctx.enter_context(nc.psum_tensor("PS", [128, 8 * 512], F32))

        def bank(b, p0, p1, off, *dims):
            return bass.AP(tensor=PS[:, :].tensor, offset=p0 * 4096 + b * 512 + off, ap=[[4096, p1 - p0]] + [list(d) for d in dims])

        XN = 0
        NB = 0
        frames = lambda off, *d: view(pool_b, off, *d)
        FRN, FC, RBY, RBX = 0, 4096, 4096, 6144
        XD = 0
        WY, WX, O1, DG, NY = 0, 1792, 3840, 5632, 6528
        AA = 0
        WRY, WRX = 0, 2048
        ZZ, YO = 0, 4352
        VV = 0
        XNB = 0
        PR, NX = 0, 384
        TOT, RN, SS, TMP = 1536, 1720, 1904, 2088
        A0 = 0
        ST, MS, RS, NM, TV = 2272, 2336, 2400, 2464, 2528
        PM, DGM, SR, H1, H2 = 2592, 2720, 2848, 0, 256
        MX, ZT, TT, ZI = 2976, 2978, 2980, 2984
        ES = 2592
        big = sb("big", 840)
        HW1, HW2, HS, ZW, D1, D2 = 0, 512, 768, 784, 792, 808
        SG = 8200

        zs = nc.dram_tensor("zs", (72, C, S * NA), F32).ap()
        ys = nc.dram_tensor("ys", (2, 2 * KB, C, 2 * S * NH), F32).ap()
        xs = nc.dram_tensor("xs", (68, C, S * N), F32).ap()
        y2s = nc.dram_tensor("y2s", (66, C, S * N), F32).ap()
        pt = nc.dram_tensor("pt", (2, PROF, FR), F32).ap()
        pd = nc.dram_tensor("pd", (2, FR, PROF), F32).ap()
        rnt = nc.dram_tensor("rnt", (2 * D, FR), F32).ap()
        rnd = nc.dram_tensor("rnd", (2, FR, N), F32).ap()
        ds = nc.dram_tensor("ds", (S, D, D), F32).ap()

        def passed(eng):
            eng.sem_inc(waits_passed, 1)

        on = {n: ctx.enter_context(nc.semaphore(n)) for n in SIGNALS}
        per = SIGNALS
        waits_passed = ctx.enter_context(nc.semaphore("waits_passed"))
        loaded = ctx.enter_context(nc.semaphore("tables_loaded"))
        zeroed = ctx.enter_context(nc.semaphore("scratch_zeroed"))
        cleared = ctx.enter_context(nc.semaphore("buffers_cleared"))
        mixing = ctx.enter_context(nc.semaphore("mix_tables_ready"))
        block = ctx.enter_context(nc.Block())

        LOADS = len(PERSIST) + 8

        @block.sync
        def _(sp):
            for n in PERSIST:
                a = src[n]
                flat = a if len(a.shape) == 2 else a.rearrange("a b c -> a (b c)")
                sp.dma_start(tab[n][0:a.shape[0], :], flat).then_inc(loaded, 16)
            sp.dma_start(view(pool_a, 0, (1, 384)), src["taps"].rearrange("a b c -> a (b c)")).then_inc(loaded, 16)
            sp.dma_start(view(pool_a, 384, (1, 64)), src["sign_a"]).then_inc(loaded, 16)
            sp.dma_start(view(pool_a, 448, (1, 64)), src["sign_b"]).then_inc(loaded, 16)
            z = src["zero"]
            W1 = C * S * NA
            for a, b in ((0, 1), (34, 38), (69, 72)):
                sp.dma_start(zs[a:b].rearrange("a b c -> a (b c)"), z[0:b - a, :]).then_inc(zeroed, 16)
            for a, b in ((0, 1), (65, 68)):
                sp.dma_start(xs[a:b].rearrange("a b c -> a (b c)"), z[0:b - a, 0:C * S * N]).then_inc(zeroed, 16)
            sp.dma_start(y2s[63:64].rearrange("a b c -> a (b c)"), z[0:1, 0:C * S * N]).then_inc(zeroed, 16)
            sp.wait_ge(zeroed, 16 * 6)
            sp.wait_ge(mixing, 13)
            with sp.Fori(0, groups) as g:
                sp.wait_ge(on["group_begun"], g + 1)
                b0 = sp.snap(g * S)
                for s in range(S):
                    for u in range(2):
                        d = x[bass.ds(b0 + s, 1), 8 * u:8 * u + 8].rearrange("s c n m -> n (s c) m")
                        sp.dma_start(rows(raw, 64 * u, 64 * u + 64, 512 * s, (64, 8), (1, 64)), d).then_inc(on["raw_loaded"], 16)
                sp.wait_ge(on["xn_ready"], g * per["xn_ready"] + 1)
                for half in range(2):
                    for q in range(4):
                        u = q // 2
                        sp.dma_start(rows(pool_a, 64 * half, 64 * half + 64, XD + 1 - half + 2048 * q, (256, S), (1, 256)),
                                              rows(pool_b, 64 * u, 64 * u + 64, FRN + 256 * (q % 2), (512, S), (1, 256))).then_inc(on["xd_loaded"], 16)
                sp.wait_ge(on["norms"], g * per["norms"] + per["norms"])
                flat = lambda t, off, *d: bass.AP(tensor=t.tensor, offset=off, ap=[list(e) for e in d])
                sp.dma_start(pd.rearrange("a f u -> f a u"), view(small, PR + 2 * PROF, (PROF, 2), (1, PROF))).then_inc(on["rec_stored"], 16)
                sp.dma_start(rnd.rearrange("a f u -> f a u"), view(small, RN + 2 * D, (N, 2), (1, N))).then_inc(on["rec_stored"], 16)
                sp.wait_ge(on["turned_profiles_copied"], g * per["turned_profiles_copied"] + per["turned_profiles_copied"])
                sp.dma_start(pt.rearrange("a u f -> u a f"), rows(big, 0, PROF, 0, (FR, 2), (1, FR))).then_inc(on["cut_stored"], 16)
                sp.dma_start(rnt, rows(big, 0, 2 * D, 2 * FR, (1, FR))).then_inc(on["cut_stored"], 16)
                sp.wait_ge(on["cut_stored"], g * per["cut_stored"] + per["cut_stored"])
                passed(sp)
                sp.wait_ge(on["conv"], g * per["conv"] + per["conv"])
                passed(sp)
                for u in range(2):
                    for ax, at, no in ((0, WY, D), (1, WX, 32)):
                        sp.dma_start(rows(pool_a, 64 * u, 64 * u + 64, at, (64, no), (1, 64)),
                                              flat(pt, (ax * PROF + 32 - no) * FR + 64 * u, (FR, 64), (FR, no), (1, 64))).then_inc(on["cut_loaded"], 16)
                for q in range(4):
                    sp.dma_start(rows(pool_a, 32 * q, 32 * q + 32, NY, (1, 7 * FR)), flat(rnt, 7 * FR * q, (0, 32), (1, 7 * FR))).then_inc(on["cut_norms_loaded"], 16)
                    sp.dma_start(rows(small, 32 * q + 32 - D, 32 * q + 32, NX, (1, FR)), rnt[D:2 * D, :]).then_inc(on["cut_norms_loaded"], 16)
                sp.wait_ge(on["rec_stored"], g * per["rec_stored"] + per["rec_stored"])
                passed(sp)
                sp.wait_ge(on["where_h1"], g * per["where_h1"] + per["where_h1"])
                passed(sp)
                for q in range(4):
                    for ax, at in ((0, RBY), (1, RBX)):
                        sp.dma_start(rows(pool_b, 32 * q, 32 * q + 32, at, (1, 2048)), flat(rnd, (ax * FR + 32 * q) * N, (0, 32), (1, 2048))).then_inc(on["rec_norms_loaded"], 16)
                sp.wait_ge(on["o1"], g * per["o1"] + per["o1"])
                for q in range(4):
                    for ax, at in ((0, WRY), (1, WRX)):
                        sp.dma_start(rows(pool_b, 32 * q, 32 * q + 32, at, (64, 32), (1, 64)),
                                              flat(pd, (ax * FR + 32 * q) * PROF, (1, 32), (PROF, 32), (1, 64))).then_inc(on["rec_loaded"], 16)
                sp.wait_ge(on["dec_sig"], g * per["dec_sig"] + per["dec_sig"])
                sp.dma_start(ds.rearrange("s a b -> s (a b)"), rows(pool_a, 0, S, SG, (1, D * D))).then_inc(on["dec_stored"], 16)
                sp.wait_ge(on["dec_stored"], g * per["dec_stored"] + per["dec_stored"])
                for q in range(4):
                    sp.dma_start(rows(digit, 32 * q + 32 - D, 32 * q + 32, 32 * q + 32 - D, (128, S), (1, D)),
                                          ds.rearrange("s a b -> a s b")).then_inc(on["digit_loaded"], 16)
                sp.wait_ge(on["dft_copied"], g * per["dft_copied"] + per["dft_copied"])
                for h in range(2):
                    for a, b, to in ((0, 32, 1), (32, 33, 33), (33, 49, 38), (49, 64, 54)):
                        dst = zs[to:to + b - a].rearrange("k (p h) n -> k h p n", h=2)[:, h]
                        sp.dma_start(dst, rows(pool_b, 64 * h + a, 64 * h + b, ZZ, (S * NA, 8), (1, S * NA))).then_inc(on["z_stored"], 16)
                sp.wait_ge(on["z_stored"], g * per["z_stored"] + per["z_stored"])
                for w in range(4):
                    for part in range(2):
                        s0 = 36 * part + w
                        d = zs[s0:s0 + 33:2].rearrange("b c n -> c b n")
                        p0 = 32 * w + 16 * part
                        sp.dma_start(rows(pool_a, p0, p0 + 16, VV, (S * NA, KB), (1, S * NA)), d).then_inc(on["v_loaded"], 16)
                sp.wait_ge(on["mixed_copied"], g * per["mixed_copied"] + per["mixed_copied"])
                for par in range(2):
                    for w in range(2):
                        for part in range(2):
                            p0 = 64 * par + 32 * w + 16 * part
                            dst = ys[part, w:w + 33:2, :, par * S * NH:(par + 1) * S * NH].rearrange("b c n -> c b n")
                            sp.dma_start(dst, rows(pool_b, p0, p0 + 16, YO, (S * NH, KB), (1, S * NH))).then_inc(on["y_stored"], 16)
                sp.wait_ge(on["y_stored"], g * per["y_stored"] + per["y_stored"])
                for h in range(2):
                    for a, b, part, k in ((0, 32, 0, 0), (32, 33, 0, 32), (33, 49, 1, 1), (49, 64, 1, 17)):
                        d = ys[part, k:k + b - a].rearrange("k (p h) n -> k h p n", h=2)[:, h]
                        sp.dma_start(rows(pool_b, 64 * h + a, 64 * h + b, ZZ, (2 * S * NH, 8), (1, 2 * S * NH)), d).then_inc(on["y_loaded"], 16)
                sp.wait_ge(on["xn_ready"], g * per["xn_ready"] + 3)
                for h in range(2):
                    dst = xs[1:65].rearrange("k (p h) n -> k h p n", h=2)[:, h]
                    sp.dma_start(dst, rows(pool_a, 64 * h, 64 * h + 64, XNB, (S * N, 8), (1, S * N))).then_inc(on["xn2_stored"], 16)
                sp.wait_ge(on["xn2_stored"], g * per["xn2_stored"] + per["xn2_stored"])
                for w in range(8):
                    d = xs[w:w + 61:6].rearrange("b c n -> c b n")
                    sp.dma_start(rows(pool_a, 16 * w, 16 * w + 16, VV, (S * N, WB), (1, S * N)), d).then_inc(on["v2_loaded"], 16)
                sp.wait_ge(on["conv2_copied"], g * per["conv2_copied"] + per["conv2_copied"])
                passed(sp)
                sp.wait_ge(on["edge_cleared"], g * per["edge_cleared"] + per["edge_cleared"])
                passed(sp)
                for w in range(6):
                    nb = WB if w < 3 else WB - 1
                    dst = y2s[w:w + 6 * (nb - 1) + 1:6].rearrange("b c n -> c b n")
                    sp.dma_start(dst, rows(pool_b, 16 * w, 16 * w + 16, 0, (S * N, nb), (1, S * N))).then_inc(on["y2_stored"], 16)
                sp.wait_ge(on["y2_stored"], g * per["y2_stored"] + per["y2_stored"])
                for h in range(2):
                    d = y2s[0:64].rearrange("k (p h) n -> k h p n", h=2)[:, h]
                    sp.dma_start(rows(pool_a, 64 * h, 64 * h + 64, 0, (S * N, 8), (1, S * N)), d).then_inc(on["y2_loaded"], 16)
                sp.wait_ge(on["turned_copied"], g * per["turned_copied"] + per["turned_copied"])
                for sh in range(2):
                    for s4 in range(4):
                        dst = out[bass.ds(b0 + (4 * sh + s4), 1)].rearrange("s (p h) (n e) m -> (s n) (p h) (e m)", h=2, e=2)
                        sp.dma_start(dst, rows(pool_b, 32 * s4, 32 * s4 + 32, 2048 * sh, (128, 16), (1, 128))).then_inc(on["out_stored"], 16)
                sp.wait_ge(on["out_stored"], g * per["out_stored"] + per["out_stored"])
                sp.sem_inc(on["group_begun"], 1)

        @block.gpsimd
        def _(pool):
            nc.gpsimd.memset(digit[:, :], 0.0).then_inc(cleared, 1)
            nc.gpsimd.memset(view(small, NX, (1, FR)), 0.0).then_inc(cleared, 1)
            nc.gpsimd.memset(view(pool_a, 8192, (1, 8)), 0.0).then_inc(cleared, 1)
            nc.gpsimd.sem_inc(on["group_begun"], 1)
            pool.wait_ge(loaded, 16 * (len(PERSIST) + 3))
            with pool.Fori(0, groups) as g:
                pool.wait_ge(on["rec_norms_loaded"], g * per["rec_norms_loaded"] + per["rec_norms_loaded"])
                pool.wait_ge(on["rec_loaded"], g * per["rec_loaded"] + per["rec_loaded"])
                w = view(pool_b, WRX, (1, 2048))
                nc.gpsimd.tensor_tensor(w, w, view(pool_b, RBX, (1, 2048)), ALU.mult).then_inc(on["wrx_normed"], 1)

        @block.scalar
        def _(act):
            def copy(o, i):
                return nc.scalar.activation(o, i, ACT.Copy)

            act.wait_ge(loaded, 16 * (len(PERSIST) + 3))
            with act.Fori(0, groups) as g:
                def squares(k, src_ap, dst_ap):
                    nc.scalar.activation(dst_ap, src_ap, ACT.Square).then_inc(on["squares"], 1)
                    act.wait_ge(on["variance"], g * per["variance"] + k)
                    v = view(small, RS, (1, 32 if k == 1 else 64))
                    nc.scalar.activation(v, v, ACT.Sqrt).then_inc(on["deviation"], 1)

                act.wait_ge(on["raw_loaded"], g * per["raw_loaded"] + per["raw_loaded"])
                squares(1, raw[:, :], view(pool_b, FRN, (1, 4096)))
                for j in range(4):
                    act.wait_ge(on["conv"], g * per["conv"] + j + 1)
                    copy(rows(pool_b, 0, CM, FC + 32 * j, (1, 32), (FR, XS)), bank(j, 0, CM, 0, (XS, 32), (1, XS))).then_inc(on["conv_copied"], 1)
                act.wait_ge(on["conv_shifted"], g * per["conv_shifted"] + per["conv_shifted"])
                fc = rows(pool_b, 0, CM, FC, (1, XS * FR))
                nc.scalar.activation(fc, fc, ACT.Exp).then_inc(on["conv_exp"], 1)
                act.wait_ge(on["where_h1"], g * per["where_h1"] + per["where_h1"])
                nc.scalar.activation(rows(big, 0, HID, H1, (1, 256)), bank(6, 0, HID, 0, (1, 256)), ACT.Relu).then_inc(on["where_h1_copied"], 1)
                act.wait_ge(on["where_h2"], g * per["where_h2"] + per["where_h2"])
                nc.scalar.activation(rows(big, 0, HID, H2, (1, FR)), bank(4, 0, HID, 0, (1, FR)), ACT.Relu).then_inc(on["where_h2_copied"], 1)
                act.wait_ge(on["where_zz"], g * per["where_zz"] + per["where_zz"])
                nc.scalar.activation(view(small, ZT, (1, 2)), view(small, ZI, (1, 2)), ACT.Tanh).then_inc(on["where_tanh"], 1)
                act.wait_ge(on["shift"], g * per["shift"] + per["shift"])
                for j in range(4):
                    t = view(small, TT + 1 - j % 2, (1, 1))
                    ins = nc.scalar.activation(view(small, PR + PROF * j, (1, PROF)), tab["iota"][:, :], ACT.Abs, bias=t, scale=1.0 if j < 2 else -1.0)
                ins.then_inc(on["profile_abs"], 1)
                act.wait_ge(on["profiles_turned"], g * per["profiles_turned"] + per["profiles_turned"])
                copy(rows(big, 0, PROF, 0, (1, 2 * FR)), bank(6, 0, PROF, 0, (1, 2 * FR)))
                copy(rows(big, 0, 2 * D, 2 * FR, (1, FR)), bank(6, 0, 2 * D, 2 * FR, (1, FR))).then_inc(on["turned_profiles_copied"], 1)
                for k in range(8):
                    act.wait_ge(on["o1"], g * per["o1"] + k + 1)
                    u = k // 4
                    copy(rows(pool_a, 64 * u, 64 * u + 64, O1 + 448 * (k % 4), (1, 448)), bank(k, 64 * u, 64 * u + 64, 0, (1, 448))).then_inc(on["o1_copied"], 1)
                for k in range(0, 8, 2):
                    act.wait_ge(on["digits"], g * per["digits"] + k + 1)
                    for q in range(4):
                        ins = copy(rows(pool_a, 32 * q, 32 * q + 32, DG + 16 * (k // 2), (1, 16), (FR, 7)), bank(4 + k % 4, 0, 32, 7 * q, (28, 16), (1, 7)))
                    ins.then_inc(on["digits_copied_a"], 1)
                act.wait_ge(on["what_h1"], g * per["what_h1"] + per["what_h1"])
                for k in range(4):
                    ins = nc.scalar.activation(rows(big, 0, HID, HW1 + FR * k, (1, FR)), bank(0, 0, HID, FR * k, (1, FR)), ACT.Relu,
                                               bias=rows(tab["what_b1"], 0, HID, k, (1, 1)))
                ins.then_inc(on["what_h1_copied"], 1)
                act.wait_ge(on["what_h2"], g * per["what_h2"] + per["what_h2"])
                for k in range(2):
                    ins = nc.scalar.activation(rows(big, 0, HID, HW2 + FR * k, (1, FR)), bank(1, 0, HID, FR * k, (1, FR)), ACT.Relu,
                                               bias=rows(tab["what_b2"], 0, HID, k, (1, 1)))
                ins.then_inc(on["what_h2_copied"], 1)
                act.wait_ge(on["what_z"], g * per["what_z"] + per["what_z"])
                nc.scalar.activation(rows(big, 0, 10, ZW, (1, S)), bank(2, 0, 10, 0, (1, S)), ACT.Identity,
                                          bias=rows(tab["what_bloc"], 0, 10, 0, (1, 1))).then_inc(on["what_z_copied"], 1)
                act.wait_ge(on["dec_h1"], g * per["dec_h1"] + per["dec_h1"])
                for k in range(2):
                    ins = nc.scalar.activation(rows(big, 0, HID, D1 + S * k, (1, S)), bank(3, 0, HID, S * k, (1, S)), ACT.Relu,
                                               bias=rows(tab["dec_b1"], 0, HID, k, (1, 1)))
                ins.then_inc(on["dec_h1_copied"], 1)
                act.wait_ge(on["dec_h2"], g * per["dec_h2"] + per["dec_h2"])
                for k in range(4):
                    ins = nc.scalar.activation(rows(big, 0, HID, D2 + S * k, (1, S)), bank(0, 0, HID, S * k, (1, S)), ACT.Relu,
                                               bias=rows(tab["dec_b2"], 0, HID, k, (1, 1)))
                ins.then_inc(on["dec_h2_copied"], 1)
                act.wait_ge(on["dec_out"], g * per["dec_out"] + per["dec_out"])
                nc.scalar.activation(rows(pool_a, 0, S, SG, (392, 2), (1, 392)), bank(1, 0, S, 0, (512, 2), (1, 392)), ACT.Tanh, scale=0.5).then_inc(on["dec_tanh"], 1)
                for k in range(8):
                    act.wait_ge(on["x1"], g * per["x1"] + k + 1)
                    q, hs = k % 4, k // 4
                    copy(view(x1, 1024 * q + 256 * hs, (512, 2), (1, 256)), bank(4 + q, 0, 128, 0, (256, 2), (1, 256))).then_inc(on["x1_copied"], 1)
                act.wait_ge(on["x1_copied"], g * per["x1_copied"] + per["x1_copied"])
                squares(2, x1[:, :], view(pool_b, ZZ, (1, 4096)))
                for k in range(10):
                    act.wait_ge(on["dft"], g * per["dft"] + k + 1)
                    w = min(7, 64 - 7 * k) * NA
                    copy(view(pool_b, ZZ + 7 * NA * k, (1, w)), bank(k % 8, 0, 128, 0, (1, w))).then_inc(on["dft_copied"], 1)
                for k in range(12):
                    act.wait_ge(on["mixed"], g * per["mixed"] + k + 1)
                    m = 3 if k < 11 else 1
                    copy(view(pool_b, YO + 3 * k, (NH, KB * S), (1, m)), bank(k % 8, 0, 128, 0, (1, KB * S), (KB * S, m))).then_inc(on["mixed_copied"], 1)
                act.wait_ge(on["corr"], g * per["corr"] + per["corr"])
                copy(view(small, ES, (1, 256)), bank(4, 0, 128, 0, (1, 256))).then_inc(on["corr_copied"], 1)
                act.wait_ge(on["x2_ready"], g * per["x2_ready"] + per["x2_ready"])
                squares(3, x1[:, :], view(pool_b, ZZ, (1, 4096)))
                act.wait_ge(on["xn_ready"], g * per["xn_ready"] + 3)
                for k in range(WB):
                    act.wait_ge(on["conv2"], g * per["conv2"] + k + 1)
                    copy(rows(pool_b, 0, 96, S * N * k, (N, S), (1, N - 1)), bank(k % 8, 0, 96, 0, (N, S), (1, N - 1))).then_inc(on["conv2_copied"], 1)
                act.wait_ge(on["x3_ready"], g * per["x3_ready"] + per["x3_ready"])
                squares(4, x1[:, :], view(pool_b, 0, (1, 4096)))
                for k in range(8):
                    act.wait_ge(on["turned"], g * per["turned"] + k + 1)
                    copy(view(pool_b, 512 * k, (128, 4), (64, 2), (1, 64)), bank(k, 0, 128, 0, (64, 4), (256, 2), (1, 64))).then_inc(on["turned_copied"], 1)

        @block.vector
        def _(dve):
            dve.wait_ge(loaded, 16 * (len(PERSIST) + 3))
            setup = [0]

            def step(ins):
                setup[0] += 1
                ins.then_inc(mixing, 1)
                dve.wait_ge(mixing, setup[0])

            P = lambda j: view(pool_a, 64 * j, (1, 64))
            sa, sb_ = view(pool_a, 384, (1, 64)), view(pool_a, 448, (1, 64))
            tmp = [view(pool_a, 512 + 64 * j, (1, 64)) for j in range(5)]
            step(nc.vector.tensor_tensor(tmp[0], P(2), sa, ALU.mult))
            step(nc.vector.tensor_tensor(tmp[1], P(0), P(4), ALU.add))
            step(nc.vector.tensor_tensor(tmp[1], tmp[1], sa, ALU.mult))
            step(nc.vector.tensor_tensor(tmp[2], P(1), P(5), ALU.subtract))
            step(nc.vector.tensor_tensor(tmp[2], tmp[2], sb_, ALU.mult))
            mw = view(mix_w, 0, (64, N), (1, 64))
            t1 = view(pool_b, 0, (64, N), (1, 64))
            ang = lambda n: view(tab[n], 0, (1, N), (0, 64))
            over = lambda j: view(pool_a, 512 + 64 * j, (0, N), (1, 64))
            step(nc.vector.tensor_tensor(mw, ang("cos"), over(1), ALU.mult))
            step(nc.vector.tensor_tensor(mw, mw, over(0), ALU.add))
            step(nc.vector.tensor_tensor(t1, ang("sin"), over(2), ALU.mult))
            step(nc.vector.tensor_tensor(mw, mw, t1, ALU.add))
            for j, (p, s_, c_) in enumerate(((0, sa, -1), (1, sb_, -1), (4, sa, -1), (5, sb_, 1))):
                step(nc.vector.scalar_tensor_tensor(view(mix_e, 64 * j, (1, 64)), P(p), c_ / N, s_, ALU.mult, ALU.mult))
            with dve.Fori(0, groups) as g:
                links = [0]

                def link(ins):
                    links[0] += 1
                    ins.then_inc(on["vector_link"], 1)
                    dve.wait_ge(on["vector_link"], g * per["vector_link"] + links[0])

                def normalise(k, source, pairs, length, dst, sums_first):
                    sq = view(pool_b, 0, (length, pairs), (1, length))
                    link(nc.vector.tensor_reduce(view(small, ST, (1, pairs)), source, AX, ALU.add))
                    dve.wait_ge(on["squares"], g * per["squares"] + k)
                    nc.vector.tensor_reduce(view(small, ST + pairs, (1, pairs)), sq, AX, ALU.add).then_inc(on["sums"], 1)
                    dve.wait_ge(on["stats"], g * per["stats"] + k)
                    pb = lambda o: bank(7, 0, 128, o, (1, pairs))
                    v = lambda o: view(small, o, (1, pairs))
                    link(nc.vector.tensor_scalar(v(MS), pb(0), 1.0 / CNT, None, ALU.mult))
                    link(nc.vector.tensor_tensor(v(TV), v(MS), v(MS), ALU.mult))
                    link(nc.vector.scalar_tensor_tensor(v(RS), pb(pairs), 1.0 / CNT, v(TV), ALU.mult, ALU.subtract))
                    nc.vector.tensor_scalar(v(RS), v(RS), EPS, None, ALU.add).then_inc(on["variance"], 1)
                    dve.wait_ge(on["deviation"], g * per["deviation"] + k)
                    link(nc.vector.reciprocal(v(RS), v(RS)))
                    link(nc.vector.scalar_tensor_tensor(v(NM), v(MS), -1.0, v(RS), ALU.mult, ALU.mult))
                    wide_ = lambda o: view(small, o, (1, pairs), (0, length))
                    link(nc.vector.tensor_tensor(dst, source, wide_(RS), ALU.mult))
                    ins = nc.vector.tensor_tensor(dst, dst, wide_(NM), ALU.add)
                    ins.then_inc(on["xn_ready"], 1)
                    dve.wait_ge(on["xn_ready"], g * per["xn_ready"] + k)

                dve.wait_ge(on["raw_loaded"], g * per["raw_loaded"] + per["raw_loaded"])
                normalise(1, view(raw, 0, (128, 32), (1, 128)), 32, 128, view(pool_b, FRN, (128, 32), (1, 128)), None)
                dve.wait_ge(on["conv_copied"], g * per["conv_copied"] + per["conv_copied"])
                last = rows(pool_b, 0, CM, FC + FR * (XS - 1), (1, FR))
                link(nc.vector.tensor_scalar(last, last, rows(tab["ok"], 0, CM, XS - 1, (1, 1)), rows(tab["low"], 0, CM, 0, (1, 1)), ALU.mult, ALU.add))
                fcv = rows(pool_b, 0, CM, FC, (1, FR), (FR, XS))
                nc.vector.tensor_reduce(rows(small, 0, CM, PM, (1, FR)), fcv, AX, ALU.max).then_inc(on["conv_max"], 1)
                dve.wait_ge(on["max_turned"], g * per["max_turned"] + per["max_turned"])
                link(nc.vector.tensor_reduce(view(small, MX, (1, 1)), bank(4, 0, 128, 0, (1, CM)), AX, ALU.max))
                nc.vector.tensor_scalar(view(small, DGM, (1, 128)), tab["ident"][:, :], view(small, MX, (1, 1)), None, ALU.mult).then_inc(on["max_diag"], 1)
                dve.wait_ge(on["max_spread"], g * per["max_spread"] + per["max_spread"])
                fcx = rows(pool_b, 0, CM, FC, (FR, XS), (1, FR))
                nc.vector.tensor_tensor(fcx, fcx, bank(5, 0, CM, 0, (0, XS), (1, FR)), ALU.subtract).then_inc(on["conv_shifted"], 1)
                dve.wait_ge(on["exp_sum"], g * per["exp_sum"] + per["exp_sum"])
                nc.vector.tensor_copy(rows(small, 0, 1, SR, (1, FR)), bank(4, 0, 1, 0, (1, FR))).then_inc(on["exp_sum_copied"], 1)
                dve.wait_ge(on["where_z"], g * per["where_z"] + per["where_z"])
                link(nc.vector.reciprocal(view(small, MX, (1, 1)), bank(5, 0, 128, 2, (1, 1))))
                nc.vector.scalar_tensor_tensor(view(small, ZI, (1, 2)), bank(5, 0, 128, 0, (1, 2)), view(small, MX, (1, 1)),
                                                    tab["where_bloc"][:, :], ALU.mult, ALU.add).then_inc(on["where_zz"], 1)
                dve.wait_ge(on["where_tanh"], g * per["where_tanh"] + per["where_tanh"])
                nc.vector.tensor_scalar(view(small, TT, (1, 2)), view(small, ZT, (1, 2)), 1.0, (N - D) / 2, ALU.add, ALU.mult).then_inc(on["shift"], 1)
                dve.wait_ge(on["profile_abs"], g * per["profile_abs"] + per["profile_abs"])
                pr = view(small, PR, (1, 384))
                t_b, t_a, t_c = view(big, 0, (1, 384)), view(big, 384, (1, 384)), view(pool_a, SG, (1, 384))
                link(nc.vector.tensor_scalar(t_b, pr, 2.0, 0.0, ALU.subtract, ALU.min))
                link(nc.vector.tensor_scalar(t_a, pr, 1.0, 0.0, ALU.subtract, ALU.min))
                link(nc.vector.tensor_tensor(t_c, t_b, t_b, ALU.mult))
                link(nc.vector.scalar_tensor_tensor(t_b, t_b, 1.0, t_c, ALU.add, ALU.mult))
                link(nc.vector.tensor_tensor(t_c, t_a, t_a, ALU.mult))
                link(nc.vector.tensor_scalar(t_a, t_a, 2.0, 1.0, ALU.mult, ALU.add))
                link(nc.vector.tensor_tensor(t_a, t_a, t_c, ALU.mult))
                link(nc.vector.scalar_tensor_tensor(pr, t_b, -0.5, t_a, ALU.mult, ALU.add))
                for ax in range(2):
                    nc.vector.tensor_reduce(view(small, TOT + D * ax, (1, D)), view(small, PR + PROF * ax + 4, (1, D), (1, N)), AX, ALU.add)
                    ins = nc.vector.tensor_reduce(view(small, TOT + 2 * D + N * ax, (1, N)), view(small, PR + PROF * (2 + ax) + 4, (1, N), (1, D)), AX, ALU.add)
                    t = view(small, TT + 1 - ax, (1, 1))
                    nc.vector.tensor_scalar(view(small, SS + D * ax, (1, D)), view(tab["place"], D * ax, (1, D)), t, 0.5, ALU.subtract, ALU.subtract)
                    o = 2 * D + N * ax
                    ins = nc.vector.tensor_scalar(view(small, SS + o, (1, N)), view(tab["place"], o, (1, N)), t, 0.5, ALU.subtract, ALU.subtract)
                link(ins)
                w = 2 * D + 2 * N
                v = lambda o: view(small, o, (1, w))
                link(nc.vector.tensor_scalar(v(TMP), v(TOT), THR, None, ALU.is_gt))
                link(nc.vector.scalar_tensor_tensor(v(TMP), v(SS), -0.5, v(TMP), ALU.is_ge, ALU.mult))
                for o, m, hi in ((0, 2 * D, N - 0.5), (2 * D, 2 * N, D - 0.5)):
                    q_ = view(small, TMP + o, (1, m))
                    ins = nc.vector.scalar_tensor_tensor(q_, view(small, SS + o, (1, m)), hi, q_, ALU.is_le, ALU.mult)
                link(ins)
                link(nc.vector.tensor_scalar(v(TOT), v(TOT), THR, None, ALU.max))
                link(nc.vector.reciprocal(v(TOT), v(TOT)))
                nc.vector.tensor_tensor(v(RN), v(TOT), v(TMP), ALU.mult).then_inc(on["norms"], 1)
                for k in range(1, 8, 2):
                    dve.wait_ge(on["digits"], g * per["digits"] + k + 1)
                    for q in range(4):
                        ins = nc.vector.tensor_copy(rows(pool_a, 32 * q, 32 * q + 32, DG + 64 + 16 * (k // 2), (1, 16), (FR, 7)),
                                                    bank(4 + k % 4, 0, 32, 7 * q, (28, 16), (1, 7)))
                    ins.then_inc(on["digits_copied_v"], 1)
                dve.wait_ge(on["digits_copied_v"], g * per["digits_copied_v"] + per["digits_copied_v"])
                dve.wait_ge(on["digits_copied_a"], g * per["digits_copied_a"] + per["digits_copied_a"])
                dve.wait_ge(on["cut_norms_loaded"], g * per["cut_norms_loaded"] + per["cut_norms_loaded"])
                dg = view(pool_a, DG, (FR, 7), (1, FR))
                link(nc.vector.tensor_tensor(dg, dg, view(pool_a, NY, (FR, 7), (1, FR)), ALU.mult))
                nc.vector.tensor_tensor(dg, dg, view(small, NX, (0, 7), (1, FR)), ALU.mult).then_inc(on["digits_normed"], 1)
                dve.wait_ge(on["what_h2_copied"], g * per["what_h2_copied"] + per["what_h2_copied"])
                for k in range(2):
                    ins = nc.vector.tensor_reduce(rows(big, 0, HID, HS + S * k, (1, S)), rows(big, 0, HID, HW2 + FR * k, (4, S), (32, 4), (1, 4)), mybir.AxisListType.XY, ALU.add)
                ins.then_inc(on["what_sum"], 1)
                dve.wait_ge(on["dec_tanh"], g * per["dec_tanh"] + per["dec_tanh"])
                sg = rows(pool_a, 0, S, SG, (1, D * D))
                nc.vector.tensor_scalar(sg, sg, 0.5, 0.5, ALU.mult, ALU.add).then_inc(on["dec_sig"], 1)
                for k in range(4):
                    dve.wait_ge(on["aa"], g * per["aa"] + k + 1)
                    nc.vector.tensor_tensor(view(pool_a, AA + 512 * k, (1, 512)), bank(k, 0, 128, 0, (1, 512)), view(pool_b, RBY + 512 * k, (1, 512)), ALU.mult).then_inc(on["aa_copied"], 1)
                dve.wait_ge(on["x1_copied"], g * per["x1_copied"] + per["x1_copied"])
                normalise(2, view(x1, 0, (64, 64), (1, 64)), 64, 64, view(pool_a, XNB, (NA, 64), (1, 64)), None)
                xn = view(pool_a, XNB, (NA, 64), (1, 64))
                for j, n in enumerate(("cos", "sin")):
                    t = view(pool_b, 0, (64, 64), (1, 64))
                    link(nc.vector.tensor_tensor(t, xn, view(tab[n], 0, (0, 64), (1, 64)), ALU.mult))
                    link(nc.vector.tensor_reduce(view(pool_a, XNB + N + 1 + j, (NA, 64)), t, AX, ALU.add))
                nc.vector.tensor_reduce(view(pool_a, XNB + N, (NA, 64)), xn, AX, ALU.add).then_inc(on["moments"], 1)
                for k in range(8):
                    dve.wait_ge(on["idft"], g * per["idft"] + k + 1)
                    o = view(x1, 512 * k, (1, 2), (64, S), (2, 32))
                    nc.vector.tensor_tensor(o, o, bank(k % 4, 0, 128, 0, (256, 2), (32, S), (1, 32)), ALU.add).then_inc(on["x2_ready"], 1)
                dve.wait_ge(on["x2_ready"], g * per["x2_ready"] + per["x2_ready"])
                full = view(x1, 0, (64, 64), (1, 64))
                normalise(3, full, 64, 64, view(pool_a, XNB, (64, 64), (1, 64)), None)
                nc.vector.memset(rows(pool_b, 0, 96, N - 1, (N, WB * S)), 0.0).then_inc(on["edge_cleared"], 1)
                dve.wait_ge(on["y2_loaded"], g * per["y2_loaded"] + per["y2_loaded"])
                nc.vector.tensor_tensor(x1[:, :], x1[:, :], view(pool_a, 0, (1, 4096)), ALU.add).then_inc(on["x3_ready"], 1)
                dve.wait_ge(on["x3_ready"], g * per["x3_ready"] + per["x3_ready"])
                normalise(4, full, 64, 64, view(pool_a, 0, (64, 64), (1, 64)), None)
                link(nc.vector.tensor_reduce(view(small, ST, (1, 64)), view(pool_a, 0, (64, 64), (1, 64)), AX, ALU.add))
                for j in range(2):
                    nc.vector.tensor_tensor(view(pool_a, 4096 + 2048 * j, (64, 32), (1, 64)), view(pool_a, 2048 * j, (64, 32), (1, 64)),
                                                 view(small, ST + 32 * (1 - j), (1, 32), (0, 64)), ALU.mult).then_inc(on["gate_prod"], 1)
                for k in range(8):
                    dve.wait_ge(on["gate_sum"], g * per["gate_sum"] + k + 1)
                    o = view(pool_a, 512 * k, (1, 512))
                    nc.vector.scalar_tensor_tensor(o, bank(k, 0, 128, 0, (1, 512)), 0.0, o, ALU.is_gt, ALU.mult).then_inc(on["gated"], 1)
                dve.wait_ge(on["gated"], g * per["gated"] + per["gated"])
                nc.vector.tensor_tensor(x1[:, :], x1[:, :], view(pool_a, 0, (1, 4096)), ALU.add).then_inc(on["added"], 1)
                assert links[0] == LINKS, links

        @block.tensor
        def _(pe):
            mm = nc.tensor.matmul
            pe.wait_ge(loaded, 16 * (len(PERSIST) + 3))
            pe.wait_ge(mixing, 13)
            pe.wait_ge(cleared, 3)
            with pe.Fori(0, groups) as g:
                def stats(k, pairs, table):
                    pe.wait_ge(on["sums"], g * per["sums"] + k)
                    mm(bank(7, 0, 128, 0, (1, 2 * pairs)), tab[table][:, :], view(small, ST, (1, 2 * pairs)), start=True, stop=True).then_inc(on["stats"], 1)

                stats(1, 32, "halves")
                pe.wait_ge(on["xd_loaded"], g * per["xd_loaded"] + per["xd_loaded"])
                for j in range(4):
                    for e in range(TAPS):
                        ins = mm(bank(j, 0, CM, 0, (XS, 32), (1, XS)), view(tab["toep"], CM * e, (1, CM)),
                                 view(pool_a, XD + 1 + 64 * 32 * j + 2 * e, (64, 32), (3, XS)), start=e == 0, stop=e == TAPS - 1)
                    ins.then_inc(on["conv"], 1)
                pe.wait_ge(on["conv_max"], g * per["conv_max"] + per["conv_max"])
                nc.tensor.transpose(bank(4, 0, 128, 0, (1, CM)), rows(small, 0, CM, PM, (1, FR)), rows(tab["ident"], 0, CM, 0, (1, CM))).then_inc(on["max_turned"], 1)
                pe.wait_ge(on["max_diag"], g * per["max_diag"] + per["max_diag"])
                mm(bank(5, 0, CM, 0, (1, FR)), view(tab["ones"], 0, (1, CM)), view(small, DGM, (1, FR)), start=True, stop=True).then_inc(on["max_spread"], 1)
                pe.wait_ge(on["conv_exp"], g * per["conv_exp"] + per["conv_exp"])
                fc = lambda X: rows(pool_b, 0, CM, FC + FR * X, (1, FR))
                for X in range(XS):
                    ins = mm(bank(4, 0, 1, 0, (1, FR)), rows(tab["ok"], 0, CM, X, (1, 1)), fc(X), start=X == 0, stop=X == XS - 1)
                ins.then_inc(on["exp_sum"], 1)
                pe.wait_ge(on["exp_sum_copied"], g * per["exp_sum_copied"] + per["exp_sum_copied"])
                sr = rows(small, 0, 1, SR, (1, FR))
                for h in range(2):
                    for X in range(XS):
                        mm(bank(6, 0, HID, FR * h, (1, FR)), rows(tab["where_w1"], 0, CM, 2 * HID * X + HID * h, (1, HID)), fc(X), start=X == 0, stop=False)
                    ins = mm(bank(6, 0, HID, FR * h, (1, FR)), rows(tab["where_b1"], 0, 1, HID * h, (1, HID)), sr, start=False, stop=True)
                ins.then_inc(on["where_h1"], 1)
                pe.wait_ge(on["where_h1_copied"], g * per["where_h1_copied"] + per["where_h1_copied"])
                for h in range(2):
                    mm(bank(4, 0, HID, 0, (1, FR)), rows(tab["where_w2"], 0, HID, HID * h, (1, HID)), rows(big, 0, HID, H1 + FR * h, (1, FR)), start=h == 0, stop=False)
                mm(bank(4, 0, HID, 0, (1, FR)), tab["where_b2"][0:1, :], sr, start=False, stop=True).then_inc(on["where_h2"], 1)
                pe.wait_ge(on["where_h2_copied"], g * per["where_h2_copied"] + per["where_h2_copied"])
                mm(bank(5, 0, 128, 0, (1, 2)), rows(big, 0, HID, H2, (1, FR)), tab["where_wloc"][0:HID, :], start=True, stop=True)
                mm(bank(5, 0, 128, 2, (1, 1)), sr, rows(tab["ones"], 0, 1, 0, (1, 1)), start=True, stop=True).then_inc(on["where_z"], 1)

                pe.wait_ge(on["norms"], g * per["norms"] + per["norms"])
                for j in range(2):
                    nc.tensor.transpose(bank(6, 0, PROF, FR * j, (1, FR)), view(small, PR + PROF * j, (1, PROF)), tab["ident"][:, :])
                nc.tensor.transpose(bank(6, 0, 2 * D, 2 * FR, (1, FR)), view(small, RN, (1, 2 * D)), tab["ident"][:, :]).then_inc(on["profiles_turned"], 1)
                pe.wait_ge(on["turned_profiles_copied"], g * per["turned_profiles_copied"] + per["turned_profiles_copied"])
                pe.wait_ge(on["cut_loaded"], g * per["cut_loaded"] + per["cut_loaded"])
                for k in range(8):
                    u, t4 = k // 4, k % 4
                    passed(pe)
                    for j in range(16):
                        fu = 16 * t4 + j
                        q2, s_, r = fu // 32, fu // 4 % 8, fu % 4
                        ins = mm(bank(k, 64 * u, 64 * u + 64, 28 * j, (1, D)),
                                 rows(pool_b, 64 * u, 64 * u + 64, FRN + 64 * (8 * s_ + 4 * q2 + r), (1, 64)),
                                 rows(pool_a, 64 * u, 64 * u + 64, WY + fu, (64, D)), start=j == 0, stop=True, skip_group_check=True)
                    ins.then_inc(on["o1"], 1)
                pe.wait_ge(on["o1_copied"], g * per["o1_copied"] + per["o1_copied"])
                for k in range(8):
                    u, t4 = k % 2, k // 2
                    if k >= 4:
                        if u == 0:
                            pe.wait_ge(on["digits_copied_a"], g * per["digits_copied_a"] + k // 2 - 1)
                        else:
                            pe.wait_ge(on["digits_copied_v"], g * per["digits_copied_v"] + k // 2 - 1)
                    passed(pe)
                    for j in range(16):
                        fu = 16 * t4 + j
                        ins = mm(bank(4 + k % 4, 0, 32, 28 * j, (1, D)), rows(pool_a, 64 * u, 64 * u + 64, WX + fu, (64, 32)),
                                 rows(pool_a, 64 * u, 64 * u + 64, O1 + 28 * fu, (1, D)), start=j == 0, stop=True, skip_group_check=True)
                    ins.then_inc(on["digits"], 1)
                pe.wait_ge(on["digits_normed"], g * per["digits_normed"] + per["digits_normed"])
                for k in range(4):
                    for i in range(7):
                        ins = mm(bank(0, 0, HID, FR * k, (1, FR)), view(tab["what_w1"], 400 * i + HID * k, (1, HID)),
                                 view(pool_a, DG + FR * i, (1, FR)), start=i == 0, stop=i == 6)
                ins.then_inc(on["what_h1"], 1)
                pe.wait_ge(on["what_h1_copied"], g * per["what_h1_copied"] + per["what_h1_copied"])
                for h in range(2):
                    for k in range(4):
                        ins = mm(bank(1, 0, HID, FR * h, (1, FR)), rows(tab["what_w2"], 0, HID, 200 * k + HID * h, (1, HID)),
                                 rows(big, 0, HID, HW1 + FR * k, (1, FR)), start=k == 0, stop=k == 3)
                ins.then_inc(on["what_h2"], 1)
                pe.wait_ge(on["what_sum"], g * per["what_sum"] + per["what_sum"])
                for k in range(2):
                    ins = mm(bank(2, 0, 10, 0, (1, S)), rows(tab["what_wloc"], 0, HID, 10 * k, (1, 10)), rows(big, 0, HID, HS + S * k, (1, S)), start=k == 0, stop=k == 1)
                ins.then_inc(on["what_z"], 1)
                pe.wait_ge(on["what_z_copied"], g * per["what_z_copied"] + per["what_z_copied"])
                for k in range(2):
                    ins = mm(bank(3, 0, HID, S * k, (1, S)), rows(tab["dec_w1"], 0, 10, HID * k, (1, HID)), rows(big, 0, 10, ZW, (1, S)), start=True, stop=True)
                ins.then_inc(on["dec_h1"], 1)
                pe.wait_ge(on["dec_h1_copied"], g * per["dec_h1_copied"] + per["dec_h1_copied"])
                for k in range(4):
                    for h in range(2):
                        ins = mm(bank(0, 0, HID, S * k, (1, S)), rows(tab["dec_w2"], 0, HID, 400 * h + HID * k, (1, HID)),
                                 rows(big, 0, HID, D1 + S * h, (1, S)), start=h == 0, stop=h == 1)
                ins.then_inc(on["dec_h2"], 1)
                pe.wait_ge(on["dec_h2_copied"], g * per["dec_h2_copied"] + per["dec_h2_copied"])
                for h in range(2):
                    for k in range(4):
                        mm(bank(1 + h, 0, S, 0, (1, 392)), rows(big, 0, HID, D2 + S * k, (1, S)),
                           rows(tab["dec_w3"], 0, HID, D * D * k + 392 * h, (1, 392)), start=k == 0, stop=False)
                    ins = mm(bank(1 + h, 0, S, 0, (1, 392)), rows(tab["ones"], 0, 1, 0, (1, S)), rows(tab["dec_b3"], 0, 1, 392 * h, (1, 392)), start=False, stop=True)
                ins.then_inc(on["dec_out"], 1)
                pe.wait_ge(on["digit_loaded"], g * per["digit_loaded"] + per["digit_loaded"])
                pe.wait_ge(on["rec_loaded"], g * per["rec_loaded"] + per["rec_loaded"])
                for k in range(4):
                    for j in range(2):
                        s_ = 2 * k + j
                        ins = mm(bank(k, 0, 128, 256 * j, (1, 256)), view(digit, 128 * s_, (1, 128)), view(pool_b, WRY + 256 * s_, (1, 256)), start=j == 0, stop=True, skip_group_check=True)
                    ins.then_inc(on["aa"], 1)
                pe.wait_ge(on["aa_copied"], g * per["aa_copied"] + per["aa_copied"])
                pe.wait_ge(on["wrx_normed"], g * per["wrx_normed"] + per["wrx_normed"])
                for hs in range(2):
                    for q in range(4):
                        u = q // 2
                        if hs:
                            pe.wait_ge(on["x1_copied"], g * per["x1_copied"] + q + 1)
                        for j in range(2):
                            for s4 in range(4):
                                s_ = 4 * hs + s4
                                mm(bank(4 + q, 0, 128, 256 * j + 64 * s4, (1, 64)),
                                   rows(raw, 64 * u, 64 * u + 64, 512 * s_ + 256 * (q % 2) + 128 * j, (1, 128)),
                                   rows(tab["ident"], 64 * u, 64 * u + 64, 64 * u, (1, 64)), start=j == 0 and s4 == 0, stop=False, skip_group_check=True)
                    for s4 in range(4):
                        for r in range(4):
                            for q in range(4):
                                s_ = 4 * hs + s4
                                j, h = r // 2, r % 2
                                ins = mm(bank(4 + q, 64 * h, 64 * h + 64, 256 * j + 64 * s4, (1, 64)),
                                         rows(pool_b, 32 * q, 32 * q + 32, WRX + 64 * (4 * s_ + r), (1, 64)),
                                         rows(pool_a, 32 * q, 32 * q + 32, AA + 64 * (4 * s_ + r), (1, 64)), start=False, stop=True, skip_group_check=True)
                                if s4 == 3 and r == 3:
                                    ins.then_inc(on["x1"], 1)
                stats(2, 64, "ones")
                pe.wait_ge(on["moments"], g * per["moments"] + per["moments"])
                for k in range(10):
                    w = min(7, 64 - 7 * k) * NA
                    if k >= 8:
                        pe.wait_ge(on["dft_copied"], g * per["dft_copied"] + k - 7)
                    mm(bank(k % 8, 0, 128, 0, (1, w)), tab["dft"][:, :], view(pool_a, XNB + 7 * NA * k, (1, w)), start=True, stop=True).then_inc(on["dft"], 1)
                pe.wait_ge(on["v_loaded"], g * per["v_loaded"] + per["v_loaded"])
                pe.wait_ge(on["dft_copied"], g * per["dft_copied"] + per["dft_copied"])
                row = lambda n1: view(pool_a, VV + n1, (NA, KB * S))
                for k in range(12):
                    if k >= 8:
                        pe.wait_ge(on["mixed_copied"], g * per["mixed_copied"] + k - 7)
                    for j in range(3 if k < 11 else 1):
                        for par in range(2):
                            n1 = 2 * (3 * k + j) + par
                            o = bank(k % 8, 64 * par, 64 * par + 64, KB * S * j, (1, KB * S))
                            if n1 < N:
                                terms = [(view(mix_w, 64 * n1, (1, 64)), n1)]
                            else:
                                e = lambda i: view(mix_e, 64 * i, (1, 64))
                                terms = {0: [(e(0), N + 1), (e(1), N + 2)], 1: [(e(2), N)], 2: [(e(3), N)], 3: [(e(3), N)]}[n1 - N]
                            for i, (l, r_) in enumerate(terms):
                                last = i == len(terms) - 1 and n1 > 0
                                ins = mm(o, l, row(r_), start=j == 0 and i == 0, stop=last, skip_group_check=True)
                            if n1 == 0:
                                ins = mm(o, tab["l1_bias"][0:1, :], rows(tab["ones"], 0, 1, 0, (0, 2), (1, 68)), start=False, stop=True, skip_group_check=True)
                    ins.then_inc(on["mixed"], 1)
                pe.wait_ge(on["y_loaded"], g * per["y_loaded"] + per["y_loaded"])
                pe.wait_ge(on["mixed_copied"], g * per["mixed_copied"] + per["mixed_copied"])
                for k in range(2):
                    for jj in range(2):
                        ins = mm(bank(4, 64 * jj, 64 * jj + 64, 128 * k, (1, 128)), view(pool_b, ZZ + 4 * 2 * S * NH * k + 32 + jj, (NH, 64)), tab["idft"][:, :],
                                 start=k == 0, stop=True, skip_group_check=True)
                ins.then_inc(on["corr"], 1)
                pe.wait_ge(on["corr_copied"], g * per["corr_copied"] + per["corr_copied"])
                for k in range(8):
                    if k >= 4:
                        pe.wait_ge(on["x2_ready"], g * per["x2_ready"] + k - 3)
                    mm(bank(k % 4, 0, 128, 0, (1, 512)), view(small, ES + 128 * (k // 4), (1, 128)), view(tab["sel"], 512 * (k % 4), (1, 512)), start=True, stop=False, skip_group_check=True)
                    for par in range(2):
                        ins = mm(bank(k % 4, 0, 128, 256 * par, (1, 256)), tab["idft"][:, :],
                                 view(pool_b, ZZ + S * NH * (2 * k + par), (NH, S), (1, 32)), start=False, stop=True, skip_group_check=True)
                    ins.then_inc(on["idft"], 1)
                stats(3, 64, "ones")
                pe.wait_ge(on["v2_loaded"], g * per["v2_loaded"] + per["v2_loaded"])
                for k in range(WB):
                    if k >= 8:
                        pe.wait_ge(on["conv2_copied"], g * per["conv2_copied"] + k - 7)
                    t = lambda ky: view(tab["l2_taps"], 96 * ky, (1, 96))
                    mm(bank(k % 8, 0, 96, 0, (1, 512)), t(1), view(pool_a, 512 * k, (1, 512)), start=True, stop=False, skip_group_check=True)
                    mm(bank(k % 8, 0, 96, 1, (N, S), (1, N - 1)), t(0), view(pool_a, 512 * k, (N, S), (1, N - 1)), start=False, stop=False, skip_group_check=True)
                    mm(bank(k % 8, 0, 96, 0, (N, S), (1, N - 1)), t(2), view(pool_a, 512 * k + 1, (N, S), (1, N - 1)), start=False, stop=True, skip_group_check=True).then_inc(on["conv2"], 1)
                stats(4, 64, "ones")
                for k in range(8):
                    if k % 4 == 0:
                        pe.wait_ge(on["gate_prod"], g * per["gate_prod"] + k // 4 + 1)
                    if k == 7:
                        pe.wait_ge(on["xn_ready"], g * per["xn_ready"] + 4)
                    mm(bank(k, 0, 128, 0, (1, 512)), tab["halves"][:, :], view(pool_a, 4096 + 512 * k, (1, 512)), start=True, stop=True).then_inc(on["gate_sum"], 1)
                pe.wait_ge(on["added"], g * per["added"] + per["added"])
                for k in range(8):
                    sh, p2 = k // 4, k % 4
                    for par in range(2):
                        for j in range(2):
                            pair = 2 * p2 + j
                            ins = nc.tensor.transpose(bank(k, 0, 128, 256 * par + 128 * j, (1, 128)),
                                                      view(x1, 512 * pair + 256 * sh + par, (2, 128)), tab["ident"][:, :])
                    ins.then_inc(on["turned"], 1)


def kernel(**inputs):
    import concourse.bacc as bacc
    from concourse.bass_utils import run_bass_kernel_spmd

    a = {n: np.asarray(v) for n, v in inputs.items()}
    x = np.ascontiguousarray(a.pop("x"))
    nc = bacc.Bacc("TRN2", target_bir_lowering=False, num_devices=1)
    arrays = {"x_dram": x, **{f"{n}_dram": v for n, v in {**layouts(a), **constants()}.items()}}
    aps = {n[:-5]: nc.dram_tensor(n, v.shape, F32, kind="ExternalInput").ap() for n, v in arrays.items()}
    out = nc.dram_tensor("out_dram", x.shape, F32, kind="ExternalOutput").ap()
    program(nc, aps["x"], out, aps, x.shape[0] // S)
    r = run_bass_kernel_spmd(nc, [arrays], core_ids=[0])
    return r.results[0]["out_dram"]
```

```python
from contextlib import ExitStack

import numpy as np

import concourse.bass as bass
from concourse import mybir

F32 = mybir.dt.float32
ALU = mybir.AluOpType
ACT = mybir.ActivationFunctionType
AX = mybir.AxisListType.X

B, C, N = 512, 16, 64
S = 8
SH = S // 2
GROUPS = B // S
FR = S * C
D = 28
CO = N - D + 1
PH, XS = 3, 13
CM = PH * CO
TAPS = 15
HID = 100
PROF = 96
K2 = N // 2 + 1
KB = 17
NA = N + 3
NH = 34
WB = 11
CNT = 2 * N * N
THR = 1000.0 * float(np.finfo(np.float32).eps)
EPS = 1e-5
MIX_STEPS = 13
LINKS = 23
B_LINKS = 22

SIGNALS = {
    "raw_loaded": 256, "squares": 1, "sums": 1, "variance": 1, "deviation": 1, "stats": 1, "xn_ready": 1,
    "vector_link": LINKS, "xd_loaded": 128, "conv": 4, "conv_copied": 4, "conv_max": 1, "max_turned": 1,
    "max_diag": 1, "max_spread": 1, "conv_shifted": 1, "conv_exp": 1, "exp_sum": 1, "exp_sum_copied": 1,
    "where_h1": 1, "where_h1_copied": 1, "where_h2": 1, "where_h2_copied": 1, "where_z": 1, "where_zz": 1,
    "where_tanh": 1, "shift": 1, "profile_abs": 1, "norms": 1, "profiles_turned": 1,
    "turned_profiles_copied": 1, "rec_stored": 32, "cut_stored": 32, "cut_loaded": 64,
    "cut_norms_loaded": 128, "rec_loaded": 128, "rec_norms_loaded": 128, "wrx_normed": 1, "o1": 8,
    "o1_copied": 8, "digits": 8, "digits_copied_a": 4, "digits_copied_v": 4, "digits_normed": 1, "what_h1": 1,
    "what_h1_copied": 1, "what_h2": 1, "what_h2_copied": 1, "what_sum": 1, "what_z": 1, "what_z_copied": 1,
    "dec_h1": 1, "dec_h1_copied": 1, "dec_h2": 1, "dec_h2_copied": 1, "dec_out": 1, "dec_tanh": 1,
    "dec_sig": 1, "dec_stored": 16, "digit_loaded": 64, "aa": 4, "aa_copied": 4, "x1": 8, "x1_copied": 8,
}
HALF_SIGNALS = {
    "b_squares": 3, "b_sums": 3, "b_variance": 3, "b_deviation": 3, "b_stats": 3, "b_xn_ready": 3,
    "b_link": B_LINKS, "moments": 1, "dft": 5, "dft_copied": 5, "z_stored": 128, "v_loaded": 128,
    "mixed": 5, "mixed_copied": 5, "y_stored": 128, "y_loaded": 128, "corr": 1, "corr_copied": 1, "idft": 4,
    "x2_ready": 4, "xn2_stored": 32, "edge_cleared": 1, "v2_loaded": 128, "conv2": 6, "conv2_copied": 6,
    "y2_stored": 96, "y2_loaded": 32, "x3_ready": 1, "gate_prod": 2, "gate_sum": 4, "gated": 4, "added": 1,
    "turned": 4, "turned_copied": 4, "out_stored": 64,
}


def constants():
    k = {}
    p = np.arange(128)
    k["ident"] = np.eye(128)
    k["ones"] = np.ones((128, 128))
    k["halves"] = (p[:, None] // 64 == p[None, :] // 64) * 1.0
    n = np.arange(N)
    f = np.zeros((N, N))
    g = np.zeros((N, N))
    for kk in range(K2):
        f[:, kk] = np.cos(2 * np.pi * kk * n / N)
        g[kk, :] = (1 if kk in (0, N // 2) else 2) * np.cos(2 * np.pi * kk * n / N) / N
    for kk in range(1, N // 2):
        f[:, N // 2 + kk] = -np.sin(2 * np.pi * kk * n / N)
        g[N // 2 + kk, :] = -2 * np.sin(2 * np.pi * kk * n / N) / N
    k["dft"] = np.kron(np.eye(2), f)
    k["idft"] = np.kron(np.eye(2), g)
    k["iota"] = np.broadcast_to(np.arange(PROF) - 31.0, (128, PROF))
    i = np.concatenate([np.arange(D)[::-1], np.arange(D)[::-1], np.arange(N), np.arange(N)]) + 0.5
    k["place"] = np.broadcast_to(i, (128, 2 * D + 2 * N))
    ok = np.zeros((128, XS))
    for ph in range(PH):
        for x in range(XS):
            if PH * x + ph < CO:
                ok[ph * CO:(ph + 1) * CO, x] = 1
    k["ok"] = ok
    k["low"] = (1 - ok[:, XS - 1:]) * -1e30
    th = 2 * np.pi * n / N
    k["cos"] = np.broadcast_to(np.cos(th), (128, N))
    k["sin"] = np.broadcast_to(np.sin(th), (128, N))
    sel = np.zeros((2, 8, 2, SH, 8, 2, SH, 32))
    for a in range(8):
        for t in range(SH):
            for par in range(2):
                rows = 2 * np.arange(32) + par
                sel[0, a, 0, t, a, par, t] = 1
                sel[0, a, 1, t, a, par, t] = np.cos(th)[rows]
                sel[1, a, 0, t, a, par, t] = np.sin(th)[rows]
    k["sel"] = sel.reshape(128, 2048)
    sa = np.ones((4, 2, C, 2, 2, C))
    sa[:, 1, :, :, 0] = -1
    sb = np.ones((4, 2, C, 2, 2, C))
    sb[:, :, :, :, 0] = -1
    sb[:, 1, :, :, 1] = -1
    sb[:, 0, :, :, 0] = -1
    k["sign_a"], k["sign_b"] = sa.reshape(128, 64), sb.reshape(128, 64)
    k["zero"] = np.zeros((4, C * SH * NA))
    return {n_: np.ascontiguousarray(a, dtype=np.float32) for n_, a in k.items()}


def layouts(a):
    w = {}
    k = a["L0_conv_digit_mean"][::-1, ::-1]
    t = np.zeros((TAPS, 2, N, PH, CO), np.float32)
    for e in range(2 * TAPS):
        for ph in range(PH):
            if 0 <= e - ph < D:
                for y in range(CO):
                    t[e // 2, e % 2, y:y + D, ph, y] = k[:, e - ph]
    w["toep"] = t.reshape(TAPS, 128, CM).transpose(1, 0, 2)
    t = np.zeros((PH, CO, XS, 2 * HID), np.float32)
    w1 = a["L0_conv_where_w1"].reshape(CO, CO, 2 * HID)
    for ph in range(PH):
        for x in range(XS):
            if PH * x + ph < CO:
                t[ph, :, x] = w1[:, PH * x + ph]
    w["where_w1"] = t.reshape(CM, XS, 2 * HID)
    w["where_b1"] = a["L0_conv_where_b1"][None]
    w["where_w2"] = a["L0_conv_where_w2"].reshape(2, HID, 2 * HID)[:, :, :HID].transpose(1, 0, 2)
    w["where_b2"] = a["L0_conv_where_b2"][None, :HID]
    w["where_wloc"] = a["L0_conv_where_wloc"]
    w["where_bloc"] = np.broadcast_to(a["L0_conv_where_bloc"], (128, 2))
    t = np.zeros((4, 32, 7, 400), np.float32)
    t[:, 32 - D:] = a["L0_conv_what_w1"].reshape(D, D, 400)[::-1, ::-1].reshape(4, 7, D, 400).transpose(0, 2, 1, 3)
    w["what_w1"] = t.reshape(128, 7, 400)
    w["what_b1"] = a["L0_conv_what_b1"].reshape(4, HID).T
    w["what_w2"] = a["L0_conv_what_w2"].reshape(4, HID, 200).transpose(1, 0, 2)
    w["what_b2"] = a["L0_conv_what_b2"].reshape(2, HID).T
    w["what_wloc"] = a["L0_conv_what_wloc"].reshape(2, HID, 10).transpose(1, 0, 2)
    w["what_bloc"] = a["L0_conv_what_bloc"][:, None]
    w["dec_w1"] = a["L0_conv_dec_w1"]
    w["dec_b1"] = a["L0_conv_dec_b1"].reshape(2, HID).T
    w["dec_w2"] = a["L0_conv_dec_w2"].reshape(2, HID, 400).transpose(1, 0, 2)
    w["dec_b2"] = a["L0_conv_dec_b2"].reshape(4, HID).T
    t = np.zeros((HID + 1, 4, D * D), np.float32)
    t[:HID] = a["L0_conv_dec_w3"][:, ::-1].reshape(4, HID, D * D).transpose(1, 0, 2)
    t[HID, 3] = a["L0_conv_dec_b3"][::-1]
    w["dec_w3"] = t
    real, imag = a["L1_conv_w_real"], a["L1_conv_w_imag"]
    pl = np.zeros((3, 2, 4, 2, C, 2, 2, C), np.float32)
    for t_ in range(3):
        for b in range(3):
            wr, wi = real[:, :, 2 - t_, 2 - b], imag[:, :, 2 - t_, 2 - b]
            for w_ in range(2):
                for part in range(2):
                    pl[t_, 0, w_ + b, part, :, w_, part] = wr
                    pl[t_, 0, w_ + b, part, :, w_, 1 - part] = wi
                    pl[t_, 1, w_ + b, part, :, w_, part] = wi
                    pl[t_, 1, w_ + b, part, :, w_, 1 - part] = wr
    w["taps"] = pl.reshape(6, 128, 64).transpose(1, 0, 2)
    w["l1_bias"] = np.stack([np.stack([a["L1_conv_b_real"], a["L1_conv_b_imag"]])] * 2).reshape(1, 64)
    kw = a["L2_conv_K"].reshape(C, 3, 3, C)
    t = np.zeros((3, 8, C, 6, C), np.float32)
    for ky in range(3):
        for kx in range(3):
            for w_ in range(6):
                t[ky, w_ + kx, :, w_] = kw[:, ky, kx]
    w["l2_taps"] = t.reshape(3, 128, 96).transpose(1, 0, 2)
    return {n_: np.ascontiguousarray(v) for n_, v in w.items()}


PERSIST = ["toep", "where_w1", "where_b1", "where_w2", "where_b2", "where_wloc", "where_bloc", "what_w1", "what_b1",
           "what_w2", "what_b2", "what_wloc", "what_bloc", "dec_w1", "dec_b1", "dec_w2", "dec_b2", "dec_w3",
           "l1_bias", "l2_taps", "ident", "ones", "halves", "dft", "idft", "iota", "place", "ok", "low", "cos", "sin", "sel"]


def program(nc, x, out, src, groups=GROUPS):
    ctx = ExitStack()
    with ctx:
        def sb(name, *shape):
            return ctx.enter_context(nc.sbuf_tensor(name, [128, *shape], F32))

        def view(t, off, *dims):
            row = t.shape[1]
            return bass.AP(tensor=t[:, :].tensor, offset=off, ap=[[row, 128]] + [list(d) for d in dims])

        def rows(t, p0, p1, off, *dims):
            row = t.shape[1]
            return bass.AP(tensor=t[:, :].tensor, offset=p0 * row + off, ap=[[row, p1 - p0]] + [list(d) for d in dims])

        tab = {}
        for n in PERSIST:
            shape = src[n].shape
            tab[n] = sb("t_" + n, int(np.prod(shape[1:])))
        mix_w = sb("mix_w", N * 64)
        mix_e = sb("mix_e", 4 * 64)
        raw = sb("raw", 4096)
        x1 = sb("x1", 4096)
        digit = sb("digit", S * 128)
        cut = sb("cut", 8200)
        frm = sb("frm", 4096)
        fcb = sb("fcb", KB * SH * NH)
        small = sb("small", 1904)
        big = sb("big", 840)
        d2 = sb("d2", 32)
        work = sb("work", 5632)
        bsmall = sb("bsmall", 320)
        PS = ctx.enter_context(nc.psum_tensor("PS", [128, 8 * 512], F32))

        def bank(b, p0, p1, off, *dims):
            return bass.AP(tensor=PS[:, :].tensor, offset=p0 * 4096 + b * 512 + off, ap=[[4096, p1 - p0]] + [list(d) for d in dims])

        WY, WX, O1, DG, NY = 0, 1792, 3840, 5632, 6528
        AA, RBX, RBY, SG = 0, 2048, 4096, 6144
        WRY, WRX = 0, 2048
        PR, NX, TOT, RN, SS, TMP = 0, 384, 512, 696, 880, 1064
        ST, MS, RS, NM, TV = 1248, 1312, 1344, 1376, 1408
        PM, DGM, SR, MX, ZT, TT, ZI = 1440, 1568, 1696, 1824, 1826, 1828, 1832
        HW1, HW2, HS, ZW, D1 = 0, 512, 768, 784, 792
        H1, H2 = 0, 256
        XNB, ZZ, VV = 0, 2304, 0
        YK = 0
        SQ = 0
        V2, Y2O, PRODS, OUT = 0, 2816, 2048, 3584
        BST, BMS, BRS, BNM, BTV, ES = 0, 64, 96, 128, 160, 192

        zs = nc.dram_tensor("zs", (72, C, SH * NA), F32).ap()
        ys = nc.dram_tensor("ys", (2, 2 * KB, C, 2 * SH * NH), F32).ap()
        xs = nc.dram_tensor("xs", (68, C, SH * N), F32).ap()
        y2s = nc.dram_tensor("y2s", (66, C, SH * N), F32).ap()
        pt = nc.dram_tensor("pt", (2, PROF, FR), F32).ap()
        pd = nc.dram_tensor("pd", (2, FR, PROF), F32).ap()
        rnt = nc.dram_tensor("rnt", (2 * D, FR), F32).ap()
        rnd = nc.dram_tensor("rnd", (2, FR, N), F32).ap()
        ds = nc.dram_tensor("ds", (S, D, D), F32).ap()

        def passed(eng):
            eng.sem_inc(waits_passed, 1)

        on = {n: ctx.enter_context(nc.semaphore(n)) for n in [*SIGNALS, *HALF_SIGNALS]}
        per = {**SIGNALS, **HALF_SIGNALS}
        waits_passed = ctx.enter_context(nc.semaphore("waits_passed"))
        loaded = ctx.enter_context(nc.semaphore("tables_loaded"))
        zeroed = ctx.enter_context(nc.semaphore("scratch_zeroed"))
        cleared = ctx.enter_context(nc.semaphore("buffers_cleared"))
        mixing = ctx.enter_context(nc.semaphore("mix_tables_ready"))
        TABLES = 16 * (len(PERSIST) + 3)
        half = lambda i, off, *d: view(x1, 256 * i + off, *d)
        flat = lambda t, off, *d: bass.AP(tensor=t.tensor, offset=off, ap=[list(e) for e in d])
        block = ctx.enter_context(nc.Block())


        @block.sync
        def _(sp):
            for n in PERSIST:
                a = src[n]
                sp.dma_start(tab[n][0:a.shape[0], :], a if len(a.shape) == 2 else a.rearrange("a b c -> a (b c)")).then_inc(loaded, 16)
            sp.dma_start(view(cut, 0, (1, 384)), src["taps"].rearrange("a b c -> a (b c)")).then_inc(loaded, 16)
            sp.dma_start(view(cut, 384, (1, 64)), src["sign_a"]).then_inc(loaded, 16)
            sp.dma_start(view(cut, 448, (1, 64)), src["sign_b"]).then_inc(loaded, 16)
            z = src["zero"]
            for a, b in ((0, 1), (34, 38), (69, 72)):
                sp.dma_start(zs[a:b].rearrange("a b c -> a (b c)"), z[0:b - a, :]).then_inc(zeroed, 16)
            for a, b in ((0, 1), (65, 68)):
                sp.dma_start(xs[a:b].rearrange("a b c -> a (b c)"), z[0:b - a, 0:C * SH * N]).then_inc(zeroed, 16)
            sp.dma_start(y2s[63:64].rearrange("a b c -> a (b c)"), z[0:1, 0:C * SH * N]).then_inc(zeroed, 16)
            sp.wait_ge(zeroed, 16 * 6)
            sp.wait_ge(mixing, MIX_STEPS)

            def layer0_load(a, first):
                b0 = a * S if first else sp.snap(a * S)
                if not first:
                    sp.wait_ge(on["x1"], a * per["x1"])
                    passed(sp)
                for s in range(S):
                    for u in range(2):
                        d = x[bass.ds(b0 + s, 1), 8 * u:8 * u + 8].rearrange("s c n m -> n (s c) m")
                        sp.dma_start(rows(raw, 64 * u, 64 * u + 64, 512 * s, (64, 8), (1, 64)), d).then_inc(on["raw_loaded"], 16)

            def layer0_copies(a):
                sp.wait_ge(on["xn_ready"], a * per["xn_ready"] + 1)
                for h in range(2):
                    for q in range(4):
                        u = q // 2
                        sp.dma_start(rows(cut, 64 * h, 64 * h + 64, 1 - h + 2048 * q, (256, S), (1, 256)),
                                     rows(frm, 64 * u, 64 * u + 64, 256 * (q % 2), (512, S), (1, 256))).then_inc(on["xd_loaded"], 16)

            def layer0_profiles(a):
                sp.wait_ge(on["norms"], a * per["norms"] + 1)
                sp.dma_start(pd.rearrange("a f u -> f a u"), view(small, PR + 2 * PROF, (PROF, 2), (1, PROF))).then_inc(on["rec_stored"], 16)
                sp.dma_start(rnd.rearrange("a f u -> f a u"), view(small, RN + 2 * D, (N, 2), (1, N))).then_inc(on["rec_stored"], 16)
                sp.wait_ge(on["turned_profiles_copied"], a * per["turned_profiles_copied"] + 1)
                sp.dma_start(pt.rearrange("a u f -> u a f"), rows(big, 0, PROF, 0, (FR, 2), (1, FR))).then_inc(on["cut_stored"], 16)
                sp.dma_start(rnt, rows(big, 0, 2 * D, 2 * FR, (1, FR))).then_inc(on["cut_stored"], 16)
                sp.wait_ge(on["cut_stored"], a * per["cut_stored"] + per["cut_stored"])
                passed(sp)
                for u in range(2):
                    for ax, at, no in ((0, WY, D), (1, WX, 32)):
                        sp.dma_start(rows(cut, 64 * u, 64 * u + 64, at, (64, no), (1, 64)),
                                     flat(pt, (ax * PROF + 32 - no) * FR + 64 * u, (FR, 64), (FR, no), (1, 64))).then_inc(on["cut_loaded"], 16)
                for q in range(4):
                    sp.dma_start(rows(cut, 32 * q, 32 * q + 32, NY, (1, 7 * FR)), flat(rnt, 7 * FR * q, (0, 32), (1, 7 * FR))).then_inc(on["cut_norms_loaded"], 16)
                    sp.dma_start(rows(small, 32 * q + 32 - D, 32 * q + 32, NX, (1, FR)), rnt[D:2 * D, :]).then_inc(on["cut_norms_loaded"], 16)

            def layer0_rec(a):
                sp.wait_ge(on["rec_stored"], a * per["rec_stored"] + per["rec_stored"])
                passed(sp)
                sp.wait_ge(on["o1"], a * per["o1"] + per["o1"])
                passed(sp)
                for q in range(4):
                    for ax, at in ((0, WRY), (1, WRX)):
                        sp.dma_start(rows(frm, 32 * q, 32 * q + 32, at, (64, 32), (1, 64)),
                                     flat(pd, (ax * FR + 32 * q) * PROF, (1, 32), (PROF, 32), (1, 64))).then_inc(on["rec_loaded"], 16)

            def layer0_rec_norms(a):
                sp.wait_ge(on["what_h1"], a * per["what_h1"] + 1)
                passed(sp)
                for q in range(4):
                    for ax, at in ((0, RBY), (1, RBX)):
                        sp.dma_start(rows(cut, 32 * q, 32 * q + 32, at, (1, 2048)), flat(rnd, (ax * FR + 32 * q) * N, (0, 32), (1, 2048))).then_inc(on["rec_norms_loaded"], 16)

            def layer0_digit(a):
                sp.wait_ge(on["dec_sig"], a * per["dec_sig"] + 1)
                sp.dma_start(ds.rearrange("s a b -> s (a b)"), rows(cut, 0, S, SG, (1, D * D))).then_inc(on["dec_stored"], 16)
                sp.wait_ge(on["dec_stored"], a * per["dec_stored"] + 16)
                passed(sp)
                for q in range(4):
                    sp.dma_start(rows(digit, 32 * q + 32 - D, 32 * q + 32, 32 * q + 32 - D, (128, S), (1, D)), ds.rearrange("s a b -> a s b")).then_inc(on["digit_loaded"], 16)

            def half_windows(t):
                sp.wait_ge(on["dft_copied"], t * per["dft_copied"] + per["dft_copied"])
                for h in range(2):
                    for a, b, to in ((0, 32, 1), (32, 33, 33), (33, 49, 38), (49, 64, 54)):
                        dst = zs[to:to + b - a].rearrange("k (p h) n -> k h p n", h=2)[:, h]
                        sp.dma_start(dst, rows(work, 64 * h + a, 64 * h + b, ZZ, (SH * NA, 8), (1, SH * NA))).then_inc(on["z_stored"], 16)
                sp.wait_ge(on["z_stored"], t * per["z_stored"] + per["z_stored"])
                passed(sp)
                for w in range(4):
                    for part in range(2):
                        s0, p0 = 36 * part + w, 32 * w + 16 * part
                        sp.dma_start(rows(work, p0, p0 + 16, VV, (SH * NA, KB), (1, SH * NA)), zs[s0:s0 + 33:2].rearrange("b c n -> c b n")).then_inc(on["v_loaded"], 16)

            def half_mixed(t):
                sp.wait_ge(on["mixed_copied"], t * per["mixed_copied"] + per["mixed_copied"])
                for par in range(2):
                    for w in range(2):
                        for part in range(2):
                            p0 = 64 * par + 32 * w + 16 * part
                            dst = ys[part, w:w + 33:2, :, par * SH * NH:(par + 1) * SH * NH].rearrange("b c n -> c b n")
                            sp.dma_start(dst, rows(fcb, p0, p0 + 16, 0, (SH * NH, KB), (1, SH * NH))).then_inc(on["y_stored"], 16)
                sp.wait_ge(on["y_stored"], t * per["y_stored"] + per["y_stored"])
                passed(sp)
                for h in range(2):
                    for a, b, part, k in ((0, 32, 0, 0), (32, 33, 0, 32), (33, 49, 1, 1), (49, 64, 1, 17)):
                        d = ys[part, k:k + b - a].rearrange("k (p h) n -> k h p n", h=2)[:, h]
                        sp.dma_start(rows(work, 64 * h + a, 64 * h + b, YK, (2 * SH * NH, 8), (1, 2 * SH * NH)), d).then_inc(on["y_loaded"], 16)

            def half_columns(t):
                sp.wait_ge(on["b_xn_ready"], t * per["b_xn_ready"] + 2)
                for h in range(2):
                    dst = xs[1:65].rearrange("k (p h) n -> k h p n", h=2)[:, h]
                    sp.dma_start(dst, rows(work, 64 * h, 64 * h + 64, XNB, (SH * N, 8), (1, SH * N))).then_inc(on["xn2_stored"], 16)
                sp.wait_ge(on["xn2_stored"], t * per["xn2_stored"] + per["xn2_stored"])
                passed(sp)
                for w in range(8):
                    sp.dma_start(rows(work, 16 * w, 16 * w + 16, V2, (SH * N, WB), (1, SH * N)), xs[w:w + 61:6].rearrange("b c n -> c b n")).then_inc(on["v2_loaded"], 16)

            def half_back(t):
                sp.wait_ge(on["conv2_copied"], t * per["conv2_copied"] + per["conv2_copied"])
                passed(sp)
                sp.wait_ge(on["edge_cleared"], t * per["edge_cleared"] + 1)
                for w in range(6):
                    nb = WB if w < 3 else WB - 1
                    dst = y2s[w:w + 6 * (nb - 1) + 1:6].rearrange("b c n -> c b n")
                    sp.dma_start(dst, rows(work, 16 * w, 16 * w + 16, Y2O, (SH * N, nb), (1, SH * N))).then_inc(on["y2_stored"], 16)
                sp.wait_ge(on["y2_stored"], t * per["y2_stored"] + per["y2_stored"])
                passed(sp)
                for h in range(2):
                    d = y2s[0:64].rearrange("k (p h) n -> k h p n", h=2)[:, h]
                    sp.dma_start(rows(work, 64 * h, 64 * h + 64, 0, (SH * N, 8), (1, SH * N)), d).then_inc(on["y2_loaded"], 16)

            def half_out(t):
                b0 = sp.snap(t * SH) if not isinstance(t, int) else t * SH
                sp.wait_ge(on["turned_copied"], t * per["turned_copied"] + per["turned_copied"])
                passed(sp)
                for s4 in range(SH):
                    dst = out[bass.ds(b0 + s4, 1)].rearrange("s (p h) (n e) m -> (s n) (p h) (e m)", h=2, e=2)
                    sp.dma_start(dst, rows(work, 32 * s4, 32 * s4 + 32, OUT, (128, 16), (1, 128))).then_inc(on["out_stored"], 16)

            def turn(g, a):
                for i in range(2):
                    t = g * 2 + i if isinstance(g, int) else sp.snap(g * 2 + i)
                    if a is not None and i == 0:
                        layer0_load(a, False)
                    half_windows(t)
                    if a is not None and i == 0:
                        layer0_copies(a)
                    if a is not None and i == 1:
                        layer0_rec(a)
                    half_mixed(t)
                    if a is not None and i == 1:
                        layer0_rec_norms(a)
                    half_columns(t)
                    if a is not None and i == 1:
                        layer0_digit(a)
                    half_back(t)
                    if a is not None and i == 0:
                        layer0_profiles(a)
                    half_out(t)

            layer0_load(0, True)
            layer0_copies(0)
            layer0_profiles(0)
            layer0_rec(0)
            layer0_rec_norms(0)
            layer0_digit(0)
            if groups > 1:
                with sp.Fori(0, groups - 1) as g:
                    turn(g, sp.snap(g + 1))
            turn(groups - 1, None)
            sp.wait_ge(on["out_stored"], 16 + 2 * groups * per["out_stored"])

        @block.gpsimd
        def _(pool):
            nc.gpsimd.memset(digit[:, :], 0.0).then_inc(cleared, 1)
            nc.gpsimd.memset(d2[:, :], 1.0).then_inc(cleared, 1)
            nc.gpsimd.memset(view(small, NX, (1, FR)), 0.0).then_inc(cleared, 1)
            nc.gpsimd.memset(view(cut, 8192, (1, 8)), 0.0).then_inc(cleared, 1)
            nc.gpsimd.sem_inc(on["out_stored"], 16)
            with pool.Fori(0, groups) as a:
                pool.wait_ge(on["rec_norms_loaded"], a * per["rec_norms_loaded"] + per["rec_norms_loaded"])
                pool.wait_ge(on["rec_loaded"], a * per["rec_loaded"] + per["rec_loaded"])
                w = view(frm, WRX, (1, 2048))
                nc.gpsimd.tensor_tensor(w, w, view(cut, RBX, (1, 2048)), ALU.mult).then_inc(on["wrx_normed"], 1)

        @block.scalar
        def _(act):
            def copy(o, i):
                return nc.scalar.activation(o, i, ACT.Copy)

            act.wait_ge(loaded, TABLES)
            act.wait_ge(cleared, 4)

            def layer0_squares(a):
                act.wait_ge(on["raw_loaded"], a * per["raw_loaded"] + per["raw_loaded"])
                nc.scalar.activation(frm[:, :], raw[:, :], ACT.Square).then_inc(on["squares"], 1)
                act.wait_ge(on["variance"], a * per["variance"] + 1)
                v = view(small, RS, (1, 32))
                nc.scalar.activation(v, v, ACT.Sqrt).then_inc(on["deviation"], 1)

            def layer0_conv(a, j):
                act.wait_ge(on["conv"], a * per["conv"] + j + 1)
                copy(rows(fcb, 0, CM, 32 * j, (1, 32), (FR, XS)), bank(j, 0, CM, 0, (XS, 32), (1, XS))).then_inc(on["conv_copied"], 1)

            def layer0_where(a):
                act.wait_ge(on["conv_shifted"], a * per["conv_shifted"] + 1)
                fc = rows(fcb, 0, CM, 0, (1, XS * FR))
                nc.scalar.activation(fc, fc, ACT.Exp).then_inc(on["conv_exp"], 1)
                act.wait_ge(on["where_h1"], a * per["where_h1"] + 1)
                nc.scalar.activation(rows(big, 0, HID, H1, (1, 256)), bank(2, 0, HID, 0, (1, 256)), ACT.Relu).then_inc(on["where_h1_copied"], 1)
                act.wait_ge(on["where_h2"], a * per["where_h2"] + 1)
                nc.scalar.activation(rows(big, 0, HID, H2, (1, FR)), bank(0, 0, HID, 0, (1, FR)), ACT.Relu).then_inc(on["where_h2_copied"], 1)
                act.wait_ge(on["where_zz"], a * per["where_zz"] + 1)
                nc.scalar.activation(view(small, ZT, (1, 2)), view(small, ZI, (1, 2)), ACT.Tanh).then_inc(on["where_tanh"], 1)
                act.wait_ge(on["shift"], a * per["shift"] + 1)
                for j in range(4):
                    t = view(small, TT + 1 - j % 2, (1, 1))
                    ins = nc.scalar.activation(view(small, PR + PROF * j, (1, PROF)), tab["iota"][:, :], ACT.Abs, bias=t, scale=1.0 if j < 2 else -1.0)
                ins.then_inc(on["profile_abs"], 1)

            def layer0_profiles(a):
                act.wait_ge(on["profiles_turned"], a * per["profiles_turned"] + 1)
                copy(rows(big, 0, PROF, 0, (1, 2 * FR)), bank(2, 0, PROF, 0, (1, 2 * FR)))
                copy(rows(big, 0, 2 * D, 2 * FR, (1, FR)), bank(2, 0, 2 * D, 2 * FR, (1, FR))).then_inc(on["turned_profiles_copied"], 1)

            def layer0_cut(a):
                for k in range(8):
                    act.wait_ge(on["o1"], a * per["o1"] + k + 1)
                    u = k // 4
                    copy(rows(cut, 64 * u, 64 * u + 64, O1 + 448 * (k % 4), (1, 448)), bank(k % 4, 64 * u, 64 * u + 64, 0, (1, 448))).then_inc(on["o1_copied"], 1)

            def layer0_digits(a):
                for k in range(0, 8, 2):
                    act.wait_ge(on["digits"], a * per["digits"] + k + 1)
                    for q in range(4):
                        ins = copy(rows(cut, 32 * q, 32 * q + 32, DG + 16 * (k // 2), (1, 16), (FR, 7)), bank(k % 4, 0, 32, 7 * q, (28, 16), (1, 7)))
                    ins.then_inc(on["digits_copied_a"], 1)

            def layer0_what(a):
                act.wait_ge(on["what_h1"], a * per["what_h1"] + 1)
                for k in range(4):
                    ins = nc.scalar.activation(rows(big, 0, HID, HW1 + FR * k, (1, FR)), bank(0, 0, HID, FR * k, (1, FR)), ACT.Relu,
                                               bias=rows(tab["what_b1"], 0, HID, k, (1, 1)))
                ins.then_inc(on["what_h1_copied"], 1)
                act.wait_ge(on["what_h2"], a * per["what_h2"] + 1)
                for k in range(2):
                    ins = nc.scalar.activation(rows(big, 0, HID, HW2 + FR * k, (1, FR)), bank(1, 0, HID, FR * k, (1, FR)), ACT.Relu,
                                               bias=rows(tab["what_b2"], 0, HID, k, (1, 1)))
                ins.then_inc(on["what_h2_copied"], 1)

            def layer0_dec(a):
                act.wait_ge(on["what_z"], a * per["what_z"] + 1)
                nc.scalar.activation(rows(big, 0, 10, ZW, (1, S)), bank(2, 0, 10, 0, (1, S)), ACT.Identity,
                                     bias=rows(tab["what_bloc"], 0, 10, 0, (1, 1))).then_inc(on["what_z_copied"], 1)
                act.wait_ge(on["dec_h1"], a * per["dec_h1"] + 1)
                for k in range(2):
                    ins = nc.scalar.activation(rows(big, 0, HID, D1 + S * k, (1, S)), bank(3, 0, HID, S * k, (1, S)), ACT.Relu,
                                               bias=rows(tab["dec_b1"], 0, HID, k, (1, 1)))
                ins.then_inc(on["dec_h1_copied"], 1)
                act.wait_ge(on["dec_h2"], a * per["dec_h2"] + 1)
                for k in range(4):
                    ins = nc.scalar.activation(rows(d2, 0, HID, S * k, (1, S)), bank(0, 0, HID, S * k, (1, S)), ACT.Relu,
                                               bias=rows(tab["dec_b2"], 0, HID, k, (1, 1)))
                ins.then_inc(on["dec_h2_copied"], 1)
                act.wait_ge(on["dec_out"], a * per["dec_out"] + 1)
                nc.scalar.activation(rows(cut, 0, S, SG, (392, 2), (1, 392)), bank(1, 0, S, 0, (512, 2), (1, 392)), ACT.Tanh, scale=0.5).then_inc(on["dec_tanh"], 1)

            def layer0_x1(a):
                for k in range(8):
                    act.wait_ge(on["x1"], a * per["x1"] + k + 1)
                    q, hs = k % 4, k // 4
                    copy(view(x1, 1024 * q + 256 * hs, (512, 2), (1, 256)), bank(q, 0, 128, 0, (256, 2), (1, 256))).then_inc(on["x1_copied"], 1)

            def half_squares(t, i, k):
                sq = view(work, SQ, (256, 8), (1, 256))
                nc.scalar.activation(sq, half(i, 0, (512, 8), (1, 256)), ACT.Square).then_inc(on["b_squares"], 1)
                act.wait_ge(on["b_variance"], t * per["b_variance"] + k)
                v = view(bsmall, BRS, (1, 32))
                nc.scalar.activation(v, v, ACT.Sqrt).then_inc(on["b_deviation"], 1)

            def half_norm1(g, t, i):
                act.wait_ge(on["x1_copied"], g * per["x1_copied"] + per["x1_copied"])
                half_squares(t, i, 1)

            def half_freq(t):
                for k in range(5):
                    act.wait_ge(on["dft"], t * per["dft"] + k + 1)
                    w = min(7, 32 - 7 * k) * NA
                    copy(view(work, ZZ + 7 * NA * k, (1, w)), bank(4 + k % 4, 0, 128, 0, (1, w))).then_inc(on["dft_copied"], 1)

            def half_mix(t):
                for k in range(5):
                    act.wait_ge(on["mixed"], t * per["mixed"] + k + 1)
                    m = min(7, NH - 7 * k)
                    copy(view(fcb, 7 * k, (NH, KB * SH), (1, m)), bank(4 + k % 4, 0, 128, 0, (1, KB * SH), (KB * SH, m))).then_inc(on["mixed_copied"], 1)

            def half_inverse(t, i):
                act.wait_ge(on["corr"], t * per["corr"] + 1)
                copy(view(bsmall, ES, (1, 128)), bank(4, 0, 128, 0, (1, 128))).then_inc(on["corr_copied"], 1)
                act.wait_ge(on["x2_ready"], t * per["x2_ready"] + per["x2_ready"])
                half_squares(t, i, 2)

            def half_conv2(t, i):
                for k in range(6):
                    act.wait_ge(on["conv2"], t * per["conv2"] + k + 1)
                    m = SH * min(2, WB - 2 * k)
                    copy(rows(work, 0, 96, Y2O + 512 * k, (N, m), (1, N - 1)), bank(4 + k % 4, 0, 96, 0, (N, m), (1, N - 1))).then_inc(on["conv2_copied"], 1)
                act.wait_ge(on["x3_ready"], t * per["x3_ready"] + 1)
                half_squares(t, i, 3)

            def half_out(t):
                for k in range(4):
                    act.wait_ge(on["turned"], t * per["turned"] + k + 1)
                    copy(view(work, OUT + 512 * k, (128, 4), (64, 2), (1, 64)), bank(4 + k, 0, 128, 0, (64, 4), (256, 2), (1, 64))).then_inc(on["turned_copied"], 1)

            def turn(g, a):
                for i in range(2):
                    t = g * 2 + i if isinstance(g, int) else act.snap(g * 2 + i)
                    half_norm1(g, t, i)
                    half_freq(t)
                    if a is not None and i == 0:
                        layer0_squares(a)
                    if a is not None and i == 1:
                        layer0_cut(a)
                    half_mix(t)
                    if a is not None and i == 0:
                        act.wait_ge(on["y_stored"], t * per["y_stored"] + per["y_stored"])
                        for j in range(4):
                            layer0_conv(a, j)
                    if a is not None and i == 1:
                        layer0_digits(a)
                        layer0_what(a)
                    half_inverse(t, i)
                    if a is not None and i == 0:
                        layer0_where(a)
                    if a is not None and i == 1:
                        layer0_dec(a)
                    half_conv2(t, i)
                    if a is not None and i == 0:
                        layer0_profiles(a)
                    half_out(t)
                if a is not None:
                    layer0_x1(a)

            layer0_squares(0)
            for j in range(4):
                layer0_conv(0, j)
            layer0_where(0)
            layer0_profiles(0)
            layer0_cut(0)
            layer0_digits(0)
            layer0_what(0)
            layer0_dec(0)
            layer0_x1(0)
            if groups > 1:
                with act.Fori(0, groups - 1) as g:
                    turn(g, act.snap(g + 1))
            turn(groups - 1, None)

        @block.vector
        def _(dve):
            dve.wait_ge(loaded, TABLES)
            setup = [0]

            def step(ins):
                setup[0] += 1
                ins.then_inc(mixing, 1)
                dve.wait_ge(mixing, setup[0])

            P = lambda j: view(cut, 64 * j, (1, 64))
            sa, sb_ = view(cut, 384, (1, 64)), view(cut, 448, (1, 64))
            tmp = [view(cut, 512 + 64 * j, (1, 64)) for j in range(3)]
            step(nc.vector.tensor_tensor(tmp[0], P(2), sa, ALU.mult))
            step(nc.vector.tensor_tensor(tmp[1], P(0), P(4), ALU.add))
            step(nc.vector.tensor_tensor(tmp[1], tmp[1], sa, ALU.mult))
            step(nc.vector.tensor_tensor(tmp[2], P(1), P(5), ALU.subtract))
            step(nc.vector.tensor_tensor(tmp[2], tmp[2], sb_, ALU.mult))
            mw = view(mix_w, 0, (64, N), (1, 64))
            t1 = view(frm, 0, (64, N), (1, 64))
            ang = lambda n: view(tab[n], 0, (1, N), (0, 64))
            over = lambda j: view(cut, 512 + 64 * j, (0, N), (1, 64))
            step(nc.vector.tensor_tensor(mw, ang("cos"), over(1), ALU.mult))
            step(nc.vector.tensor_tensor(mw, mw, over(0), ALU.add))
            step(nc.vector.tensor_tensor(t1, ang("sin"), over(2), ALU.mult))
            step(nc.vector.tensor_tensor(mw, mw, t1, ALU.add))
            for j, (p, s_, c_) in enumerate(((0, sa, -1), (1, sb_, -1), (4, sa, -1), (5, sb_, 1))):
                step(nc.vector.scalar_tensor_tensor(view(mix_e, 64 * j, (1, 64)), P(p), c_ / N, s_, ALU.mult, ALU.mult))
            assert setup[0] == MIX_STEPS

            links = {}

            def link(ins, a):
                links["a"] = links.get("a", 0) % LINKS + 1
                ins.then_inc(on["vector_link"], 1)
                dve.wait_ge(on["vector_link"], a * per["vector_link"] + links["a"])

            def blink(ins, t):
                links["b"] = links.get("b", 0) % B_LINKS + 1
                ins.then_inc(on["b_link"], 1)
                dve.wait_ge(on["b_link"], t * per["b_link"] + links["b"])

            def layer0_norm(a):
                pairs = 32
                source, dst = view(raw, 0, (128, pairs), (1, 128)), view(frm, 0, (128, pairs), (1, 128))
                dve.wait_ge(on["raw_loaded"], a * per["raw_loaded"] + per["raw_loaded"])
                nc.vector.tensor_reduce(view(small, ST, (1, pairs)), source, AX, ALU.add)
                dve.wait_ge(on["squares"], a * per["squares"] + 1)
                nc.vector.tensor_reduce(view(small, ST + pairs, (1, pairs)), dst, AX, ALU.add).then_inc(on["sums"], 1)
                dve.wait_ge(on["stats"], a * per["stats"] + 1)
                v = lambda o: view(small, o, (1, pairs))
                link(nc.vector.tensor_scalar(v(MS), bank(3, 0, 128, 0, (1, pairs)), 1.0 / CNT, None, ALU.mult), a)
                link(nc.vector.tensor_tensor(v(TV), v(MS), v(MS), ALU.mult), a)
                link(nc.vector.scalar_tensor_tensor(v(RS), bank(3, 0, 128, pairs, (1, pairs)), 1.0 / CNT, v(TV), ALU.mult, ALU.subtract), a)
                nc.vector.tensor_scalar(v(RS), v(RS), EPS, None, ALU.add).then_inc(on["variance"], 1)
                dve.wait_ge(on["deviation"], a * per["deviation"] + 1)
                link(nc.vector.reciprocal(v(RS), v(RS)), a)
                link(nc.vector.scalar_tensor_tensor(v(NM), v(MS), -1.0, v(RS), ALU.mult, ALU.mult), a)
                wide = lambda o: view(small, o, (1, pairs), (0, 128))
                link(nc.vector.tensor_tensor(dst, source, wide(RS), ALU.mult), a)
                nc.vector.tensor_tensor(dst, dst, wide(NM), ALU.add).then_inc(on["xn_ready"], 1)

            def layer0_max(a):
                dve.wait_ge(on["conv_copied"], a * per["conv_copied"] + per["conv_copied"])
                last = rows(fcb, 0, CM, FR * (XS - 1), (1, FR))
                link(nc.vector.tensor_scalar(last, last, rows(tab["ok"], 0, CM, XS - 1, (1, 1)), rows(tab["low"], 0, CM, 0, (1, 1)), ALU.mult, ALU.add), a)
                nc.vector.tensor_reduce(rows(small, 0, CM, PM, (1, FR)), rows(fcb, 0, CM, 0, (1, FR), (FR, XS)), AX, ALU.max).then_inc(on["conv_max"], 1)
                dve.wait_ge(on["max_turned"], a * per["max_turned"] + 1)
                link(nc.vector.tensor_reduce(view(small, MX, (1, 1)), bank(0, 0, 128, 0, (1, CM)), AX, ALU.max), a)
                nc.vector.tensor_scalar(view(small, DGM, (1, 128)), tab["ident"][:, :], view(small, MX, (1, 1)), None, ALU.mult).then_inc(on["max_diag"], 1)
                dve.wait_ge(on["max_spread"], a * per["max_spread"] + 1)
                fc = rows(fcb, 0, CM, 0, (FR, XS), (1, FR))
                nc.vector.tensor_tensor(fc, fc, bank(1, 0, CM, 0, (0, XS), (1, FR)), ALU.subtract).then_inc(on["conv_shifted"], 1)

            def layer0_where(a):
                dve.wait_ge(on["exp_sum"], a * per["exp_sum"] + 1)
                nc.vector.tensor_copy(rows(small, 0, 1, SR, (1, FR)), bank(0, 0, 1, 0, (1, FR))).then_inc(on["exp_sum_copied"], 1)
                dve.wait_ge(on["where_z"], a * per["where_z"] + 1)
                link(nc.vector.reciprocal(view(small, MX, (1, 1)), bank(1, 0, 128, 2, (1, 1))), a)
                nc.vector.scalar_tensor_tensor(view(small, ZI, (1, 2)), bank(1, 0, 128, 0, (1, 2)), view(small, MX, (1, 1)),
                                               tab["where_bloc"][:, :], ALU.mult, ALU.add).then_inc(on["where_zz"], 1)
                dve.wait_ge(on["where_tanh"], a * per["where_tanh"] + 1)
                nc.vector.tensor_scalar(view(small, TT, (1, 2)), view(small, ZT, (1, 2)), 1.0, (N - D) / 2, ALU.add, ALU.mult).then_inc(on["shift"], 1)

            def layer0_profiles(a):
                dve.wait_ge(on["profile_abs"], a * per["profile_abs"] + 1)
                pr = view(small, PR, (1, 384))
                t_b, t_a, t_c = (view(fcb, 384 * j, (1, 384)) for j in range(3))
                nc.vector.tensor_scalar(t_b, pr, 2.0, 0.0, ALU.subtract, ALU.min)
                link(nc.vector.tensor_scalar(t_a, pr, 1.0, 0.0, ALU.subtract, ALU.min), a)
                link(nc.vector.tensor_tensor(t_c, t_b, t_b, ALU.mult), a)
                link(nc.vector.scalar_tensor_tensor(t_b, t_b, 1.0, t_c, ALU.add, ALU.mult), a)
                link(nc.vector.tensor_tensor(t_c, t_a, t_a, ALU.mult), a)
                link(nc.vector.tensor_scalar(t_a, t_a, 2.0, 1.0, ALU.mult, ALU.add), a)
                link(nc.vector.tensor_tensor(t_a, t_a, t_c, ALU.mult), a)
                link(nc.vector.scalar_tensor_tensor(pr, t_b, -0.5, t_a, ALU.mult, ALU.add), a)
                for ax in range(2):
                    nc.vector.tensor_reduce(view(small, TOT + D * ax, (1, D)), view(small, PR + PROF * ax + 4, (1, D), (1, N)), AX, ALU.add)
                    nc.vector.tensor_reduce(view(small, TOT + 2 * D + N * ax, (1, N)), view(small, PR + PROF * (2 + ax) + 4, (1, N), (1, D)), AX, ALU.add)
                    t_ = view(small, TT + 1 - ax, (1, 1))
                    nc.vector.tensor_scalar(view(small, SS + D * ax, (1, D)), view(tab["place"], D * ax, (1, D)), t_, 0.5, ALU.subtract, ALU.subtract)
                    o = 2 * D + N * ax
                    ins = nc.vector.tensor_scalar(view(small, SS + o, (1, N)), view(tab["place"], o, (1, N)), t_, 0.5, ALU.subtract, ALU.subtract)
                link(ins, a)
                v = lambda o: view(small, o, (1, 2 * D + 2 * N))
                link(nc.vector.tensor_scalar(v(TMP), v(TOT), THR, None, ALU.is_gt), a)
                link(nc.vector.scalar_tensor_tensor(v(TMP), v(SS), -0.5, v(TMP), ALU.is_ge, ALU.mult), a)
                for o, m, hi in ((0, 2 * D, N - 0.5), (2 * D, 2 * N, D - 0.5)):
                    q_ = view(small, TMP + o, (1, m))
                    ins = nc.vector.scalar_tensor_tensor(q_, view(small, SS + o, (1, m)), hi, q_, ALU.is_le, ALU.mult)
                link(ins, a)
                link(nc.vector.tensor_scalar(v(TOT), v(TOT), THR, None, ALU.max), a)
                link(nc.vector.reciprocal(v(TOT), v(TOT)), a)
                nc.vector.tensor_tensor(v(RN), v(TOT), v(TMP), ALU.mult).then_inc(on["norms"], 1)

            def layer0_digits(a):
                for k in range(1, 8, 2):
                    dve.wait_ge(on["digits"], a * per["digits"] + k + 1)
                    for q in range(4):
                        ins = nc.vector.tensor_copy(rows(cut, 32 * q, 32 * q + 32, DG + 64 + 16 * (k // 2), (1, 16), (FR, 7)),
                                                    bank(k % 4, 0, 32, 7 * q, (28, 16), (1, 7)))
                    ins.then_inc(on["digits_copied_v"], 1)
                dve.wait_ge(on["digits_copied_v"], a * per["digits_copied_v"] + per["digits_copied_v"])
                dve.wait_ge(on["digits_copied_a"], a * per["digits_copied_a"] + per["digits_copied_a"])
                dve.wait_ge(on["cut_norms_loaded"], a * per["cut_norms_loaded"] + per["cut_norms_loaded"])
                dg = view(cut, DG, (FR, 7), (1, FR))
                link(nc.vector.tensor_tensor(dg, dg, view(cut, NY, (FR, 7), (1, FR)), ALU.mult), a)
                nc.vector.tensor_tensor(dg, dg, view(small, NX, (0, 7), (1, FR)), ALU.mult).then_inc(on["digits_normed"], 1)

            def layer0_what(a):
                dve.wait_ge(on["what_h2_copied"], a * per["what_h2_copied"] + 1)
                for k in range(2):
                    ins = nc.vector.tensor_reduce(rows(big, 0, HID, HS + S * k, (1, S)), rows(big, 0, HID, HW2 + FR * k, (4, S), (32, 4), (1, 4)), mybir.AxisListType.XY, ALU.add)
                ins.then_inc(on["what_sum"], 1)

            def layer0_dec(a):
                dve.wait_ge(on["dec_tanh"], a * per["dec_tanh"] + 1)
                sg = rows(cut, 0, S, SG, (1, D * D))
                nc.vector.tensor_scalar(sg, sg, 0.5, 0.5, ALU.mult, ALU.add).then_inc(on["dec_sig"], 1)

            def layer0_aa(a):
                dve.wait_ge(on["rec_norms_loaded"], a * per["rec_norms_loaded"] + per["rec_norms_loaded"])
                for k in range(4):
                    dve.wait_ge(on["aa"], a * per["aa"] + k + 1)
                    nc.vector.tensor_tensor(view(cut, AA + 512 * k, (1, 512)), bank(k, 0, 128, 0, (1, 512)), view(cut, RBY + 512 * k, (1, 512)), ALU.mult).then_inc(on["aa_copied"], 1)

            def normalise(t, i, k, row):
                source = half(i, 0, (512, 8), (64, SH), (1, 64))
                dst = view(work, XNB, (SH * row, 8), (row, SH), (1, 64))
                pairs = 8 * SH
                nc.vector.tensor_reduce(view(bsmall, BST, (SH, 8), (1, SH)), source, AX, ALU.add)
                dve.wait_ge(on["b_squares"], t * per["b_squares"] + k)
                nc.vector.tensor_reduce(view(bsmall, BST + pairs, (1, pairs)), view(work, SQ, (64, pairs), (1, 64)), AX, ALU.add).then_inc(on["b_sums"], 1)
                dve.wait_ge(on["b_stats"], t * per["b_stats"] + k)
                v = lambda o: view(bsmall, o, (1, pairs))
                blink(nc.vector.tensor_scalar(v(BMS), bank(7, 0, 128, 0, (1, pairs)), 1.0 / CNT, None, ALU.mult), t)
                blink(nc.vector.tensor_tensor(v(BTV), v(BMS), v(BMS), ALU.mult), t)
                blink(nc.vector.scalar_tensor_tensor(v(BRS), bank(7, 0, 128, pairs, (1, pairs)), 1.0 / CNT, v(BTV), ALU.mult, ALU.subtract), t)
                nc.vector.tensor_scalar(v(BRS), v(BRS), EPS, None, ALU.add).then_inc(on["b_variance"], 1)
                dve.wait_ge(on["b_deviation"], t * per["b_deviation"] + k)
                blink(nc.vector.reciprocal(v(BRS), v(BRS)), t)
                blink(nc.vector.scalar_tensor_tensor(v(BNM), v(BMS), -1.0, v(BRS), ALU.mult, ALU.mult), t)
                wide = lambda o: view(bsmall, o, (SH, 8), (1, SH), (0, 64))
                blink(nc.vector.tensor_tensor(dst, source, wide(BRS), ALU.mult), t)
                nc.vector.tensor_tensor(dst, dst, wide(BNM), ALU.add).then_inc(on["b_xn_ready"], 1)

            def half_norm1(g, t, i):
                dve.wait_ge(on["x1_copied"], g * per["x1_copied"] + per["x1_copied"])
                normalise(t, i, 1, NA)
                dve.wait_ge(on["b_xn_ready"], t * per["b_xn_ready"] + 1)
                xn = view(work, XNB, (NA, 32), (1, 64))
                dve.wait_ge(on["out_stored"], t * per["out_stored"] + 16)
                for j, n in enumerate(("cos", "sin")):
                    p = view(work, ZZ, (64, 32), (1, 64))
                    blink(nc.vector.tensor_tensor(p, xn, view(tab[n], 0, (0, 32), (1, 64)), ALU.mult), t)
                    ins = nc.vector.tensor_reduce(view(work, XNB + N + 1 + j, (NA, 32)), p, AX, ALU.add)
                    if j == 0:
                        blink(ins, t)
                nc.vector.tensor_reduce(view(work, XNB + N, (NA, 32)), xn, AX, ALU.add).then_inc(on["moments"], 1)

            def half_inverse(t, i):
                for k in range(4):
                    dve.wait_ge(on["idft"], t * per["idft"] + k + 1)
                    for j in range(2):
                        o = half(i, 512 * (2 * k + j), (1, 2), (64, SH), (2, 32))
                        ins = nc.vector.tensor_tensor(o, o, bank(4 + k, 0, 128, 256 * j, (128, 2), (32, SH), (1, 32)), ALU.add)
                    ins.then_inc(on["x2_ready"], 1)
                dve.wait_ge(on["x2_ready"], t * per["x2_ready"] + per["x2_ready"])
                normalise(t, i, 2, N)
                dve.wait_ge(on["v2_loaded"], t * per["v2_loaded"] + per["v2_loaded"])
                nc.vector.memset(rows(work, 0, 96, Y2O + N - 1, (N, WB * SH)), 0.0).then_inc(on["edge_cleared"], 1)

            def half_layer3(t, i):
                dve.wait_ge(on["y2_loaded"], t * per["y2_loaded"] + per["y2_loaded"])
                xh = half(i, 0, (512, 8), (1, 256))
                nc.vector.tensor_tensor(xh, xh, view(work, 0, (256, 8), (1, 256)), ALU.add).then_inc(on["x3_ready"], 1)
                dve.wait_ge(on["x3_ready"], t * per["x3_ready"] + 1)
                normalise(t, i, 3, N)
                dve.wait_ge(on["b_xn_ready"], t * per["b_xn_ready"] + 3)
                blink(nc.vector.tensor_reduce(view(bsmall, BST, (1, 32)), view(work, 0, (64, 32), (1, 64)), AX, ALU.add), t)
                for j in range(2):
                    nc.vector.tensor_tensor(view(work, PRODS + 1024 * j, (64, 16), (1, 64)), view(work, 1024 * j, (64, 16), (1, 64)),
                                            view(bsmall, BST + 16 * (1 - j), (1, 16), (0, 64)), ALU.mult).then_inc(on["gate_prod"], 1)
                for k in range(4):
                    dve.wait_ge(on["gate_sum"], t * per["gate_sum"] + k + 1)
                    o = view(work, 512 * k, (1, 512))
                    nc.vector.scalar_tensor_tensor(o, bank(4 + k, 0, 128, 0, (1, 512)), 0.0, o, ALU.is_gt, ALU.mult).then_inc(on["gated"], 1)
                dve.wait_ge(on["gated"], t * per["gated"] + per["gated"])
                nc.vector.tensor_tensor(xh, xh, view(work, 0, (256, 8), (1, 256)), ALU.add).then_inc(on["added"], 1)

            def turn(g, a):
                for i in range(2):
                    t = g * 2 + i if isinstance(g, int) else dve.snap(g * 2 + i)
                    half_norm1(g, t, i)
                    if a is not None and i == 0:
                        layer0_norm(a)
                    if a is not None and i == 1:
                        layer0_digits(a)
                        layer0_what(a)
                    half_inverse(t, i)
                    if a is not None and i == 0:
                        layer0_max(a)
                        layer0_where(a)
                        layer0_profiles(a)
                    if a is not None and i == 1:
                        layer0_dec(a)
                    half_layer3(t, i)
                    if a is not None and i == 1:
                        layer0_aa(a)

            layer0_norm(0)
            layer0_max(0)
            layer0_where(0)
            layer0_profiles(0)
            layer0_digits(0)
            layer0_what(0)
            layer0_dec(0)
            layer0_aa(0)
            assert links["a"] == LINKS, links
            if groups > 1:
                with dve.Fori(0, groups - 1) as g:
                    turn(g, dve.snap(g + 1))
            turn(groups - 1, None)
            assert links == {"a": LINKS, "b": B_LINKS}, links

        @block.tensor
        def _(pe):
            mm = nc.tensor.matmul
            pe.wait_ge(loaded, TABLES)
            pe.wait_ge(mixing, MIX_STEPS)
            pe.wait_ge(cleared, 4)
            fc = lambda X: rows(fcb, 0, CM, FR * X, (1, FR))
            sr = rows(small, 0, 1, SR, (1, FR))

            def layer0_stats(a):
                pe.wait_ge(on["sums"], a * per["sums"] + 1)
                mm(bank(3, 0, 128, 0, (1, 64)), tab["halves"][:, :], view(small, ST, (1, 64)), start=True, stop=True).then_inc(on["stats"], 1)

            def layer0_conv(a, j):
                pe.wait_ge(on["xd_loaded"], a * per["xd_loaded"] + per["xd_loaded"])
                for e in range(TAPS):
                    ins = mm(bank(j, 0, CM, 0, (XS, 32), (1, XS)), view(tab["toep"], CM * e, (1, CM)),
                             view(cut, 1 + 64 * 32 * j + 2 * e, (64, 32), (3, XS)), start=e == 0, stop=e == TAPS - 1)
                ins.then_inc(on["conv"], 1)

            def layer0_max(a):
                pe.wait_ge(on["conv_max"], a * per["conv_max"] + 1)
                nc.tensor.transpose(bank(0, 0, 128, 0, (1, CM)), rows(small, 0, CM, PM, (1, FR)), rows(tab["ident"], 0, CM, 0, (1, CM))).then_inc(on["max_turned"], 1)
                pe.wait_ge(on["max_diag"], a * per["max_diag"] + 1)
                mm(bank(1, 0, CM, 0, (1, FR)), view(tab["ones"], 0, (1, CM)), view(small, DGM, (1, FR)), start=True, stop=True).then_inc(on["max_spread"], 1)

            def layer0_where(a):
                pe.wait_ge(on["conv_exp"], a * per["conv_exp"] + 1)
                for X in range(XS):
                    ins = mm(bank(0, 0, 1, 0, (1, FR)), rows(tab["ok"], 0, CM, X, (1, 1)), fc(X), start=X == 0, stop=X == XS - 1)
                ins.then_inc(on["exp_sum"], 1)
                for h in range(2):
                    for X in range(XS):
                        mm(bank(2, 0, HID, FR * h, (1, FR)), rows(tab["where_w1"], 0, CM, 2 * HID * X + HID * h, (1, HID)), fc(X), start=X == 0, stop=False)
                    if h == 0:
                        pe.wait_ge(on["exp_sum_copied"], a * per["exp_sum_copied"] + 1)
                    ins = mm(bank(2, 0, HID, FR * h, (1, FR)), rows(tab["where_b1"], 0, 1, HID * h, (1, HID)), sr, start=False, stop=True)
                ins.then_inc(on["where_h1"], 1)
                pe.wait_ge(on["where_h1_copied"], a * per["where_h1_copied"] + 1)
                for h in range(2):
                    mm(bank(0, 0, HID, 0, (1, FR)), rows(tab["where_w2"], 0, HID, HID * h, (1, HID)), rows(big, 0, HID, H1 + FR * h, (1, FR)), start=h == 0, stop=False)
                mm(bank(0, 0, HID, 0, (1, FR)), tab["where_b2"][0:1, :], sr, start=False, stop=True).then_inc(on["where_h2"], 1)
                pe.wait_ge(on["where_h2_copied"], a * per["where_h2_copied"] + 1)
                mm(bank(1, 0, 128, 0, (1, 2)), rows(big, 0, HID, H2, (1, FR)), tab["where_wloc"][0:HID, :], start=True, stop=True)
                mm(bank(1, 0, 128, 2, (1, 1)), sr, rows(tab["ones"], 0, 1, 0, (1, 1)), start=True, stop=True).then_inc(on["where_z"], 1)

            def layer0_profiles(a):
                pe.wait_ge(on["norms"], a * per["norms"] + 1)
                for j in range(2):
                    nc.tensor.transpose(bank(2, 0, PROF, FR * j, (1, FR)), view(small, PR + PROF * j, (1, PROF)), tab["ident"][:, :])
                nc.tensor.transpose(bank(2, 0, 2 * D, 2 * FR, (1, FR)), view(small, RN, (1, 2 * D)), tab["ident"][:, :]).then_inc(on["profiles_turned"], 1)

            def layer0_cut(a):
                pe.wait_ge(on["turned_profiles_copied"], a * per["turned_profiles_copied"] + 1)
                pe.wait_ge(on["cut_loaded"], a * per["cut_loaded"] + per["cut_loaded"])
                passed(pe)
                for k in range(8):
                    u, t4 = k // 4, k % 4
                    if k >= 4:
                        pe.wait_ge(on["o1_copied"], a * per["o1_copied"] + k - 3)
                        passed(pe)
                    for j in range(16):
                        fu = 16 * t4 + j
                        q2, s_, r = fu // 32, fu // 4 % 8, fu % 4
                        ins = mm(bank(k % 4, 64 * u, 64 * u + 64, 28 * j, (1, D)), rows(frm, 64 * u, 64 * u + 64, 64 * (8 * s_ + 4 * q2 + r), (1, 64)),
                                 rows(cut, 64 * u, 64 * u + 64, WY + fu, (64, D)), start=j == 0, stop=True, skip_group_check=True)
                    ins.then_inc(on["o1"], 1)

            def layer0_digits(a):
                pe.wait_ge(on["o1_copied"], a * per["o1_copied"] + per["o1_copied"])
                passed(pe)
                for k in range(8):
                    u, t4 = k % 2, k // 2
                    if k >= 4:
                        if u == 0:
                            pe.wait_ge(on["digits_copied_a"], a * per["digits_copied_a"] + k // 2 - 1)
                        else:
                            pe.wait_ge(on["digits_copied_v"], a * per["digits_copied_v"] + k // 2 - 1)
                        passed(pe)
                    for j in range(16):
                        fu = 16 * t4 + j
                        ins = mm(bank(k % 4, 0, 32, 28 * j, (1, D)), rows(cut, 64 * u, 64 * u + 64, WX + fu, (64, 32)),
                                 rows(cut, 64 * u, 64 * u + 64, O1 + 28 * fu, (1, D)), start=j == 0, stop=True, skip_group_check=True)
                    ins.then_inc(on["digits"], 1)

            def layer0_what(a):
                pe.wait_ge(on["digits_normed"], a * per["digits_normed"] + 1)
                for k in range(4):
                    for j in range(7):
                        ins = mm(bank(0, 0, HID, FR * k, (1, FR)), view(tab["what_w1"], 400 * j + HID * k, (1, HID)), view(cut, DG + FR * j, (1, FR)), start=j == 0, stop=j == 6)
                ins.then_inc(on["what_h1"], 1)
                pe.wait_ge(on["what_h1_copied"], a * per["what_h1_copied"] + 1)
                for h in range(2):
                    for k in range(4):
                        ins = mm(bank(1, 0, HID, FR * h, (1, FR)), rows(tab["what_w2"], 0, HID, 200 * k + HID * h, (1, HID)),
                                 rows(big, 0, HID, HW1 + FR * k, (1, FR)), start=k == 0, stop=k == 3)
                ins.then_inc(on["what_h2"], 1)

            def layer0_dec(a):
                pe.wait_ge(on["what_sum"], a * per["what_sum"] + 1)
                for k in range(2):
                    ins = mm(bank(2, 0, 10, 0, (1, S)), rows(tab["what_wloc"], 0, HID, 10 * k, (1, 10)), rows(big, 0, HID, HS + S * k, (1, S)), start=k == 0, stop=k == 1)
                ins.then_inc(on["what_z"], 1)
                pe.wait_ge(on["what_z_copied"], a * per["what_z_copied"] + 1)
                for k in range(2):
                    ins = mm(bank(3, 0, HID, S * k, (1, S)), rows(tab["dec_w1"], 0, 10, HID * k, (1, HID)), rows(big, 0, 10, ZW, (1, S)), start=True, stop=True)
                ins.then_inc(on["dec_h1"], 1)
                pe.wait_ge(on["dec_h1_copied"], a * per["dec_h1_copied"] + 1)
                for k in range(4):
                    for h in range(2):
                        ins = mm(bank(0, 0, HID, S * k, (1, S)), rows(tab["dec_w2"], 0, HID, 400 * h + HID * k, (1, HID)),
                                 rows(big, 0, HID, D1 + S * h, (1, S)), start=h == 0, stop=h == 1)
                ins.then_inc(on["dec_h2"], 1)
                pe.wait_ge(on["dec_h2_copied"], a * per["dec_h2_copied"] + 1)
                for h in range(2):
                    for k in range(4):
                        ins = mm(bank(1 + h, 0, S, 0, (1, 392)), rows(d2, 0, HID + 1, S * k, (1, S)),
                                 rows(tab["dec_w3"], 0, HID + 1, D * D * k + 392 * h, (1, 392)), start=k == 0, stop=k == 3)
                ins.then_inc(on["dec_out"], 1)

            def layer0_aa(a):
                pe.wait_ge(on["digit_loaded"], a * per["digit_loaded"] + per["digit_loaded"])
                pe.wait_ge(on["rec_loaded"], a * per["rec_loaded"] + per["rec_loaded"])
                for k in range(4):
                    for j in range(2):
                        s_ = 2 * k + j
                        ins = mm(bank(k, 0, 128, 256 * j, (1, 256)), view(digit, 128 * s_, (1, 128)), view(frm, WRY + 256 * s_, (1, 256)), start=j == 0, stop=True, skip_group_check=True)
                    ins.then_inc(on["aa"], 1)

            def layer0_x1(a):
                pe.wait_ge(on["aa_copied"], a * per["aa_copied"] + per["aa_copied"])
                pe.wait_ge(on["wrx_normed"], a * per["wrx_normed"] + 1)
                for hs in range(2):
                    for q in range(4):
                        u = q // 2
                        if hs:
                            pe.wait_ge(on["x1_copied"], a * per["x1_copied"] + q + 1)
                        for j in range(2):
                            for s4 in range(4):
                                s_ = 4 * hs + s4
                                mm(bank(q, 0, 128, 256 * j + 64 * s4, (1, 64)),
                                   rows(raw, 64 * u, 64 * u + 64, 512 * s_ + 256 * (q % 2) + 128 * j, (1, 128)),
                                   rows(tab["ident"], 64 * u, 64 * u + 64, 64 * u, (1, 64)), start=j == 0 and s4 == 0, stop=False, skip_group_check=True)
                    for s4 in range(4):
                        for r in range(4):
                            for q in range(4):
                                s_ = 4 * hs + s4
                                j, h = r // 2, r % 2
                                ins = mm(bank(q, 64 * h, 64 * h + 64, 256 * j + 64 * s4, (1, 64)),
                                         rows(frm, 32 * q, 32 * q + 32, WRX + 64 * (4 * s_ + r), (1, 64)),
                                         rows(cut, 32 * q, 32 * q + 32, AA + 64 * (4 * s_ + r), (1, 64)), start=False, stop=True, skip_group_check=True)
                                if s4 == 3 and r == 3:
                                    ins.then_inc(on["x1"], 1)

            def half_stats(t, k):
                pe.wait_ge(on["b_sums"], t * per["b_sums"] + k)
                mm(bank(7, 0, 128, 0, (1, 64)), tab["ones"][:, :], view(bsmall, BST, (1, 64)), start=True, stop=True).then_inc(on["b_stats"], 1)

            def half_freq(t):
                pe.wait_ge(on["moments"], t * per["moments"] + 1)
                for k in range(5):
                    w = min(7, 32 - 7 * k) * NA
                    if k >= 4:
                        pe.wait_ge(on["dft_copied"], t * per["dft_copied"] + k - 3)
                    mm(bank(4 + k % 4, 0, 128, 0, (1, w)), tab["dft"][:, :], view(work, XNB + 7 * NA * k, (1, w)), start=True, stop=True).then_inc(on["dft"], 1)

            def half_mix(t):
                pe.wait_ge(on["v_loaded"], t * per["v_loaded"] + per["v_loaded"])
                pe.wait_ge(on["dft_copied"], t * per["dft_copied"] + per["dft_copied"])
                row = lambda n1: view(work, VV + n1, (NA, KB * SH))
                e = lambda j: view(mix_e, 64 * j, (1, 64))
                behind = {0: [(e(0), N + 1), (e(1), N + 2)], 1: [(e(2), N)], 2: [(e(3), N)], 3: [(e(3), N)]}
                for k in range(5):
                    if k >= 4:
                        pe.wait_ge(on["mixed_copied"], t * per["mixed_copied"] + k - 3)
                    for j in range(min(7, NH - 7 * k)):
                        for par in range(2):
                            n1 = 2 * (7 * k + j) + par
                            o = bank(4 + k % 4, 64 * par, 64 * par + 64, KB * SH * j, (1, KB * SH))
                            terms = [(view(mix_w, 64 * n1, (1, 64)), n1)] if n1 < N else behind[n1 - N]
                            for m, (l, r_) in enumerate(terms):
                                ins = mm(o, l, row(r_), start=j == 0 and m == 0, stop=m == len(terms) - 1 and n1 > 0, skip_group_check=True)
                            if n1 == 0:
                                ins = mm(o, tab["l1_bias"][0:1, :], rows(tab["ones"], 0, 1, 0, (1, KB * SH)), start=False, stop=True, skip_group_check=True)
                    ins.then_inc(on["mixed"], 1)

            def half_inverse(t):
                pe.wait_ge(on["y_loaded"], t * per["y_loaded"] + per["y_loaded"])
                pe.wait_ge(on["mixed_copied"], t * per["mixed_copied"] + per["mixed_copied"])
                for jj in range(2):
                    ins = mm(bank(4, 64 * jj, 64 * jj + 64, 0, (1, 128)), view(work, YK + 32 + jj, (NH, 64)), tab["idft"][:, :], start=True, stop=True, skip_group_check=True)
                ins.then_inc(on["corr"], 1)
                pe.wait_ge(on["corr_copied"], t * per["corr_copied"] + 1)
                for k in range(4):
                    for j in range(2):
                        mm(bank(4 + k, 0, 128, 256 * j, (1, 256)), tab["idft"][:, :], view(work, YK + 2 * SH * NH * (2 * k + j), (NH, 2 * SH), (1, 32)),
                           start=j == 0, stop=False, skip_group_check=True)
                    mm(bank(4 + k, 0, 128, 0, (1, 512)), view(bsmall, ES, (1, 128)), view(tab["sel"], 512 * k, (1, 512)), start=False, stop=True, skip_group_check=True).then_inc(on["idft"], 1)
                half_stats(t, 2)

            def half_conv2(t):
                pe.wait_ge(on["v2_loaded"], t * per["v2_loaded"] + per["v2_loaded"])
                pe.wait_ge(on["b_xn_ready"], t * per["b_xn_ready"] + 2)
                tap = lambda ky: view(tab["l2_taps"], 96 * ky, (1, 96))
                for k in range(6):
                    if k >= 4:
                        pe.wait_ge(on["conv2_copied"], t * per["conv2_copied"] + k - 3)
                    m = min(2, WB - 2 * k) * SH
                    b, v = 4 + k % 4, V2 + 512 * k
                    mm(bank(b, 0, 96, 0, (1, N * m)), tap(1), view(work, v, (1, N * m)), start=True, stop=False, skip_group_check=True)
                    mm(bank(b, 0, 96, 1, (N, m), (1, N - 1)), tap(0), view(work, v, (N, m), (1, N - 1)), start=False, stop=False, skip_group_check=True)
                    mm(bank(b, 0, 96, 0, (N, m), (1, N - 1)), tap(2), view(work, v + 1, (N, m), (1, N - 1)), start=False, stop=True, skip_group_check=True).then_inc(on["conv2"], 1)
                half_stats(t, 3)

            def half_gate(t, i):
                pe.wait_ge(on["b_xn_ready"], t * per["b_xn_ready"] + 3)
                for k in range(4):
                    if k % 2 == 0:
                        pe.wait_ge(on["gate_prod"], t * per["gate_prod"] + k // 2 + 1)
                    mm(bank(4 + k, 0, 128, 0, (1, 512)), tab["halves"][:, :], view(work, PRODS + 512 * k, (1, 512)), start=True, stop=True).then_inc(on["gate_sum"], 1)

            def half_turn(t, i):
                pe.wait_ge(on["added"], t * per["added"] + 1)
                for k in range(4):
                    for par in range(2):
                        for j in range(2):
                            ins = nc.tensor.transpose(bank(4 + k, 0, 128, 256 * par + 128 * j, (1, 128)), half(i, 512 * (2 * k + j) + par, (2, 128)), tab["ident"][:, :])
                    ins.then_inc(on["turned"], 1)

            def turn(g, a):
                for i in range(2):
                    t = g * 2 + i if isinstance(g, int) else pe.snap(g * 2 + i)
                    half_stats(t, 1)
                    half_freq(t)
                    if a is not None and i == 0:
                        layer0_stats(a)
                    if a is not None and i == 1:
                        layer0_cut(a)
                    half_mix(t)
                    if a is not None and i == 0:
                        for j in range(4):
                            layer0_conv(a, j)
                    if a is not None and i == 1:
                        layer0_digits(a)
                        layer0_what(a)
                    half_inverse(t)
                    if a is not None and i == 0:
                        layer0_max(a)
                        layer0_where(a)
                    if a is not None and i == 1:
                        layer0_dec(a)
                    half_conv2(t)
                    if a is not None and i == 0:
                        layer0_profiles(a)
                    half_gate(t, i)
                    if a is not None and i == 1:
                        layer0_aa(a)
                    half_turn(t, i)
                if a is not None:
                    layer0_x1(a)

            layer0_stats(0)
            for j in range(4):
                layer0_conv(0, j)
            layer0_max(0)
            layer0_where(0)
            layer0_profiles(0)
            layer0_cut(0)
            layer0_digits(0)
            layer0_what(0)
            layer0_dec(0)
            layer0_aa(0)
            layer0_x1(0)
            if groups > 1:
                with pe.Fori(0, groups - 1) as g:
                    turn(g, pe.snap(g + 1))
            turn(groups - 1, None)


def kernel(**inputs):
    import concourse.bacc as bacc
    from concourse.bass_utils import run_bass_kernel_spmd

    a = {n: np.asarray(v) for n, v in inputs.items()}
    x = np.ascontiguousarray(a.pop("x"))
    nc = bacc.Bacc("TRN2", target_bir_lowering=False, num_devices=1)
    arrays = {"x_dram": x, **{f"{n}_dram": v for n, v in {**layouts(a), **constants()}.items()}}
    aps = {n[:-5]: nc.dram_tensor(n, v.shape, F32, kind="ExternalInput").ap() for n, v in arrays.items()}
    out = nc.dram_tensor("out_dram", x.shape, F32, kind="ExternalOutput").ap()
    program(nc, aps["x"], out, aps, x.shape[0] // S)
    r = run_bass_kernel_spmd(nc, [arrays], core_ids=[0])
    return r.results[0]["out_dram"]
```

```python
from contextlib import ExitStack

import numpy as np

import concourse.bass as bass
from concourse import mybir

F32 = mybir.dt.float32
ALU = mybir.AluOpType
ACT = mybir.ActivationFunctionType
AX = mybir.AxisListType.X

B, C, N = 512, 16, 64
S = 8
SH = S // 2
GROUPS = B // S
FR = S * C
D = 28
CO = N - D + 1
PH, XS = 3, 13
CM = PH * CO
TAPS = 15
HID = 100
PROF = 96
K2 = N // 2 + 1
KB = 17
NA = N + 3
NH = 34
WB = 11
CNT = 2 * N * N
THR = 1000.0 * float(np.finfo(np.float32).eps)
EPS = 1e-5
SETUP = 26
LINKS = 20
B_LINKS = 19
VP = 6

SIGNALS = {
    "raw_loaded": 256, "squares": 1, "sums": 1, "variance": 1, "deviation": 1, "stats": 1, "xn_ready": 1,
    "vector_link": LINKS, "xd_loaded": 64, "xd_copied": 1, "conv": 4, "conv_copied": 4, "conv_max": 1, "max_turned": 1,
    "max_diag": 1, "max_spread": 1, "conv_shifted": 1, "conv_exp": 1,
    "where_h1": 1, "where_h1_copied": 1, "where_h2": 1, "where_h2_copied": 1, "where_z": 1, "where_zz": 1,
    "where_tanh": 1, "shift": 1, "profile_abs": 1, "profiles": 1, "norms": 1, "profiles_turned": 1, "totals": 1, "norms_turned": 1,
    "turned_profiles_copied": 1, "turned_norms_copied": 1, "rec_stored": 32, "cut_stored": 32, "norms_stored": 16, "cut_rows_loaded": 32, "cut_loaded": 32,
    "cut_norms_loaded": 128, "rec_loaded": 128, "rec_norms_loaded": 128, "wrx_normed": 1, "o1": 8,
    "o1_copied": 8, "digits": 8, "digits_copied": 8, "digits_normed": 1, "what_h1": 1,
    "what_h1_copied": 1, "what_h2": 1, "what_h2_copied": 1, "what_sum": 1, "what_z": 1, "what_z_copied": 1,
    "dec_h1": 1, "dec_h1_copied": 1, "dec_h2": 1, "dec_h2_copied": 1, "dec_out": 1, "dec_tanh": 1,
    "dec_sig": 1, "dec_stored": 16, "digit_loaded": 64, "aa": 4, "aa_copied": 4, "x1": 8, "x1_copied": 8,
}
HALF_SIGNALS = {
    "b_squares": 3, "b_sums": 3, "b_variance": 3, "b_deviation": 3, "b_stats": 3, "b_scales": 3, "b_xn_ready": 3, "b_xn_rest": 3,
    "b_link": B_LINKS, "moments": 1, "dft": 5, "dft_copied": 5, "z_stored": 128, "v_loaded": 128,
    "mixed": 5, "mixed_copied": 5, "y_stored": 128, "y_loaded": 128, "corr": 1, "corr_copied": 1, "idft": 4,
    "x2_ready": 4, "xn2_stored": 32, "edge_cleared": 1, "v2_loaded": 128, "conv2": 6, "conv2_copied": 6,
    "y2_stored": 96, "y2_loaded": 32, "x3_ready": 1, "gate_prod": 2, "gate_sum": 4, "gated": 4, "added": 1,
    "turned": 4, "turned_copied": 4, "out_stored": 64,
}


def constants():
    k = {}
    p = np.arange(128)
    k["ident"] = np.eye(128)
    k["ones"] = np.ones((128, 128))
    k["halves"] = (p[:, None] // 64 == p[None, :] // 64) * 1.0
    n = np.arange(N)
    f = np.zeros((N, N))
    g = np.zeros((N, N))
    for kk in range(K2):
        f[:, kk] = np.cos(2 * np.pi * kk * n / N)
        g[kk, :] = (1 if kk in (0, N // 2) else 2) * np.cos(2 * np.pi * kk * n / N) / N
    for kk in range(1, N // 2):
        f[:, N // 2 + kk] = -np.sin(2 * np.pi * kk * n / N)
        g[N // 2 + kk, :] = -2 * np.sin(2 * np.pi * kk * n / N) / N
    k["dft"] = np.kron(np.eye(2), f)
    k["idft"] = np.kron(np.eye(2), g)
    k["iota"] = np.broadcast_to(np.arange(PROF) - 31.0, (128, PROF))
    i = np.concatenate([np.arange(D)[::-1], np.arange(D)[::-1], np.arange(N), np.arange(N)]) + 0.5
    u = np.arange(PROF)[:, None] - 4
    k["windows"] = np.concatenate([(u >= np.arange(m)) & (u < np.arange(m) + w) for m, w in ((D, N), (N, D))], 1) * 1.0
    k["place"] = np.broadcast_to(i, (128, 2 * D + 2 * N))
    ok = np.zeros((128, XS))
    for ph in range(PH):
        for x in range(XS):
            if PH * x + ph < CO:
                ok[ph * CO:(ph + 1) * CO, x] = 1
    k["ok"] = ok
    k["low"] = (1 - ok[:, XS - 1:]) * -1e30
    th = 2 * np.pi * n / N
    k["cos_sin"] = np.broadcast_to(np.concatenate([np.cos(th), np.sin(th)]), (128, 2 * N))
    sel = np.zeros((2, 8, 2, SH, 8, 2, SH, 32))
    for a in range(8):
        for t in range(SH):
            for par in range(2):
                rows = 2 * np.arange(32) + par
                sel[0, a, 0, t, a, par, t] = 1
                sel[0, a, 1, t, a, par, t] = np.cos(th)[rows]
                sel[1, a, 0, t, a, par, t] = np.sin(th)[rows]
    k["sel"] = sel.reshape(128, 2048)
    sa = np.ones((4, 2, C, 2, 2, C))
    sa[:, 1, :, :, 0] = -1
    sb = np.ones((4, 2, C, 2, 2, C))
    sb[:, :, :, :, 0] = -1
    sb[:, 1, :, :, 1] = -1
    sb[:, 0, :, :, 0] = -1
    k["sign_a"], k["sign_b"] = sa.reshape(128, 64), sb.reshape(128, 64)
    k["zero"] = np.zeros((4, C * SH * NA))
    return {n_: np.ascontiguousarray(a, dtype=np.float32) for n_, a in k.items()}


def layouts(a):
    w = {}
    k = a["L0_conv_digit_mean"][::-1, ::-1]
    t = np.zeros((TAPS, 2, N, PH, CO), np.float32)
    for e in range(2 * TAPS):
        for ph in range(PH):
            if 0 <= e - ph < D:
                for y in range(CO):
                    t[e // 2, e % 2, y:y + D, ph, y] = k[:, e - ph]
    w["toep"] = t.reshape(TAPS, 128, CM).transpose(1, 0, 2)
    t = np.zeros((PH, CO, XS, 2 * HID + 1), np.float32)
    w1 = a["L0_conv_where_w1"].reshape(CO, CO, 2 * HID)
    for ph in range(PH):
        for x in range(XS):
            if PH * x + ph < CO:
                t[ph, :, x, 0] = 1
                t[ph, :, x, 1:] = w1[:, PH * x + ph]
    w["where_w1"] = t.reshape(CM, XS, 2 * HID + 1)
    w["where_b1"] = np.broadcast_to(a["L0_conv_where_b1"], (128, 2 * HID))
    t = np.zeros((HID + 1, 2, HID), np.float32)
    t[0, 0] = a["L0_conv_where_b2"][:HID]
    t[1:, 0] = a["L0_conv_where_w2"][:HID, :HID]
    t[:HID, 1] = a["L0_conv_where_w2"][HID:, :HID]
    w["where_w2"] = t
    w["where_wloc"] = a["L0_conv_where_wloc"]
    w["where_bloc"] = np.broadcast_to(a["L0_conv_where_bloc"], (128, 2))
    t = np.zeros((4, 32, 7, 400), np.float32)
    t[:, 32 - D:] = a["L0_conv_what_w1"].reshape(D, D, 400)[::-1, ::-1].reshape(4, 7, D, 400).transpose(0, 2, 1, 3)
    w["what_w1"] = t.reshape(128, 7, 400)
    w["what_b1"] = a["L0_conv_what_b1"].reshape(4, HID).T
    w["what_w2"] = a["L0_conv_what_w2"].reshape(4, HID, 200).transpose(1, 0, 2)
    w["what_b2"] = a["L0_conv_what_b2"].reshape(2, HID).T
    w["what_wloc"] = a["L0_conv_what_wloc"].reshape(2, HID, 10).transpose(1, 0, 2)
    w["what_bloc"] = a["L0_conv_what_bloc"][:, None]
    w["dec_w1"] = a["L0_conv_dec_w1"]
    w["dec_b1"] = a["L0_conv_dec_b1"].reshape(2, HID).T
    w["dec_w2"] = a["L0_conv_dec_w2"].reshape(2, HID, 400).transpose(1, 0, 2)
    w["dec_b2"] = a["L0_conv_dec_b2"].reshape(4, HID).T
    t = np.zeros((HID + 1, 4, D * D), np.float32)
    t[:HID] = a["L0_conv_dec_w3"][:, ::-1].reshape(4, HID, D * D).transpose(1, 0, 2)
    t[HID, 3] = a["L0_conv_dec_b3"][::-1]
    w["dec_w3"] = t
    real, imag = a["L1_conv_w_real"], a["L1_conv_w_imag"]
    pl = np.zeros((3, 2, 4, 2, C, 2, 2, C), np.float32)
    for t_ in range(3):
        for b in range(3):
            wr, wi = real[:, :, 2 - t_, 2 - b], imag[:, :, 2 - t_, 2 - b]
            for w_ in range(2):
                for part in range(2):
                    pl[t_, 0, w_ + b, part, :, w_, part] = wr
                    pl[t_, 0, w_ + b, part, :, w_, 1 - part] = wi
                    pl[t_, 1, w_ + b, part, :, w_, part] = wi
                    pl[t_, 1, w_ + b, part, :, w_, 1 - part] = wr
    w["taps"] = pl.reshape(6, 128, 64).transpose(1, 0, 2)
    w["l1_bias"] = np.stack([np.stack([a["L1_conv_b_real"], a["L1_conv_b_imag"]])] * 2).reshape(1, 64)
    kw = a["L2_conv_K"].reshape(C, 3, 3, C)
    t = np.zeros((3, 8, C, 6, C), np.float32)
    for ky in range(3):
        for kx in range(3):
            for w_ in range(6):
                t[ky, w_ + kx, :, w_] = kw[:, ky, kx]
    w["l2_taps"] = t.reshape(3, 128, 96).transpose(1, 0, 2)
    return {n_: np.ascontiguousarray(v) for n_, v in w.items()}


PERSIST = ["toep", "where_w1", "where_w2", "where_wloc", "where_bloc", "what_w1", "what_b1",
           "what_w2", "what_b2", "what_wloc", "what_bloc", "dec_w1", "dec_b1", "dec_w2", "dec_b2", "dec_w3",
           "l1_bias", "l2_taps", "ident", "ones", "halves", "dft", "idft", "iota", "windows", "place", "ok", "low", "cos_sin", "sel"]


def program(nc, x, out, src, groups=GROUPS):
    ctx = ExitStack()
    with ctx:
        def sb(name, *shape):
            return ctx.enter_context(nc.sbuf_tensor(name, [128, *shape], F32))

        def view(t, off, *dims):
            row = t.shape[1]
            return bass.AP(tensor=t[:, :].tensor, offset=off, ap=[[row, 128]] + [list(d) for d in dims])

        def rows(t, p0, p1, off, *dims):
            row = t.shape[1]
            return bass.AP(tensor=t[:, :].tensor, offset=p0 * row + off, ap=[[row, p1 - p0]] + [list(d) for d in dims])

        tab = {}
        for n in PERSIST:
            shape = src[n].shape
            tab[n] = sb("t_" + n, int(np.prod(shape[1:])))
        mix_w = sb("mix_w", N * 64)
        mix_e = sb("mix_e", 4 * 64)
        raw = sb("raw", 4096)
        x1 = sb("x1", 4096)
        digit = sb("digit", S * 128)
        cut = sb("cut", 8200)
        frm = sb("frm", 4096)
        fcb = sb("fcb", KB * SH * NH)
        small = sb("small", 1712)
        big = sb("big", 840)
        d2 = sb("d2", 32)
        work = sb("work", 5632)
        bsmall = sb("bsmall", 320)
        PS = ctx.enter_context(nc.psum_tensor("PS", [128, 8 * 512], F32))

        def bank(b, p0, p1, off, *dims):
            return bass.AP(tensor=PS[:, :].tensor, offset=p0 * 4096 + b * 512 + off, ap=[[4096, p1 - p0]] + [list(d) for d in dims])

        WY, WX, O1, DG, NY = 0, 1792, 3840, 5632, 6528
        AA, RBX, RBY, SG = 0, 2048, 4096, 6144
        WRY, WRX = 0, 2048
        PR, NX, TOT, RN, SS, TMP = 0, 384, 512, 696, 880, 1064
        ST, MS, RS, NM, TV = 1248, 1312, 1344, 1376, 1408
        PM, DGM, MX, ZT, TT, ZI = 1440, 1568, 1696, 1698, 1700, 1704
        HW1, HW2, HS, ZW, D1 = 0, 512, 768, 784, 792
        H1, H2 = 0, 256
        XNB, ZZ, VV = 0, 2304, 0
        YK = 0
        SQ = 0
        V2, Y2O, PRODS, OUT = 0, 2816, 2048, 3584
        BST, BMS, BRS, BNM, BTV, ES = 0, 64, 96, 128, 160, 192

        zs = nc.dram_tensor("zs", (72, C, SH * NA), F32).ap()
        ys = nc.dram_tensor("ys", (2, 2 * KB, C, 2 * SH * NH), F32).ap()
        xs = nc.dram_tensor("xs", (68, C, SH * N), F32).ap()
        y2s = nc.dram_tensor("y2s", (66, C, SH * N), F32).ap()
        pt = nc.dram_tensor("pt", (2, 2, PROF, FR // 2), F32).ap()
        pd = nc.dram_tensor("pd", (2, FR, PROF), F32).ap()
        rnt = nc.dram_tensor("rnt", (2 * D, FR), F32).ap()
        rnd = nc.dram_tensor("rnd", (2, FR, N), F32).ap()
        ds = nc.dram_tensor("ds", (S, D, D), F32).ap()

        def passed(eng):
            eng.sem_inc(waits_passed, 1)

        on = {n: ctx.enter_context(nc.semaphore(n)) for n in [*SIGNALS, *HALF_SIGNALS]}
        per = {**SIGNALS, **HALF_SIGNALS}
        waits_passed = ctx.enter_context(nc.semaphore("waits_passed"))
        loaded = ctx.enter_context(nc.semaphore("tables_loaded"))
        zeroed = ctx.enter_context(nc.semaphore("scratch_zeroed"))
        cleared = ctx.enter_context(nc.semaphore("buffers_cleared"))
        mixing = ctx.enter_context(nc.semaphore("mix_tables_ready"))
        TABLES = 16 * (len(PERSIST) + 4)
        half = lambda i, off, *d: view(x1, 256 * i + off, *d)
        flat = lambda t, off, *d: bass.AP(tensor=t.tensor, offset=off, ap=[list(e) for e in d])
        block = ctx.enter_context(nc.Block())


        @block.sync
        def _(sp):
            for n in PERSIST:
                a = src[n]
                sp.dma_start(tab[n][0:a.shape[0], :], a if len(a.shape) == 2 else a.rearrange("a b c -> a (b c)")).then_inc(loaded, 16)
            sp.dma_start(view(cut, 0, (1, 384)), src["taps"].rearrange("a b c -> a (b c)")).then_inc(loaded, 16)
            sp.dma_start(view(cut, 384, (1, 64)), src["sign_a"]).then_inc(loaded, 16)
            sp.dma_start(view(cut, 448, (1, 64)), src["sign_b"]).then_inc(loaded, 16)
            sp.dma_start(view(cut, 704, (1, 2 * HID)), src["where_b1"]).then_inc(loaded, 16)
            z = src["zero"]
            for a, b in ((0, 1), (34, 38), (69, 72)):
                sp.dma_start(zs[a:b].rearrange("a b c -> a (b c)"), z[0:b - a, :]).then_inc(zeroed, 16)
            for a, b in ((0, 1), (65, 68)):
                sp.dma_start(xs[a:b].rearrange("a b c -> a (b c)"), z[0:b - a, 0:C * SH * N]).then_inc(zeroed, 16)
            sp.dma_start(y2s[63:64].rearrange("a b c -> a (b c)"), z[0:1, 0:C * SH * N]).then_inc(zeroed, 16)
            sp.wait_ge(zeroed, 16 * 6)
            sp.wait_ge(mixing, SETUP)

            def layer0_load(a, first):
                b0 = a * S if first else sp.snap(a * S)
                for s in range(S):
                    if not first and s % 4 == 0:
                        sp.wait_ge(on["x1"], a * per["x1"] - 4 + s)
                        passed(sp)
                    for u in range(2):
                        d = x[bass.ds(b0 + s, 1), 8 * u:8 * u + 8].rearrange("s c n m -> n (s c) m")
                        sp.dma_start(rows(raw, 64 * u, 64 * u + 64, 512 * s, (64, 8), (1, 64)), d).then_inc(on["raw_loaded"], 16)

            def layer0_copies(a):
                sp.wait_ge(on["xn_ready"], a * per["xn_ready"] + 1)
                for h in range(2):
                    for q in (2 - 2 * h, 3 - 2 * h):
                        u = q // 2
                        sp.dma_start(rows(cut, 64 * h, 64 * h + 64, 1 - h + 2048 * q, (256, S), (1, 256)),
                                     rows(frm, 64 * u, 64 * u + 64, 256 * (q % 2), (512, S), (1, 256))).then_inc(on["xd_loaded"], 16)

            def layer0_profiles(a):
                sp.wait_ge(on["profiles"], a * per["profiles"] + 1)
                sp.dma_start(pd.rearrange("a f u -> f a u"), view(small, PR + 2 * PROF, (PROF, 2), (1, PROF))).then_inc(on["rec_stored"], 16)
                sp.wait_ge(on["turned_profiles_copied"], a * per["turned_profiles_copied"] + 1)
                for u in range(2):
                    sp.dma_start(pt[u].rearrange("a o f -> o a f"), rows(big, 0, PROF, 64 * u, (FR, 2), (1, 64))).then_inc(on["cut_stored"], 16)

            def layer0_norms(a):
                sp.wait_ge(on["norms"], a * per["norms"] + 1)
                sp.dma_start(rnd.rearrange("a f u -> f a u"), view(small, RN + 2 * D, (N, 2), (1, N))).then_inc(on["rec_stored"], 16)
                sp.wait_ge(on["turned_norms_copied"], a * per["turned_norms_copied"] + 1)
                sp.dma_start(rnt, rows(big, 0, 2 * D, 4 * FR, (1, FR))).then_inc(on["norms_stored"], 16)

            def layer0_profiles_back(a, ax):
                if ax == 0:
                    sp.wait_ge(on["cut_stored"], a * per["cut_stored"] + per["cut_stored"])
                    passed(sp)
                at, no = ((WY, D), (WX, 32))[ax]
                for u in range(2):
                    sp.dma_start(rows(cut, 64 * u, 64 * u + 64, at, (1, 64 * no)),
                                 flat(pt, ((2 * u + ax) * PROF + 32 - no) * 64, (64, 64), (1, 64 * no))).then_inc(on[("cut_rows_loaded", "cut_loaded")[ax]], 16)

            def layer0_norms_back(a):
                sp.wait_ge(on["norms_stored"], a * per["norms_stored"] + per["norms_stored"])
                passed(sp)
                for q in range(4):
                    sp.dma_start(rows(cut, 32 * q, 32 * q + 32, NY, (1, 7 * FR)), flat(rnt, 7 * FR * q, (0, 32), (1, 7 * FR))).then_inc(on["cut_norms_loaded"], 16)
                    sp.dma_start(rows(small, 32 * q + 32 - D, 32 * q + 32, NX, (1, FR)), rnt[D:2 * D, :]).then_inc(on["cut_norms_loaded"], 16)

            def layer0_rec(a):
                sp.wait_ge(on["rec_stored"], a * per["rec_stored"] + per["rec_stored"])
                passed(sp)
                sp.wait_ge(on["o1"], a * per["o1"] + per["o1"])
                passed(sp)
                for q in range(4):
                    for ax, at in ((0, WRY), (1, WRX)):
                        sp.dma_start(rows(frm, 32 * q, 32 * q + 32, at, (64, 32), (1, 64)),
                                     flat(pd, (ax * FR + 32 * q) * PROF, (1, 32), (PROF, 32), (1, 64))).then_inc(on["rec_loaded"], 16)

            def layer0_rec_norms(a):
                sp.wait_ge(on["what_h1"], a * per["what_h1"] + 1)
                passed(sp)
                for q in range(4):
                    for ax, at in ((0, RBY), (1, RBX)):
                        sp.dma_start(rows(cut, 32 * q, 32 * q + 32, at, (1, 2048)), flat(rnd, (ax * FR + 32 * q) * N, (0, 32), (1, 2048))).then_inc(on["rec_norms_loaded"], 16)

            def layer0_digit(a):
                sp.wait_ge(on["dec_sig"], a * per["dec_sig"] + 1)
                sp.dma_start(ds.rearrange("s a b -> s (a b)"), rows(cut, 0, S, SG, (1, D * D))).then_inc(on["dec_stored"], 16)
                sp.wait_ge(on["dec_stored"], a * per["dec_stored"] + 16)
                passed(sp)
                for q in range(4):
                    sp.dma_start(rows(digit, 32 * q + 32 - D, 32 * q + 32, 32 * q + 32 - D, (128, S), (1, D)), ds.rearrange("s a b -> a s b")).then_inc(on["digit_loaded"], 16)

            def half_windows(t):
                sp.wait_ge(on["dft_copied"], t * per["dft_copied"] + per["dft_copied"])
                for h in range(2):
                    for a, b, to in ((0, 32, 1), (32, 33, 33), (33, 49, 38), (49, 64, 54)):
                        dst = zs[to:to + b - a].rearrange("k (p h) n -> k h p n", h=2)[:, h]
                        sp.dma_start(dst, rows(work, 64 * h + a, 64 * h + b, ZZ, (SH * NA, 8), (1, SH * NA))).then_inc(on["z_stored"], 16)

            def half_windows_back(t):
                sp.wait_ge(on["z_stored"], t * per["z_stored"] + per["z_stored"])
                passed(sp)
                for w in range(4):
                    for part in range(2):
                        s0, p0 = 36 * part + w, 32 * w + 16 * part
                        sp.dma_start(rows(work, p0, p0 + 16, VV, (SH * NA, KB), (1, SH * NA)), zs[s0:s0 + 33:2].rearrange("b c n -> c b n")).then_inc(on["v_loaded"], 16)

            def half_mixed(t):
                sp.wait_ge(on["mixed_copied"], t * per["mixed_copied"] + per["mixed_copied"])
                for par in range(2):
                    for w in range(2):
                        for part in range(2):
                            p0 = 64 * par + 32 * w + 16 * part
                            dst = ys[part, w:w + 33:2, :, par * SH * NH:(par + 1) * SH * NH].rearrange("b c n -> c b n")
                            sp.dma_start(dst, rows(fcb, p0, p0 + 16, 0, (SH * NH, KB), (1, SH * NH))).then_inc(on["y_stored"], 16)
                sp.wait_ge(on["y_stored"], t * per["y_stored"] + per["y_stored"])
                passed(sp)
                for h in range(2):
                    for a, b, part, k in ((0, 32, 0, 0), (32, 33, 0, 32), (33, 49, 1, 1), (49, 64, 1, 17)):
                        d = ys[part, k:k + b - a].rearrange("k (p h) n -> k h p n", h=2)[:, h]
                        sp.dma_start(rows(work, 64 * h + a, 64 * h + b, YK, (2 * SH * NH, 8), (1, 2 * SH * NH)), d).then_inc(on["y_loaded"], 16)

            def half_columns(t):
                sp.wait_ge(on["b_xn_ready"], t * per["b_xn_ready"] + 2)
                passed(sp)
                sp.wait_ge(on["b_xn_rest"], t * per["b_xn_rest"] + 2)
                for h in range(2):
                    dst = xs[1:65].rearrange("k (p h) n -> k h p n", h=2)[:, h]
                    sp.dma_start(dst, rows(work, 64 * h, 64 * h + 64, XNB, (SH * N, 8), (1, SH * N))).then_inc(on["xn2_stored"], 16)
                sp.wait_ge(on["xn2_stored"], t * per["xn2_stored"] + per["xn2_stored"])
                passed(sp)
                for w in range(8):
                    sp.dma_start(rows(work, 16 * w, 16 * w + 16, V2, (SH * N, WB), (1, SH * N)), xs[w:w + 61:6].rearrange("b c n -> c b n")).then_inc(on["v2_loaded"], 16)

            def half_back(t):
                sp.wait_ge(on["conv2_copied"], t * per["conv2_copied"] + per["conv2_copied"])
                passed(sp)
                sp.wait_ge(on["edge_cleared"], t * per["edge_cleared"] + 1)
                for w in range(6):
                    nb = WB if w < 3 else WB - 1
                    dst = y2s[w:w + 6 * (nb - 1) + 1:6].rearrange("b c n -> c b n")
                    sp.dma_start(dst, rows(work, 16 * w, 16 * w + 16, Y2O, (SH * N, nb), (1, SH * N))).then_inc(on["y2_stored"], 16)
                sp.wait_ge(on["y2_stored"], t * per["y2_stored"] + per["y2_stored"])
                passed(sp)
                for h in range(2):
                    d = y2s[0:64].rearrange("k (p h) n -> k h p n", h=2)[:, h]
                    sp.dma_start(rows(work, 64 * h, 64 * h + 64, 0, (SH * N, 8), (1, SH * N)), d).then_inc(on["y2_loaded"], 16)

            def half_out(t):
                b0 = sp.snap(t * SH) if not isinstance(t, int) else t * SH
                sp.wait_ge(on["turned_copied"], t * per["turned_copied"] + per["turned_copied"])
                passed(sp)
                for s4 in range(SH):
                    dst = out[bass.ds(b0 + s4, 1)].rearrange("s (p h) (n e) m -> (s n) (p h) (e m)", h=2, e=2)
                    sp.dma_start(dst, rows(work, 32 * s4, 32 * s4 + 32, OUT, (128, 16), (1, 128))).then_inc(on["out_stored"], 16)

            def turn(g, a):
                for i in range(2):
                    t = g * 2 + i if isinstance(g, int) else sp.snap(g * 2 + i)
                    first, second = a is not None and i == 0, a is not None and i == 1
                    if first:
                        layer0_load(a, False)
                    half_windows(t)
                    if second:
                        layer0_profiles(a)
                        layer0_profiles_back(a, 0)
                    half_windows_back(t)
                    if second:
                        layer0_norms(a)
                        layer0_profiles_back(a, 1)
                        layer0_norms_back(a)
                    if first:
                        layer0_copies(a)
                    half_mixed(t)
                    half_columns(t)
                    if second:
                        layer0_rec(a)
                    half_back(t)
                    if second:
                        layer0_rec_norms(a)
                        layer0_digit(a)
                    half_out(t)

            layer0_load(0, True)
            layer0_copies(0)
            layer0_profiles(0)
            layer0_profiles_back(0, 0)
            layer0_norms(0)
            layer0_profiles_back(0, 1)
            layer0_norms_back(0)
            layer0_rec(0)
            layer0_rec_norms(0)
            layer0_digit(0)
            if groups > 1:
                with sp.Fori(0, groups - 1) as g:
                    turn(g, sp.snap(g + 1))
            turn(groups - 1, None)
            sp.wait_ge(on["out_stored"], 16 + 2 * groups * per["out_stored"])

        @block.gpsimd
        def _(pool):
            nc.gpsimd.memset(digit[:, :], 0.0).then_inc(cleared, 1)
            nc.gpsimd.memset(d2[:, :], 1.0).then_inc(cleared, 1)
            nc.gpsimd.memset(view(small, NX, (1, FR)), 0.0).then_inc(cleared, 1)
            nc.gpsimd.memset(view(cut, 8192, (1, 8)), 0.0).then_inc(cleared, 1)
            nc.gpsimd.sem_inc(on["out_stored"], 16)
            with pool.Fori(0, groups) as a:
                pool.wait_ge(on["rec_norms_loaded"], a * per["rec_norms_loaded"] + per["rec_norms_loaded"])
                pool.wait_ge(on["rec_loaded"], a * per["rec_loaded"] + per["rec_loaded"])
                w = view(frm, WRX, (1, 2048))
                nc.gpsimd.tensor_tensor(w, w, view(cut, RBX, (1, 2048)), ALU.mult).then_inc(on["wrx_normed"], 1)

        @block.scalar
        def _(act):
            def copy(o, i):
                return nc.scalar.activation(o, i, ACT.Copy)

            act.wait_ge(loaded, TABLES)
            act.wait_ge(cleared, 4)

            def layer0_squares(a):
                act.wait_ge(on["raw_loaded"], a * per["raw_loaded"] + per["raw_loaded"])
                nc.scalar.activation(frm[:, :], raw[:, :], ACT.Square).then_inc(on["squares"], 1)
                act.wait_ge(on["variance"], a * per["variance"] + 1)
                v = view(small, RS, (1, 32))
                nc.scalar.activation(v, v, ACT.Sqrt).then_inc(on["deviation"], 1)

            def layer0_conv(a, j):
                act.wait_ge(on["conv"], a * per["conv"] + j + 1)
                copy(rows(fcb, 0, CM, 32 * j, (1, 32), (FR, XS)), bank(j, 0, CM, 0, (XS, 32), (1, XS))).then_inc(on["conv_copied"], 1)

            def layer0_exp(a):
                act.wait_ge(on["conv_shifted"], a * per["conv_shifted"] + 1)
                fc = rows(fcb, 0, CM, 0, (1, XS * FR))
                nc.scalar.activation(fc, fc, ACT.Exp).then_inc(on["conv_exp"], 1)

            def layer0_hidden(a):
                act.wait_ge(on["where_h1"], a * per["where_h1"] + 1)
                nc.scalar.activation(rows(big, 0, HID + 1, H1, (1, FR)), bank(2, 0, HID + 1, 0, (1, FR)), ACT.Relu)
                nc.scalar.activation(rows(big, 0, HID, H1 + FR, (1, FR)), bank(2, 0, HID, FR, (1, FR)), ACT.Relu).then_inc(on["where_h1_copied"], 1)
                act.wait_ge(on["where_h2"], a * per["where_h2"] + 1)
                nc.scalar.activation(rows(big, 0, HID, H2, (1, FR)), bank(0, 0, HID, 0, (1, FR)), ACT.Relu).then_inc(on["where_h2_copied"], 1)
                act.wait_ge(on["where_zz"], a * per["where_zz"] + 1)
                nc.scalar.activation(view(small, ZT, (1, 2)), view(small, ZI, (1, 2)), ACT.Tanh).then_inc(on["where_tanh"], 1)
                act.wait_ge(on["shift"], a * per["shift"] + 1)
                for j in range(4):
                    t = view(small, TT + 1 - j % 2, (1, 1))
                    ins = nc.scalar.activation(view(small, PR + PROF * j, (1, PROF)), tab["iota"][:, :], ACT.Abs, bias=t, scale=1.0 if j < 2 else -1.0)
                ins.then_inc(on["profile_abs"], 1)

            def layer0_profiles(a):
                act.wait_ge(on["profiles_turned"], a * per["profiles_turned"] + 1)
                copy(rows(big, 0, PROF, 0, (1, 4 * FR)), bank(2, 0, PROF, 0, (1, 4 * FR))).then_inc(on["turned_profiles_copied"], 1)

            def layer0_norms(a):
                act.wait_ge(on["norms_turned"], a * per["norms_turned"] + 1)
                copy(rows(big, 0, 2 * D, 4 * FR, (1, FR)), bank(2, 0, 2 * D, 0, (1, FR))).then_inc(on["turned_norms_copied"], 1)

            def layer0_cut(a, first, last):
                for k in range(first, last):
                    act.wait_ge(on["o1"], a * per["o1"] + k + 1)
                    u = k % 2
                    copy(rows(cut, 64 * u, 64 * u + 64, O1 + 448 * (k // 2), (1, 448)), bank(k % 4, 64 * u, 64 * u + 64, 0, (1, 448))).then_inc(on["o1_copied"], 1)

            def layer0_digits(a, first):
                for k in range(first, first + 4):
                    act.wait_ge(on["digits"], a * per["digits"] + k + 1)
                    for q in range(4):
                        ins = copy(rows(cut, 32 * q, 32 * q + 32, DG + 64 * (k % 2) + 16 * (k // 2), (1, 16), (FR, 7)), bank(k % 4, 0, 32, 7 * q, (28, 16), (1, 7)))
                    ins.then_inc(on["digits_copied"], 1)

            def layer0_what(a):
                act.wait_ge(on["what_h1"], a * per["what_h1"] + 1)
                for k in range(4):
                    ins = nc.scalar.activation(rows(big, 0, HID, HW1 + FR * k, (1, FR)), bank(0, 0, HID, FR * k, (1, FR)), ACT.Relu,
                                               bias=rows(tab["what_b1"], 0, HID, k, (1, 1)))
                ins.then_inc(on["what_h1_copied"], 1)

            def layer0_what_deep(a):
                act.wait_ge(on["what_h2"], a * per["what_h2"] + 1)
                for k in range(2):
                    ins = nc.scalar.activation(rows(big, 0, HID, HW2 + FR * k, (1, FR)), bank(1, 0, HID, FR * k, (1, FR)), ACT.Relu,
                                               bias=rows(tab["what_b2"], 0, HID, k, (1, 1)))
                ins.then_inc(on["what_h2_copied"], 1)

            def layer0_dec(a):
                act.wait_ge(on["what_z"], a * per["what_z"] + 1)
                nc.scalar.activation(rows(big, 0, 10, ZW, (1, S)), bank(2, 0, 10, 0, (1, S)), ACT.Identity,
                                     bias=rows(tab["what_bloc"], 0, 10, 0, (1, 1))).then_inc(on["what_z_copied"], 1)
                act.wait_ge(on["dec_h1"], a * per["dec_h1"] + 1)
                for k in range(2):
                    ins = nc.scalar.activation(rows(big, 0, HID, D1 + S * k, (1, S)), bank(3, 0, HID, S * k, (1, S)), ACT.Relu,
                                               bias=rows(tab["dec_b1"], 0, HID, k, (1, 1)))
                ins.then_inc(on["dec_h1_copied"], 1)

            def layer0_dec_hidden(a):
                act.wait_ge(on["dec_h2"], a * per["dec_h2"] + 1)
                for k in range(4):
                    ins = nc.scalar.activation(rows(d2, 0, HID, S * k, (1, S)), bank(0, 0, HID, S * k, (1, S)), ACT.Relu,
                                               bias=rows(tab["dec_b2"], 0, HID, k, (1, 1)))
                ins.then_inc(on["dec_h2_copied"], 1)

            def layer0_dec_out(a):
                act.wait_ge(on["dec_out"], a * per["dec_out"] + 1)
                nc.scalar.activation(rows(cut, 0, S, SG, (392, 2), (1, 392)), bank(1, 0, S, 0, (512, 2), (1, 392)), ACT.Tanh, scale=0.5).then_inc(on["dec_tanh"], 1)

            def layer0_x1(a, hs):
                for q in range(4):
                    act.wait_ge(on["x1"], a * per["x1"] + 4 * hs + q + 1)
                    copy(view(x1, 1024 * q + 256 * hs, (512, 2), (1, 256)), bank(q, 0, 128, 0, (256, 2), (1, 256))).then_inc(on["x1_copied"], 1)

            def half_squares(t, i, k):
                sq = view(work, SQ, (256, 8), (1, 256))
                nc.scalar.activation(sq, half(i, 0, (512, 8), (1, 256)), ACT.Square).then_inc(on["b_squares"], 1)

            def half_root(t, k):
                act.wait_ge(on["b_variance"], t * per["b_variance"] + k)
                v = view(bsmall, BRS, (1, 32))
                nc.scalar.activation(v, v, ACT.Sqrt).then_inc(on["b_deviation"], 1)

            def half_rest(t, i, k, row):
                act.wait_ge(on["b_scales"], t * per["b_scales"] + k)
                for p in range(VP, 8):
                    for s_ in range(SH):
                        ins = nc.scalar.activation(view(work, XNB + row * (SH * p + s_), (1, 64)), half(i, 512 * p + 64 * s_, (1, 64)), ACT.Identity,
                                                   bias=view(bsmall, BNM + SH * p + s_, (1, 1)), scale=view(bsmall, BRS + SH * p + s_, (1, 1)))
                ins.then_inc(on["b_xn_rest"], 1)

            def half_norm1(g, t, i):
                act.wait_ge(on["x1_copied"], g * per["x1_copied"] + 4 * i + 4)
                if not (isinstance(t, int) and t == 0):
                    act.wait_ge(on["added"], t * per["added"])
                half_squares(t, i, 1)

            def half_freq(t):
                for k in range(5):
                    act.wait_ge(on["dft"], t * per["dft"] + k + 1)
                    w = min(7, 32 - 7 * k) * NA
                    copy(view(work, ZZ + 7 * NA * k, (1, w)), bank(4 + k % 4, 0, 128, 0, (1, w))).then_inc(on["dft_copied"], 1)

            def half_mix(t):
                for k in range(5):
                    act.wait_ge(on["mixed"], t * per["mixed"] + k + 1)
                    m = min(7, NH - 7 * k)
                    copy(view(fcb, 7 * k, (NH, KB * SH), (1, m)), bank(4 + k % 4, 0, 128, 0, (1, KB * SH), (KB * SH, m))).then_inc(on["mixed_copied"], 1)

            def half_inverse(t, i):
                act.wait_ge(on["corr"], t * per["corr"] + 1)
                copy(view(bsmall, ES, (1, 128)), bank(4, 0, 128, 0, (1, 128))).then_inc(on["corr_copied"], 1)

            def half_norm2(t, i):
                for k in range(4):
                    act.wait_ge(on["x2_ready"], t * per["x2_ready"] + k + 1)
                    ins = nc.scalar.activation(view(work, SQ + 512 * k, (256, 2), (1, 256)), half(i, 1024 * k, (512, 2), (1, 256)), ACT.Square)
                ins.then_inc(on["b_squares"], 1)

            def half_conv2(t, i):
                for k in range(6):
                    act.wait_ge(on["conv2"], t * per["conv2"] + k + 1)
                    m = SH * min(2, WB - 2 * k)
                    copy(rows(work, 0, 96, Y2O + 512 * k, (N, m), (1, N - 1)), bank(4 + k % 4, 0, 96, 0, (N, m), (1, N - 1))).then_inc(on["conv2_copied"], 1)

            def half_norm3(t, i):
                act.wait_ge(on["x3_ready"], t * per["x3_ready"] + 1)
                half_squares(t, i, 3)

            def half_out(t):
                for k in range(4):
                    act.wait_ge(on["turned"], t * per["turned"] + k + 1)
                    copy(view(work, OUT + 512 * k, (128, 4), (64, 2), (1, 64)), bank(4 + k, 0, 128, 0, (64, 4), (256, 2), (1, 64))).then_inc(on["turned_copied"], 1)

            def turn(g, a):
                for i in range(2):
                    t = g * 2 + i if isinstance(g, int) else act.snap(g * 2 + i)
                    first, second = a is not None and i == 0, a is not None and i == 1
                    half_norm1(g, t, i)
                    if isinstance(t, int):
                        if t:
                            half_out(t - 1)
                    else:
                        half_out(act.snap(g * 2 + i - 1))
                    half_root(t, 1)
                    half_rest(t, i, 1, NA)
                    if i == 0:
                        layer0_x1(g, 1)
                    if second:
                        layer0_hidden(a)
                    half_freq(t)
                    if first:
                        layer0_squares(a)
                    if second:
                        layer0_profiles(a)
                        layer0_norms(a)
                    if second:
                        layer0_cut(a, 0, 2)
                    half_mix(t)
                    if second:
                        layer0_cut(a, 2, 8)
                    half_inverse(t, i)
                    half_norm2(t, i)
                    if second:
                        layer0_digits(a, 0)
                    half_root(t, 2)
                    half_rest(t, i, 2, N)
                    if second:
                        layer0_digits(a, 4)
                    if first:
                        act.wait_ge(on["y_stored"], t * per["y_stored"] + per["y_stored"])
                        layer0_conv(a, 0)
                        layer0_conv(a, 1)
                    if second:
                        layer0_what(a)
                    half_conv2(t, i)
                    if first:
                        layer0_conv(a, 2)
                    if second:
                        layer0_what_deep(a)
                        layer0_dec(a)
                        layer0_dec_hidden(a)
                    half_norm3(t, i)
                    if first:
                        layer0_conv(a, 3)
                    if second:
                        layer0_dec_out(a)
                    half_root(t, 3)
                    half_rest(t, i, 3, N)
                    if first:
                        layer0_exp(a)
                    if second:
                        layer0_x1(a, 0)

            layer0_squares(0)
            for j in range(4):
                layer0_conv(0, j)
            layer0_exp(0)
            layer0_hidden(0)
            layer0_profiles(0)
            layer0_norms(0)
            layer0_cut(0, 0, 8)
            layer0_digits(0, 0)
            layer0_digits(0, 4)
            layer0_what(0)
            layer0_what_deep(0)
            layer0_dec(0)
            layer0_dec_hidden(0)
            layer0_dec_out(0)
            layer0_x1(0, 0)
            if groups > 1:
                turn(0, 1)
                with act.Fori(1, groups - 1) as g:
                    turn(g, act.snap(g + 1))
            turn(groups - 1, None)
            half_out(2 * groups - 1)

        @block.vector
        def _(dve):
            dve.wait_ge(loaded, TABLES)
            setup = [0]

            def step(ins):
                setup[0] += 1
                ins.then_inc(mixing, 1)
                dve.wait_ge(mixing, setup[0])

            P = lambda j: view(cut, 64 * j, (1, 64))
            sa, sb_ = view(cut, 384, (1, 64)), view(cut, 448, (1, 64))
            tmp = [view(cut, 512 + 64 * j, (1, 64)) for j in range(3)]
            step(nc.vector.tensor_tensor(tmp[0], P(2), sa, ALU.mult))
            step(nc.vector.tensor_tensor(tmp[1], P(0), P(4), ALU.add))
            step(nc.vector.tensor_tensor(tmp[1], tmp[1], sa, ALU.mult))
            step(nc.vector.tensor_tensor(tmp[2], P(1), P(5), ALU.subtract))
            step(nc.vector.tensor_tensor(tmp[2], tmp[2], sb_, ALU.mult))
            mw = view(mix_w, 0, (64, N), (1, 64))
            t1 = view(frm, 0, (64, N), (1, 64))
            ang = lambda j: view(tab["cos_sin"], N * j, (1, N), (0, 64))
            over = lambda j: view(cut, 512 + 64 * j, (0, N), (1, 64))
            step(nc.vector.tensor_tensor(mw, ang(0), over(1), ALU.mult))
            step(nc.vector.tensor_tensor(mw, mw, over(0), ALU.add))
            step(nc.vector.tensor_tensor(t1, ang(1), over(2), ALU.mult))
            step(nc.vector.tensor_tensor(mw, mw, t1, ALU.add))
            for j, (p, s_, c_) in enumerate(((0, sa, -1), (1, sb_, -1), (4, sa, -1), (5, sb_, 1))):
                step(nc.vector.scalar_tensor_tensor(view(mix_e, 64 * j, (1, 64)), P(p), c_ / N, s_, ALU.mult, ALU.mult))
            for X in range(XS):
                w = rows(tab["where_w1"], 0, CM, (2 * HID + 1) * X + 1, (1, 2 * HID))
                step(nc.vector.scalar_tensor_tensor(w, rows(cut, 0, CM, 704, (1, 2 * HID)), rows(tab["ok"], 0, CM, X, (1, 1)), w, ALU.mult, ALU.add))
            assert setup[0] == SETUP

            links = {}

            def link(ins, a):
                links["a"] = links.get("a", 0) % LINKS + 1
                ins.then_inc(on["vector_link"], 1)
                dve.wait_ge(on["vector_link"], a * per["vector_link"] + links["a"])

            def blink(ins, t):
                links["b"] = links.get("b", 0) % B_LINKS + 1
                ins.then_inc(on["b_link"], 1)
                dve.wait_ge(on["b_link"], t * per["b_link"] + links["b"])

            def layer0_norm(a):
                pairs = 32
                source, dst = view(raw, 0, (128, pairs), (1, 128)), view(frm, 0, (128, pairs), (1, 128))
                dve.wait_ge(on["raw_loaded"], a * per["raw_loaded"] + per["raw_loaded"])
                nc.vector.tensor_reduce(view(small, ST, (1, pairs)), source, AX, ALU.add)
                dve.wait_ge(on["squares"], a * per["squares"] + 1)
                nc.vector.tensor_reduce(view(small, ST + pairs, (1, pairs)), dst, AX, ALU.add).then_inc(on["sums"], 1)
                dve.wait_ge(on["stats"], a * per["stats"] + 1)
                v = lambda o: view(small, o, (1, pairs))
                link(nc.vector.tensor_scalar(v(MS), bank(3, 0, 128, 0, (1, pairs)), 1.0 / CNT, None, ALU.mult), a)
                link(nc.vector.tensor_tensor(v(TV), v(MS), v(MS), ALU.mult), a)
                link(nc.vector.scalar_tensor_tensor(v(RS), bank(3, 0, 128, pairs, (1, pairs)), 1.0 / CNT, v(TV), ALU.mult, ALU.subtract), a)
                nc.vector.tensor_scalar(v(RS), v(RS), EPS, None, ALU.add).then_inc(on["variance"], 1)
                dve.wait_ge(on["deviation"], a * per["deviation"] + 1)
                link(nc.vector.reciprocal(v(RS), v(RS)), a)
                link(nc.vector.scalar_tensor_tensor(v(NM), v(MS), -1.0, v(RS), ALU.mult, ALU.mult), a)
                wide = lambda o: view(small, o, (1, pairs), (0, 128))
                link(nc.vector.tensor_tensor(dst, source, wide(RS), ALU.mult), a)
                nc.vector.tensor_tensor(dst, dst, wide(NM), ALU.add).then_inc(on["xn_ready"], 1)

            def layer0_copies(a):
                dve.wait_ge(on["xn_ready"], a * per["xn_ready"] + 1)
                for u in range(2):
                    ins = nc.vector.tensor_copy(rows(cut, 64 * u, 64 * u + 64, 1 - u + 4096 * u, (256, 2 * S), (1, 256)),
                               rows(frm, 64 * u, 64 * u + 64, 0, (256, 2), (512, S), (1, 256)))
                ins.then_inc(on["xd_copied"], 1)

            def layer0_max(a):
                dve.wait_ge(on["conv_copied"], a * per["conv_copied"] + per["conv_copied"])
                last = rows(fcb, 0, CM, FR * (XS - 1), (1, FR))
                link(nc.vector.tensor_scalar(last, last, rows(tab["ok"], 0, CM, XS - 1, (1, 1)), rows(tab["low"], 0, CM, 0, (1, 1)), ALU.mult, ALU.add), a)
                nc.vector.tensor_reduce(rows(small, 0, CM, PM, (1, FR)), rows(fcb, 0, CM, 0, (1, FR), (FR, XS)), AX, ALU.max).then_inc(on["conv_max"], 1)

            def layer0_diag(a):
                dve.wait_ge(on["max_turned"], a * per["max_turned"] + 1)
                link(nc.vector.tensor_reduce(view(small, MX, (1, 1)), bank(0, 0, 128, 0, (1, CM)), AX, ALU.max), a)
                nc.vector.tensor_scalar(view(small, DGM, (1, 128)), tab["ident"][:, :], view(small, MX, (1, 1)), None, ALU.mult).then_inc(on["max_diag"], 1)

            def layer0_shift(a):
                dve.wait_ge(on["max_spread"], a * per["max_spread"] + 1)
                fc = rows(fcb, 0, CM, 0, (FR, XS), (1, FR))
                nc.vector.tensor_tensor(fc, fc, bank(1, 0, CM, 0, (0, XS), (1, FR)), ALU.subtract).then_inc(on["conv_shifted"], 1)

            def layer0_where(a):
                dve.wait_ge(on["where_z"], a * per["where_z"] + 1)
                link(nc.vector.reciprocal(view(small, MX, (1, 1)), bank(1, 0, 128, 2, (1, 1))), a)
                nc.vector.scalar_tensor_tensor(view(small, ZI, (1, 2)), bank(1, 0, 128, 0, (1, 2)), view(small, MX, (1, 1)),
                                               tab["where_bloc"][:, :], ALU.mult, ALU.add).then_inc(on["where_zz"], 1)
                dve.wait_ge(on["where_tanh"], a * per["where_tanh"] + 1)
                nc.vector.tensor_scalar(view(small, TT, (1, 2)), view(small, ZT, (1, 2)), 1.0, (N - D) / 2, ALU.add, ALU.mult).then_inc(on["shift"], 1)

            def layer0_profiles(a):
                dve.wait_ge(on["profile_abs"], a * per["profile_abs"] + 1)
                pr = view(small, PR, (1, 384))
                t_b, t_a, t_c = (view(fcb, 384 * j, (1, 384)) for j in range(3))
                nc.vector.tensor_scalar(t_b, pr, 2.0, 0.0, ALU.subtract, ALU.min)
                link(nc.vector.tensor_scalar(t_a, pr, 1.0, 0.0, ALU.subtract, ALU.min), a)
                link(nc.vector.tensor_tensor(t_c, t_b, t_b, ALU.mult), a)
                link(nc.vector.scalar_tensor_tensor(t_b, t_b, 1.0, t_c, ALU.add, ALU.mult), a)
                link(nc.vector.tensor_tensor(t_c, t_a, t_a, ALU.mult), a)
                link(nc.vector.tensor_scalar(t_a, t_a, 2.0, 1.0, ALU.mult, ALU.add), a)
                link(nc.vector.tensor_tensor(t_a, t_a, t_c, ALU.mult), a)
                nc.vector.scalar_tensor_tensor(pr, t_b, -0.5, t_a, ALU.mult, ALU.add).then_inc(on["profiles"], 1)
                for ax in range(2):
                    t_ = view(small, TT + 1 - ax, (1, 1))
                    nc.vector.tensor_scalar(view(small, SS + D * ax, (1, D)), view(tab["place"], D * ax, (1, D)), t_, 0.5, ALU.subtract, ALU.subtract)
                    o = 2 * D + N * ax
                    nc.vector.tensor_scalar(view(small, SS + o, (1, N)), view(tab["place"], o, (1, N)), t_, 0.5, ALU.subtract, ALU.subtract)
                v = lambda o: view(small, o, (1, 2 * D + 2 * N))
                dve.wait_ge(on["totals"], a * per["totals"] + 1)
                total = bank(3, 0, 128, 0, (1, 2 * D + 2 * N))
                nc.vector.tensor_scalar(v(TOT), total, THR, None, ALU.max)
                link(nc.vector.tensor_scalar(v(TMP), total, THR, None, ALU.is_gt), a)
                link(nc.vector.scalar_tensor_tensor(v(TMP), v(SS), -0.5, v(TMP), ALU.is_ge, ALU.mult), a)
                for o, m, hi in ((0, 2 * D, N - 0.5), (2 * D, 2 * N, D - 0.5)):
                    q_ = view(small, TMP + o, (1, m))
                    ins = nc.vector.scalar_tensor_tensor(q_, view(small, SS + o, (1, m)), hi, q_, ALU.is_le, ALU.mult)
                link(ins, a)
                link(nc.vector.reciprocal(v(TOT), v(TOT)), a)
                nc.vector.tensor_tensor(v(RN), v(TOT), v(TMP), ALU.mult).then_inc(on["norms"], 1)

            def layer0_cut_norms(a):
                dve.wait_ge(on["cut_norms_loaded"], a * per["cut_norms_loaded"] + per["cut_norms_loaded"])
                ny = view(cut, NY, (FR, 7), (1, FR))
                link(nc.vector.tensor_tensor(ny, ny, view(small, NX, (0, 7), (1, FR)), ALU.mult), a)

            def layer0_digits(a):
                dve.wait_ge(on["digits_copied"], a * per["digits_copied"] + per["digits_copied"])
                dg = view(cut, DG, (FR, 7), (1, FR))
                nc.vector.tensor_tensor(dg, dg, view(cut, NY, (FR, 7), (1, FR)), ALU.mult).then_inc(on["digits_normed"], 1)

            def layer0_what(a):
                dve.wait_ge(on["what_h2_copied"], a * per["what_h2_copied"] + 1)
                for k in range(2):
                    ins = nc.vector.tensor_reduce(rows(big, 0, HID, HS + S * k, (1, S)), rows(big, 0, HID, HW2 + FR * k, (4, S), (32, 4), (1, 4)), mybir.AxisListType.XY, ALU.add)
                ins.then_inc(on["what_sum"], 1)

            def layer0_dec(a):
                dve.wait_ge(on["dec_tanh"], a * per["dec_tanh"] + 1)
                sg = rows(cut, 0, S, SG, (1, D * D))
                nc.vector.tensor_scalar(sg, sg, 0.5, 0.5, ALU.mult, ALU.add).then_inc(on["dec_sig"], 1)

            def layer0_aa(a):
                dve.wait_ge(on["rec_norms_loaded"], a * per["rec_norms_loaded"] + per["rec_norms_loaded"])
                for k in range(4):
                    dve.wait_ge(on["aa"], a * per["aa"] + k + 1)
                    nc.vector.tensor_tensor(view(cut, AA + 512 * k, (1, 512)), bank(k, 0, 128, 0, (1, 512)), view(cut, RBY + 512 * k, (1, 512)), ALU.mult).then_inc(on["aa_copied"], 1)

            def normalise(t, i, k, row, a=None):
                source = half(i, 0, (512, 8), (64, SH), (1, 64))
                pairs = 8 * SH
                if k != 2:
                    nc.vector.tensor_reduce(view(bsmall, BST, (SH, 8), (1, SH)), source, AX, ALU.add)
                dve.wait_ge(on["b_squares"], t * per["b_squares"] + k)
                nc.vector.tensor_reduce(view(bsmall, BST + pairs, (1, pairs)), view(work, SQ, (64, pairs), (1, 64)), AX, ALU.add).then_inc(on["b_sums"], 1)
                if a is not None and i == 0:
                    layer0_max(a)
                if a is not None and i == 1:
                    layer0_dec(a)
                dve.wait_ge(on["b_stats"], t * per["b_stats"] + k)
                v = lambda o: view(bsmall, o, (1, pairs))
                blink(nc.vector.tensor_scalar(v(BMS), bank(7, 0, 128, 0, (1, pairs)), 1.0 / CNT, None, ALU.mult), t)
                blink(nc.vector.tensor_tensor(v(BTV), v(BMS), v(BMS), ALU.mult), t)
                blink(nc.vector.scalar_tensor_tensor(v(BRS), bank(7, 0, 128, pairs, (1, pairs)), 1.0 / CNT, v(BTV), ALU.mult, ALU.subtract), t)
                nc.vector.tensor_scalar(v(BRS), v(BRS), EPS, None, ALU.add).then_inc(on["b_variance"], 1)
                dve.wait_ge(on["b_deviation"], t * per["b_deviation"] + k)
                blink(nc.vector.reciprocal(v(BRS), v(BRS)), t)
                nc.vector.scalar_tensor_tensor(v(BNM), v(BMS), -1.0, v(BRS), ALU.mult, ALU.mult).then_inc(on["b_scales"], 1)
                dve.wait_ge(on["b_scales"], t * per["b_scales"] + k)
                if a is not None and i == 0:
                    layer0_diag(a)
                source, dst = half(i, 0, (512, VP), (64, SH), (1, 64)), view(work, XNB, (SH * row, VP), (row, SH), (1, 64))
                wide = lambda o: view(bsmall, o, (SH, VP), (1, SH), (0, 64))
                blink(nc.vector.tensor_tensor(dst, source, wide(BRS), ALU.mult), t)
                nc.vector.tensor_tensor(dst, dst, wide(BNM), ALU.add).then_inc(on["b_xn_ready"], 1)

            def half_norm1(g, t, i):
                dve.wait_ge(on["x1_copied"], g * per["x1_copied"] + 4 * i + 4)
                normalise(t, i, 1, NA)
                dve.wait_ge(on["b_xn_ready"], t * per["b_xn_ready"] + 1)
                dve.wait_ge(on["b_xn_rest"], t * per["b_xn_rest"] + 1)
                xn = lambda n1: view(work, XNB + n1, (NA, 32), (1, 32))
                v = lambda o: view(bsmall, o, (1, 32))
                nc.vector.tensor_tensor(v(BTV), v(BST), v(BRS), ALU.mult)
                dve.wait_ge(on["out_stored"], t * per["out_stored"] + 16)
                fold = view(work, ZZ, (32, 32), (1, 32))
                blink(nc.vector.tensor_tensor(fold, xn(0), xn(32), ALU.subtract), t)
                prods = view(work, ZZ + 1024, (1024, 2), (32, 32), (1, 32))
                blink(nc.vector.tensor_tensor(prods, view(work, ZZ, (0, 2), (32, 32), (1, 32)), view(tab["cos_sin"], 0, (N, 2), (0, 32), (1, 32)), ALU.mult), t)
                nc.vector.tensor_reduce(view(work, XNB + N + 1, (1, 2), (NA, 32)), prods, AX, ALU.add)
                nc.vector.scalar_tensor_tensor(view(work, XNB + N, (NA, 32)), v(BNM), float(N), v(BTV), ALU.mult, ALU.add).then_inc(on["moments"], 1)

            def half_inverse(t, i):
                def sums(k):
                    nc.vector.tensor_reduce(view(bsmall, BST + 2 * SH * k, (SH, 2), (1, SH)), half(i, 1024 * k, (512, 2), (64, SH), (1, 64)), AX, ALU.add)

                for k in range(4):
                    if k:
                        dve.wait_ge(on["x2_ready"], t * per["x2_ready"] + k)
                        sums(k - 1)
                    dve.wait_ge(on["idft"], t * per["idft"] + k + 1)
                    for j in range(2):
                        o = half(i, 512 * (2 * k + j), (1, 2), (64, SH), (2, 32))
                        ins = nc.vector.tensor_tensor(o, o, bank(4 + k, 0, 128, 256 * j, (128, 2), (32, SH), (1, 32)), ALU.add)
                    ins.then_inc(on["x2_ready"], 1)
                dve.wait_ge(on["x2_ready"], t * per["x2_ready"] + per["x2_ready"])
                sums(3)
                normalise(t, i, 2, N)

            def half_edge(t):
                dve.wait_ge(on["v2_loaded"], t * per["v2_loaded"] + per["v2_loaded"])
                nc.vector.memset(rows(work, 0, 96, Y2O + N - 1, (N, WB * SH)), 0.0).then_inc(on["edge_cleared"], 1)

            def half_layer3(t, i, a):
                dve.wait_ge(on["y2_loaded"], t * per["y2_loaded"] + per["y2_loaded"])
                xh = half(i, 0, (512, 8), (1, 256))
                nc.vector.tensor_tensor(xh, xh, view(work, 0, (256, 8), (1, 256)), ALU.add).then_inc(on["x3_ready"], 1)
                dve.wait_ge(on["x3_ready"], t * per["x3_ready"] + 1)
                normalise(t, i, 3, N, a)
                dve.wait_ge(on["b_xn_ready"], t * per["b_xn_ready"] + 3)
                dve.wait_ge(on["b_xn_rest"], t * per["b_xn_rest"] + 3)
                v = lambda o: view(bsmall, o, (1, 32))
                blink(nc.vector.tensor_tensor(v(BTV), v(BST), v(BRS), ALU.mult), t)
                blink(nc.vector.scalar_tensor_tensor(v(BST), v(BNM), float(N), v(BTV), ALU.mult, ALU.add), t)
                for j in range(2):
                    nc.vector.tensor_tensor(view(work, PRODS + 1024 * j, (64, 16), (1, 64)), view(work, 1024 * j, (64, 16), (1, 64)),
                                            view(bsmall, BST + 16 * (1 - j), (1, 16), (0, 64)), ALU.mult).then_inc(on["gate_prod"], 1)

            def half_gate(t, i):
                for k in range(4):
                    dve.wait_ge(on["gate_sum"], t * per["gate_sum"] + k + 1)
                    o = view(work, 512 * k, (1, 512))
                    nc.vector.scalar_tensor_tensor(o, bank(4 + k, 0, 128, 0, (1, 512)), 0.0, o, ALU.is_gt, ALU.mult).then_inc(on["gated"], 1)
                dve.wait_ge(on["gated"], t * per["gated"] + per["gated"])
                xh = half(i, 0, (512, 8), (1, 256))
                nc.vector.tensor_tensor(xh, xh, view(work, 0, (256, 8), (1, 256)), ALU.add).then_inc(on["added"], 1)

            def turn(g, a):
                for i in range(2):
                    t = g * 2 + i if isinstance(g, int) else dve.snap(g * 2 + i)
                    first, second = a is not None and i == 0, a is not None and i == 1
                    half_norm1(g, t, i)
                    if first:
                        layer0_norm(a)
                        layer0_copies(a)
                    if second:
                        layer0_where(a)
                        layer0_profiles(a)
                        layer0_cut_norms(a)
                    half_inverse(t, i)
                    if second:
                        layer0_digits(a)
                    half_edge(t)
                    if second:
                        layer0_what(a)
                    half_layer3(t, i, a)
                    if first:
                        layer0_shift(a)
                    if second:
                        layer0_aa(a)
                    half_gate(t, i)

            layer0_norm(0)
            layer0_copies(0)
            layer0_max(0)
            layer0_diag(0)
            layer0_shift(0)
            layer0_where(0)
            layer0_profiles(0)
            layer0_cut_norms(0)
            layer0_digits(0)
            layer0_what(0)
            layer0_dec(0)
            layer0_aa(0)
            assert links["a"] == LINKS, links
            if groups > 1:
                with dve.Fori(0, groups - 1) as g:
                    turn(g, dve.snap(g + 1))
            turn(groups - 1, None)
            assert links == {"a": LINKS, "b": B_LINKS}, links

        @block.tensor
        def _(pe):
            mm = nc.tensor.matmul
            pe.wait_ge(loaded, TABLES)
            pe.wait_ge(mixing, SETUP)
            pe.wait_ge(cleared, 4)
            fc = lambda X: rows(fcb, 0, CM, FR * X, (1, FR))

            def layer0_stats(a):
                pe.wait_ge(on["sums"], a * per["sums"] + 1)
                mm(bank(3, 0, 128, 0, (1, 64)), tab["halves"][:, :], view(small, ST, (1, 64)), start=True, stop=True).then_inc(on["stats"], 1)

            def layer0_conv(a, first, last):
                if first == 0:
                    pe.wait_ge(on["xd_loaded"], a * per["xd_loaded"] + per["xd_loaded"])
                    pe.wait_ge(on["xd_copied"], a * per["xd_copied"] + 1)
                for n in range(first, last):
                    j, e = n // TAPS, n % TAPS
                    ins = mm(bank(j, 0, CM, 0, (XS, 32), (1, XS)), view(tab["toep"], CM * e, (1, CM)),
                             view(cut, 1 + 64 * 32 * j + 2 * e, (64, 32), (3, XS)), start=e == 0, stop=e == TAPS - 1)
                    if e == TAPS - 1:
                        ins.then_inc(on["conv"], 1)

            def layer0_max(a):
                pe.wait_ge(on["conv_max"], a * per["conv_max"] + 1)
                nc.tensor.transpose(bank(0, 0, 128, 0, (1, CM)), rows(small, 0, CM, PM, (1, FR)), rows(tab["ident"], 0, CM, 0, (1, CM))).then_inc(on["max_turned"], 1)

            def layer0_spread(a):
                pe.wait_ge(on["max_diag"], a * per["max_diag"] + 1)
                mm(bank(1, 0, CM, 0, (1, FR)), view(tab["ones"], 0, (1, CM)), view(small, DGM, (1, FR)), start=True, stop=True).then_inc(on["max_spread"], 1)

            def layer0_where(a):
                pe.wait_ge(on["conv_exp"], a * per["conv_exp"] + 1)
                for X in range(XS):
                    mm(bank(2, 0, HID + 1, 0, (1, FR)), rows(tab["where_w1"], 0, CM, (2 * HID + 1) * X, (1, HID + 1)), fc(X), start=X == 0, stop=X == XS - 1)

            def layer0_where_rest(a):
                for X in range(XS):
                    ins = mm(bank(2, 0, HID, FR, (1, FR)), rows(tab["where_w1"], 0, CM, (2 * HID + 1) * X + HID + 1, (1, HID)), fc(X), start=X == 0, stop=X == XS - 1)
                ins.then_inc(on["where_h1"], 1)

            def layer0_where_deep(a):
                pe.wait_ge(on["where_h1_copied"], a * per["where_h1_copied"] + 1)
                for h, m in ((0, HID + 1), (1, HID)):
                    ins = mm(bank(0, 0, HID, 0, (1, FR)), rows(tab["where_w2"], 0, m, HID * h, (1, HID)), rows(big, 0, m, H1 + FR * h, (1, FR)), start=h == 0, stop=h == 1)
                ins.then_inc(on["where_h2"], 1)
                pe.wait_ge(on["where_h2_copied"], a * per["where_h2_copied"] + 1)
                mm(bank(1, 0, 128, 0, (1, 2)), rows(big, 0, HID, H2, (1, FR)), tab["where_wloc"][0:HID, :], start=True, stop=True)
                mm(bank(1, 0, 128, 2, (1, 1)), rows(big, 0, 1, H1, (1, FR)), rows(tab["ones"], 0, 1, 0, (1, 1)), start=True, stop=True).then_inc(on["where_z"], 1)

            def layer0_profiles(a):
                pe.wait_ge(on["profiles"], a * per["profiles"] + 1)
                for j in range(4):
                    ins = nc.tensor.transpose(bank(2, 0, PROF, FR * j, (1, FR)), view(small, PR + PROF * j, (1, PROF)), tab["ident"][:, :])
                ins.then_inc(on["profiles_turned"], 1)
                pe.wait_ge(on["turned_profiles_copied"], a * per["turned_profiles_copied"] + 1)
                for j, (o, m) in enumerate(((0, D), (D, D), (2 * D, N), (2 * D + N, N))):
                    ins = mm(bank(3, 0, 128, o, (1, m)), rows(big, 0, PROF, FR * j, (1, FR)), rows(tab["windows"], 0, PROF, D * (j // 2), (1, m)), start=True, stop=True)
                ins.then_inc(on["totals"], 1)

            def layer0_norms(a):
                pe.wait_ge(on["norms"], a * per["norms"] + 1)
                passed(pe)
                nc.tensor.transpose(bank(2, 0, 2 * D, 0, (1, FR)), view(small, RN, (1, 2 * D)), tab["ident"][:, :]).then_inc(on["norms_turned"], 1)

            def layer0_cut(a, first, last):
                if first == 0:
                    pe.wait_ge(on["turned_norms_copied"], a * per["turned_norms_copied"] + 1)
                    pe.wait_ge(on["cut_rows_loaded"], a * per["cut_rows_loaded"] + per["cut_rows_loaded"])
                    passed(pe)
                for t4 in range(first, last):
                    if t4 >= 2:
                        pe.wait_ge(on["o1_copied"], a * per["o1_copied"] + 2 * t4 - 2)
                        passed(pe)
                    for j in range(16):
                        fu = 16 * t4 + j
                        q2, s_, r = fu // 32, fu // 4 % 8, fu % 4
                        for u in range(2):
                            ins = mm(bank(2 * (t4 % 2) + u, 64 * u, 64 * u + 64, 28 * j, (1, D)), rows(frm, 64 * u, 64 * u + 64, 64 * (8 * s_ + 4 * q2 + r), (1, 64)),
                                     rows(cut, 64 * u, 64 * u + 64, WY + fu, (64, D)), start=j == 0, stop=True, skip_group_check=True)
                            if j == 15:
                                ins.then_inc(on["o1"], 1)

            def layer0_digits(a, first):
                if first == 0:
                    pe.wait_ge(on["o1_copied"], a * per["o1_copied"] + per["o1_copied"])
                    passed(pe)
                    pe.wait_ge(on["cut_loaded"], a * per["cut_loaded"] + per["cut_loaded"])
                    passed(pe)
                for t4 in range(first, first + 2):
                    if t4 >= 2:
                        pe.wait_ge(on["digits_copied"], a * per["digits_copied"] + 2 * t4 - 2)
                        passed(pe)
                    for j in range(16):
                        fu = 16 * t4 + j
                        for u in range(2):
                            ins = mm(bank(2 * (t4 % 2) + u, 0, 32, 28 * j, (1, D)), rows(cut, 64 * u, 64 * u + 64, WX + fu, (64, 32)),
                                     rows(cut, 64 * u, 64 * u + 64, O1 + 28 * fu, (1, D)), start=j == 0, stop=True, skip_group_check=True)
                            if j == 15:
                                ins.then_inc(on["digits"], 1)

            def layer0_what(a):
                pe.wait_ge(on["digits_normed"], a * per["digits_normed"] + 1)
                for k in range(4):
                    for j in range(7):
                        ins = mm(bank(0, 0, HID, FR * k, (1, FR)), view(tab["what_w1"], 400 * j + HID * k, (1, HID)), view(cut, DG + FR * j, (1, FR)), start=j == 0, stop=j == 6)
                ins.then_inc(on["what_h1"], 1)

            def layer0_what_deep(a):
                pe.wait_ge(on["what_h1_copied"], a * per["what_h1_copied"] + 1)
                for h in range(2):
                    for k in range(4):
                        ins = mm(bank(1, 0, HID, FR * h, (1, FR)), rows(tab["what_w2"], 0, HID, 200 * k + HID * h, (1, HID)),
                                 rows(big, 0, HID, HW1 + FR * k, (1, FR)), start=k == 0, stop=k == 3)
                ins.then_inc(on["what_h2"], 1)

            def layer0_dec(a):
                pe.wait_ge(on["what_sum"], a * per["what_sum"] + 1)
                for k in range(2):
                    ins = mm(bank(2, 0, 10, 0, (1, S)), rows(tab["what_wloc"], 0, HID, 10 * k, (1, 10)), rows(big, 0, HID, HS + S * k, (1, S)), start=k == 0, stop=k == 1)
                ins.then_inc(on["what_z"], 1)
                pe.wait_ge(on["what_z_copied"], a * per["what_z_copied"] + 1)
                for k in range(2):
                    ins = mm(bank(3, 0, HID, S * k, (1, S)), rows(tab["dec_w1"], 0, 10, HID * k, (1, HID)), rows(big, 0, 10, ZW, (1, S)), start=True, stop=True)
                ins.then_inc(on["dec_h1"], 1)
                pe.wait_ge(on["dec_h1_copied"], a * per["dec_h1_copied"] + 1)
                for k in range(4):
                    for h in range(2):
                        ins = mm(bank(0, 0, HID, S * k, (1, S)), rows(tab["dec_w2"], 0, HID, 400 * h + HID * k, (1, HID)),
                                 rows(big, 0, HID, D1 + S * h, (1, S)), start=h == 0, stop=h == 1)
                ins.then_inc(on["dec_h2"], 1)

            def layer0_dec_out(a):
                pe.wait_ge(on["dec_h2_copied"], a * per["dec_h2_copied"] + 1)
                for h in range(2):
                    for k in range(4):
                        ins = mm(bank(1 + h, 0, S, 0, (1, 392)), rows(d2, 0, HID + 1, S * k, (1, S)),
                                 rows(tab["dec_w3"], 0, HID + 1, D * D * k + 392 * h, (1, 392)), start=k == 0, stop=k == 3)
                ins.then_inc(on["dec_out"], 1)

            def layer0_aa(a):
                pe.wait_ge(on["digit_loaded"], a * per["digit_loaded"] + per["digit_loaded"])
                pe.wait_ge(on["rec_loaded"], a * per["rec_loaded"] + per["rec_loaded"])
                for k in range(4):
                    for j in range(2):
                        s_ = 2 * k + j
                        ins = mm(bank(k, 0, 128, 256 * j, (1, 256)), view(digit, 128 * s_, (1, 128)), view(frm, WRY + 256 * s_, (1, 256)), start=j == 0, stop=True, skip_group_check=True)
                    ins.then_inc(on["aa"], 1)

            def layer0_x_turned(a, hs):
                for q in range(4):
                    u = q // 2
                    if hs:
                        pe.wait_ge(on["x1_copied"], a * per["x1_copied"] + q + 1)
                    else:
                        pe.wait_ge(on["aa_copied"], a * per["aa_copied"] + q + 1)
                    passed(pe)
                    for j in range(2):
                        for s4 in range(4):
                            s_ = 4 * hs + s4
                            mm(bank(q, 0, 128, 256 * j + 64 * s4, (1, 64)),
                               rows(raw, 64 * u, 64 * u + 64, 512 * s_ + 256 * (q % 2) + 128 * j, (1, 128)),
                               rows(tab["ident"], 64 * u, 64 * u + 64, 64 * u, (1, 64)), start=j == 0 and s4 == 0, stop=False, is_transpose=True, skip_group_check=True)

            def layer0_x1(a, hs):
                if hs == 0:
                    pe.wait_ge(on["wrx_normed"], a * per["wrx_normed"] + 1)
                    passed(pe)
                for s4 in range(4):
                    for r in range(4):
                        for q in range(4):
                            s_ = 4 * hs + s4
                            j, h = r // 2, r % 2
                            ins = mm(bank(q, 64 * h, 64 * h + 64, 256 * j + 64 * s4, (1, 64)),
                                     rows(frm, 32 * q, 32 * q + 32, WRX + 64 * (4 * s_ + r), (1, 64)),
                                     rows(cut, 32 * q, 32 * q + 32, AA + 64 * (4 * s_ + r), (1, 64)), start=False, stop=True, skip_group_check=True)
                            if s4 == 3 and r == 3:
                                ins.then_inc(on["x1"], 1)

            def half_stats(t, k):
                pe.wait_ge(on["b_sums"], t * per["b_sums"] + k)
                mm(bank(7, 0, 128, 0, (1, 64)), tab["ones"][:, :], view(bsmall, BST, (1, 64)), start=True, stop=True).then_inc(on["b_stats"], 1)

            def half_freq(t):
                pe.wait_ge(on["moments"], t * per["moments"] + 1)
                for k in range(5):
                    w = min(7, 32 - 7 * k) * NA
                    if k >= 4:
                        pe.wait_ge(on["dft_copied"], t * per["dft_copied"] + k - 3)
                    mm(bank(4 + k % 4, 0, 128, 0, (1, w)), tab["dft"][:, :], view(work, XNB + 7 * NA * k, (1, w)), start=True, stop=True).then_inc(on["dft"], 1)

            def half_mix(t):
                pe.wait_ge(on["v_loaded"], t * per["v_loaded"] + per["v_loaded"])
                pe.wait_ge(on["dft_copied"], t * per["dft_copied"] + per["dft_copied"])
                row = lambda n1: view(work, VV + n1, (NA, KB * SH))
                e = lambda j: view(mix_e, 64 * j, (1, 64))
                behind = {0: [(e(0), N + 1), (e(1), N + 2)], 1: [(e(2), N)], 2: [(e(3), N)], 3: [(e(3), N)]}
                for k in range(5):
                    if k >= 4:
                        pe.wait_ge(on["mixed_copied"], t * per["mixed_copied"] + k - 3)
                    for j in range(min(7, NH - 7 * k)):
                        for par in range(2):
                            n1 = 2 * (7 * k + j) + par
                            o = bank(4 + k % 4, 64 * par, 64 * par + 64, KB * SH * j, (1, KB * SH))
                            terms = [(view(mix_w, 64 * n1, (1, 64)), n1)] if n1 < N else behind[n1 - N]
                            for m, (l, r_) in enumerate(terms):
                                ins = mm(o, l, row(r_), start=j == 0 and m == 0, stop=m == len(terms) - 1 and n1 > 0, skip_group_check=True)
                            if n1 == 0:
                                ins = mm(o, tab["l1_bias"][0:1, :], rows(tab["ones"], 0, 1, 0, (1, KB * SH)), start=False, stop=True, skip_group_check=True)
                    ins.then_inc(on["mixed"], 1)

            def half_inverse(t):
                pe.wait_ge(on["y_loaded"], t * per["y_loaded"] + per["y_loaded"])
                pe.wait_ge(on["mixed_copied"], t * per["mixed_copied"] + per["mixed_copied"])
                for jj in range(2):
                    ins = mm(bank(4, 64 * jj, 64 * jj + 64, 0, (1, 128)), view(work, YK + 32 + jj, (NH, 64)), tab["idft"][:, :], start=True, stop=True, skip_group_check=True)
                ins.then_inc(on["corr"], 1)
                pe.wait_ge(on["corr_copied"], t * per["corr_copied"] + 1)
                for k in range(4):
                    for j in range(2):
                        mm(bank(4 + k, 0, 128, 256 * j, (1, 256)), tab["idft"][:, :], view(work, YK + 2 * SH * NH * (2 * k + j), (NH, 2 * SH), (1, 32)),
                           start=j == 0, stop=False, skip_group_check=True)
                    mm(bank(4 + k, 0, 128, 0, (1, 512)), view(bsmall, ES, (1, 128)), view(tab["sel"], 512 * k, (1, 512)), start=False, stop=True, skip_group_check=True).then_inc(on["idft"], 1)

            def half_conv2(t):
                pe.wait_ge(on["v2_loaded"], t * per["v2_loaded"] + per["v2_loaded"])
                pe.wait_ge(on["b_xn_ready"], t * per["b_xn_ready"] + 2)
                tap = lambda ky: view(tab["l2_taps"], 96 * ky, (1, 96))
                for k in range(6):
                    if k >= 4:
                        pe.wait_ge(on["conv2_copied"], t * per["conv2_copied"] + k - 3)
                    m = min(2, WB - 2 * k) * SH
                    b, v = 4 + k % 4, V2 + 512 * k
                    mm(bank(b, 0, 96, 0, (1, N * m)), tap(1), view(work, v, (1, N * m)), start=True, stop=False, skip_group_check=True)
                    mm(bank(b, 0, 96, 1, (N, m), (1, N - 1)), tap(0), view(work, v, (N, m), (1, N - 1)), start=False, stop=False, skip_group_check=True)
                    mm(bank(b, 0, 96, 0, (N, m), (1, N - 1)), tap(2), view(work, v + 1, (N, m), (1, N - 1)), start=False, stop=True, skip_group_check=True).then_inc(on["conv2"], 1)

            def half_gate(t, i):
                pe.wait_ge(on["b_xn_ready"], t * per["b_xn_ready"] + 3)
                for k in range(4):
                    if k % 2 == 0:
                        pe.wait_ge(on["gate_prod"], t * per["gate_prod"] + k // 2 + 1)
                    mm(bank(4 + k, 0, 128, 0, (1, 512)), tab["halves"][:, :], view(work, PRODS + 512 * k, (1, 512)), start=True, stop=True).then_inc(on["gate_sum"], 1)

            def half_turn(t, i):
                pe.wait_ge(on["added"], t * per["added"] + 1)
                for k in range(4):
                    for par in range(2):
                        for j in range(2):
                            ins = nc.tensor.transpose(bank(4 + k, 0, 128, 256 * par + 128 * j, (1, 128)), half(i, 512 * (2 * k + j) + par, (2, 128)), tab["ident"][:, :])
                    ins.then_inc(on["turned"], 1)

            def turn(g, a):
                for i in range(2):
                    t = g * 2 + i if isinstance(g, int) else pe.snap(g * 2 + i)
                    first, second = a is not None and i == 0, a is not None and i == 1
                    if i == 0:
                        layer0_x_turned(g, 1)
                    if second:
                        layer0_where_rest(a)
                    if not (isinstance(t, int) and t == 0):
                        pe.wait_ge(on["turned_copied"], t * per["turned_copied"])
                    half_stats(t, 1)
                    if i == 0:
                        layer0_x1(g, 1)
                    if second:
                        layer0_where_deep(a)
                    half_freq(t)
                    if first:
                        layer0_stats(a)
                    if second:
                        layer0_profiles(a)
                        layer0_norms(a)
                    if second:
                        layer0_cut(a, 0, 1)
                    half_mix(t)
                    if first:
                        layer0_conv(a, 0, 13)
                    if second:
                        layer0_cut(a, 1, 4)
                    half_inverse(t)
                    if first:
                        layer0_conv(a, 13, 17)
                    if second:
                        layer0_digits(a, 0)
                    half_stats(t, 2)
                    if second:
                        layer0_digits(a, 2)
                    if first:
                        layer0_conv(a, 17, 40)
                    if second:
                        layer0_what(a)
                    half_conv2(t)
                    if first:
                        layer0_conv(a, 40, 4 * TAPS)
                    if second:
                        layer0_what_deep(a)
                        layer0_dec(a)
                        layer0_dec_out(a)
                    half_stats(t, 3)
                    if second:
                        layer0_aa(a)
                    if first:
                        layer0_max(a)
                        layer0_spread(a)
                    half_gate(t, i)
                    if second:
                        layer0_x_turned(a, 0)
                        layer0_x1(a, 0)
                    if first:
                        layer0_where(a)
                    half_turn(t, i)

            layer0_stats(0)
            layer0_conv(0, 0, 4 * TAPS)
            layer0_max(0)
            layer0_spread(0)
            layer0_where(0)
            layer0_where_rest(0)
            layer0_where_deep(0)
            layer0_profiles(0)
            layer0_norms(0)
            layer0_cut(0, 0, 4)
            layer0_digits(0, 0)
            layer0_digits(0, 2)
            layer0_what(0)
            layer0_what_deep(0)
            layer0_dec(0)
            layer0_dec_out(0)
            layer0_aa(0)
            layer0_x_turned(0, 0)
            layer0_x1(0, 0)
            if groups > 1:
                turn(0, 1)
                with pe.Fori(1, groups - 1) as g:
                    turn(g, pe.snap(g + 1))
            turn(groups - 1, None)


def kernel(**inputs):
    import concourse.bacc as bacc
    from concourse.bass_utils import run_bass_kernel_spmd

    a = {n: np.asarray(v) for n, v in inputs.items()}
    x = np.ascontiguousarray(a.pop("x"))
    nc = bacc.Bacc("TRN2", target_bir_lowering=False, num_devices=1)
    arrays = {"x_dram": x, **{f"{n}_dram": v for n, v in {**layouts(a), **constants()}.items()}}
    aps = {n[:-5]: nc.dram_tensor(n, v.shape, F32, kind="ExternalInput").ap() for n, v in arrays.items()}
    out = nc.dram_tensor("out_dram", x.shape, F32, kind="ExternalOutput").ap()
    program(nc, aps["x"], out, aps, x.shape[0] // S)
    r = run_bass_kernel_spmd(nc, [arrays], core_ids=[0])
    return r.results[0]["out_dram"]
```
